# Optimizing a Trainium2 kernel written in Bass

```python
import numpy as np
import jax
import jax.numpy as jnp

def _softmax(x, axis=-1):
    return jax.nn.softmax(x, axis=axis)

def _gelu(x):
    return jax.nn.gelu(x, approximate=True)

def _silu(x):
    return jax.nn.silu(x)

def _sigmoid(x):
    return jax.nn.sigmoid(x)

def _layernorm(x, axis=-1, eps=1e-05):
    m = jnp.mean(x, axis=axis, keepdims=True)
    v = jnp.var(x, axis=axis, keepdims=True)
    return (x - m) / jnp.sqrt(v + eps)

def _scatter_add(tgt, idx, src, axis=0):
    return tgt.at[idx].add(src)

def _segment_sum(src, seg, n):
    return jax.ops.segment_sum(src, seg, n)
kernel_name = 'mk_prb_d2_jaxref_r8_00fd4c'

def setup_inputs(seed: int=0):
    np.random.seed(seed)
    _w = jnp.asarray

    def _L0_attn_setup():
        import jax, jax.numpy as jnp
        import numpy as np
        B, T, D_MODEL = (4, 256, 256)
        NUM_HEADS, HEAD_SIZE = (16, 128)
        MODEL_SIZE = 256
        key = jax.random.key(seed)
        ks = jax.random.split(key, 9)
        s = 0.02 / np.sqrt(D_MODEL)
        so = 0.02 / np.sqrt(NUM_HEADS * HEAD_SIZE)
        return {'query': jax.random.normal(ks[0], (B, T, D_MODEL), jnp.float32), 'w_q': jax.random.normal(ks[1], (D_MODEL, NUM_HEADS * HEAD_SIZE), jnp.float32) * s, 'b_q': jnp.zeros((NUM_HEADS * HEAD_SIZE,), jnp.float32), 'w_k': jax.random.normal(ks[2], (D_MODEL, NUM_HEADS * HEAD_SIZE), jnp.float32) * s, 'b_k': jnp.zeros((NUM_HEADS * HEAD_SIZE,), jnp.float32), 'w_v': jax.random.normal(ks[3], (D_MODEL, NUM_HEADS * HEAD_SIZE), jnp.float32) * s, 'b_v': jnp.zeros((NUM_HEADS * HEAD_SIZE,), jnp.float32), 'w_o': jax.random.normal(ks[4], (NUM_HEADS * HEAD_SIZE, MODEL_SIZE), jnp.float32) * so, 'b_o': jnp.zeros((MODEL_SIZE,), jnp.float32)}
    _L0_attn_in = _L0_attn_setup()

    def _L0_ffn_setup():
        import jax, jax.numpy as jnp
        import numpy as np
        B, T, C = (8, 256, 256)
        E, H = (32, 64)

        def _gating(hidden_states, sim_matrix, gates):
            seq_rep = jnp.mean(hidden_states, axis=1)
            sr_n = seq_rep / jnp.linalg.norm(seq_rep, axis=-1, keepdims=True)
            sm_n = sim_matrix / jnp.linalg.norm(sim_matrix, axis=0, keepdims=True)
            affinity = sr_n @ sm_n
            logits = affinity - jax.nn.sigmoid(gates)
            gated = jax.nn.relu(logits)
            mask = (gated > 0).astype(hidden_states.dtype)
            inactive = jnp.sum(mask, axis=1) == 0
            k_fb = E // 2
            _, fb_idx = jax.lax.top_k(logits, k_fb)
            fb_mask = jnp.sum(jax.nn.one_hot(fb_idx, E, dtype=mask.dtype), axis=1)
            mask = jnp.where(inactive[:, None], jnp.maximum(mask, fb_mask), mask)
            fallback_count = jnp.sum(inactive).astype(jnp.float32)
            neg = -jnp.finfo(hidden_states.dtype).max
            routing = jax.nn.softmax(jnp.where(mask > 0, gated, neg), axis=-1)
            return (routing, mask, fallback_count)
        key = jax.random.key(seed)
        ks = jax.random.split(key, 7)
        scale = 1.0 / np.sqrt(C)
        return {'hidden_states': jax.random.normal(ks[0], (B, T, C), dtype=jnp.float32), 'sim_matrix': jax.random.normal(ks[1], (C, E), dtype=jnp.float32), 'gates': jnp.zeros((E,), dtype=jnp.float32), 'w_q': jax.random.normal(ks[2], (E, H, C), dtype=jnp.float32) * scale, 'w_k': jax.random.normal(ks[3], (E, H, C), dtype=jnp.float32) * scale, 'w_v': jax.random.normal(ks[4], (E, H, C), dtype=jnp.float32) * scale, 'o_weights': jax.random.normal(ks[5], (E, H, C), dtype=jnp.float32)}
    _L0_ffn_in = _L0_ffn_setup()

    def _L1_attn_setup():
        import math
        import jax, jax.numpy as jnp
        import numpy as np
        NUM_HEAD = 16
        EMB = 256
        HEAD_DIM = EMB // NUM_HEAD
        B, T = (2, 256)

        def get_slopes(n):
            start = 2 ** (-2 ** (-(math.log2(n) - 3)))
            return np.array([start * start ** i for i in range(n)], dtype=np.float32)
        key = jax.random.key(seed)
        ks = jax.random.split(key, 5)
        x = jax.random.normal(ks[0], (B, T, EMB), jnp.float32)

        def w(k, scale=0.02):
            return jax.random.normal(k, (EMB, EMB), jnp.float32) * scale
        return {'x': x, 'Wq': w(ks[1]), 'bq': jnp.zeros((EMB,), jnp.float32), 'Wk': w(ks[2]), 'bk': jnp.zeros((EMB,), jnp.float32), 'Wv': w(ks[3]), 'bv': jnp.zeros((EMB,), jnp.float32), 'Wo': w(ks[4], scale=0.02 / math.sqrt(24)), 'bo': jnp.zeros((EMB,), jnp.float32)}
    _L1_attn_in = _L1_attn_setup()

    def _L1_ffn_setup():
        import jax, jax.numpy as jnp
        import numpy as np
        B, S, H, I, E, K = (4, 256, 256, 512, 8, 2)
        key = jax.random.key(seed)
        k1, k2, k3, k4 = jax.random.split(key, 4)
        return {'hidden_states': jax.random.normal(k1, (B, S, H), dtype=jnp.float32), 'gate_weight': jax.random.normal(k2, (E, H), dtype=jnp.float32) * 0.02, 'gate_up_proj': jax.random.normal(k3, (E, 2 * I, H), dtype=jnp.float32) * 0.02, 'down_proj': jax.random.normal(k4, (E, H, I), dtype=jnp.float32) * 0.02}
    _L1_ffn_in = _L1_ffn_setup()
    _d = {'L0_attn_query': _L0_attn_in['query'], 'L0_attn_w_q': _L0_attn_in['w_q'], 'L0_attn_b_q': _L0_attn_in['b_q'], 'L0_attn_w_k': _L0_attn_in['w_k'], 'L0_attn_b_k': _L0_attn_in['b_k'], 'L0_attn_w_v': _L0_attn_in['w_v'], 'L0_attn_b_v': _L0_attn_in['b_v'], 'L0_attn_w_o': _L0_attn_in['w_o'], 'L0_attn_b_o': _L0_attn_in['b_o'], 'L0_ffn_sim_matrix': _L0_ffn_in['sim_matrix'], 'L0_ffn_gates': _L0_ffn_in['gates'], 'L0_ffn_w_q': _L0_ffn_in['w_q'], 'L0_ffn_w_k': _L0_ffn_in['w_k'], 'L0_ffn_w_v': _L0_ffn_in['w_v'], 'L0_ffn_o_weights': _L0_ffn_in['o_weights'], 'L1_attn_Wq': _L1_attn_in['Wq'], 'L1_attn_bq': _L1_attn_in['bq'], 'L1_attn_Wk': _L1_attn_in['Wk'], 'L1_attn_bk': _L1_attn_in['bk'], 'L1_attn_Wv': _L1_attn_in['Wv'], 'L1_attn_bv': _L1_attn_in['bv'], 'L1_attn_Wo': _L1_attn_in['Wo'], 'L1_attn_bo': _L1_attn_in['bo'], 'L1_ffn_gate_weight': _L1_ffn_in['gate_weight'], 'L1_ffn_gate_up_proj': _L1_ffn_in['gate_up_proj'], 'L1_ffn_down_proj': _L1_ffn_in['down_proj']}
    _x0 = _d['L0_attn_query']
    _d['L0_attn_query'] = jax.random.normal(jax.random.fold_in(jax.random.key(seed), 1), (2, 512, 256), dtype=_x0.dtype)
    del _x0
    return _d

def reference(L0_attn_query, L0_attn_w_q, L0_attn_b_q, L0_attn_w_k, L0_attn_b_k, L0_attn_w_v, L0_attn_b_v, L0_attn_w_o, L0_attn_b_o, L0_ffn_sim_matrix, L0_ffn_gates, L0_ffn_w_q, L0_ffn_w_k, L0_ffn_w_v, L0_ffn_o_weights, L1_attn_Wq, L1_attn_bq, L1_attn_Wk, L1_attn_bk, L1_attn_Wv, L1_attn_bv, L1_attn_Wo, L1_attn_bo, L1_ffn_gate_weight, L1_ffn_gate_up_proj, L1_ffn_down_proj):

    def _L0_attn_ref(query, w_q, b_q, w_k, b_k, w_v, b_v, w_o, b_o):
        import jax, jax.numpy as jnp
        import numpy as np
        B, T, D_MODEL = (4, 256, 256)
        NUM_HEADS, HEAD_SIZE = (16, 128)
        MODEL_SIZE = 256
        B_, T_, _ = query.shape
        q = (query @ w_q + b_q).reshape(B_, T_, NUM_HEADS, HEAD_SIZE)
        k = (query @ w_k + b_k).reshape(B_, T_, NUM_HEADS, HEAD_SIZE)
        v = (query @ w_v + b_v).reshape(B_, T_, NUM_HEADS, HEAD_SIZE)
        logits = jnp.einsum('bthd,bThd->bhtT', q, k) * jax.lax.rsqrt(jnp.float32(HEAD_SIZE))
        i = jnp.arange(T_, dtype=jnp.int32)[:, None]
        j = jnp.arange(T_, dtype=jnp.int32)
        mask = (i >= j).astype(logits.dtype)
        logits = logits - 10000000000.0 * (1.0 - mask)
        weights = jax.nn.softmax(logits, axis=-1)
        attn = jnp.einsum('bhtT,bThd->bthd', weights, v).reshape(B_, T_, NUM_HEADS * HEAD_SIZE)
        out = attn @ w_o + b_o
        return out

    def _L0_ffn_ref(hidden_states, sim_matrix, gates, w_q, w_k, w_v, o_weights):
        import jax, jax.numpy as jnp
        import numpy as np
        B, T, C = (8, 256, 256)
        E, H = (32, 64)

        def _gating(hidden_states, sim_matrix, gates):
            seq_rep = jnp.mean(hidden_states, axis=1)
            sr_n = seq_rep / jnp.linalg.norm(seq_rep, axis=-1, keepdims=True)
            sm_n = sim_matrix / jnp.linalg.norm(sim_matrix, axis=0, keepdims=True)
            affinity = sr_n @ sm_n
            logits = affinity - jax.nn.sigmoid(gates)
            gated = jax.nn.relu(logits)
            mask = (gated > 0).astype(hidden_states.dtype)
            inactive = jnp.sum(mask, axis=1) == 0
            k_fb = E // 2
            _, fb_idx = jax.lax.top_k(logits, k_fb)
            fb_mask = jnp.sum(jax.nn.one_hot(fb_idx, E, dtype=mask.dtype), axis=1)
            mask = jnp.where(inactive[:, None], jnp.maximum(mask, fb_mask), mask)
            fallback_count = jnp.sum(inactive).astype(jnp.float32)
            neg = -jnp.finfo(hidden_states.dtype).max
            routing = jax.nn.softmax(jnp.where(mask > 0, gated, neg), axis=-1)
            return (routing, mask, fallback_count)
        routing, mask, fallback_count = _gating(hidden_states, sim_matrix, gates)
        v_all = jnp.einsum('btc,ehc->bteh', hidden_states, w_v)
        full_expert_outputs = v_all * mask[:, None, :, None]
        combined = jnp.einsum('be,bteh->bth', routing, full_expert_outputs)
        w_o_dyn = jnp.einsum('be,ehd->bhd', routing, o_weights)
        final_output = jnp.einsum('bth,bhd->btd', combined, w_o_dyn)
        return final_output

    def _L1_attn_ref(x, Wq, bq, Wk, bk, Wv, bv, Wo, bo):
        import math
        import jax, jax.numpy as jnp
        import numpy as np
        NUM_HEAD = 16
        EMB = 256
        HEAD_DIM = EMB // NUM_HEAD
        B, T = (2, 256)

        def get_slopes(n):
            start = 2 ** (-2 ** (-(math.log2(n) - 3)))
            return np.array([start * start ** i for i in range(n)], dtype=np.float32)
        Bx, Tx, C = x.shape
        slopes = jnp.asarray(get_slopes(NUM_HEAD))

        def split_heads(y):
            return y.reshape(Bx, Tx, NUM_HEAD, HEAD_DIM).transpose(0, 2, 1, 3)
        q = split_heads(x @ Wq + bq)
        k = split_heads(x @ Wk + bk)
        v = split_heads(x @ Wv + bv)
        attn = jnp.einsum('bhqd,bhkd->bhqk', q, k) / jnp.sqrt(jnp.float32(HEAD_DIM))
        alibi = -slopes[:, None, None] * (Tx - 1 - jnp.arange(Tx, dtype=jnp.float32))[None, None, :]
        attn = attn + alibi
        causal = jnp.tril(jnp.ones((Tx, Tx), dtype=bool))[None, None]
        attn = jnp.where(causal, attn, jnp.finfo(jnp.float32).min)
        p = jax.nn.softmax(attn, axis=-1)
        out = jnp.einsum('bhqk,bhkd->bhqd', p, v).transpose(0, 2, 1, 3).reshape(Bx, Tx, C)
        return out @ Wo + bo

    def _L1_ffn_ref(hidden_states, gate_weight, gate_up_proj, down_proj):
        import jax, jax.numpy as jnp
        import numpy as np
        B, S, H, I, E, K = (4, 256, 256, 512, 8, 2)
        b, s, h = hidden_states.shape
        num_experts, top_k = (gate_weight.shape[0], K)
        x = hidden_states.reshape(-1, h)
        router_logits = x @ gate_weight.T
        probs = jax.nn.softmax(router_logits.astype(jnp.float32), axis=-1)
        top_v, top_i = jax.lax.top_k(probs, top_k)
        top_v = top_v / top_v.sum(axis=-1, keepdims=True)
        combine_w = jnp.einsum('tke,tk->te', jax.nn.one_hot(top_i, num_experts, dtype=top_v.dtype), top_v).astype(x.dtype)

        def expert_step(acc, inp):
            gu, dp, w = inp
            gate, up = jnp.split(x @ gu.T, 2, axis=-1)
            hidden = jax.nn.silu(gate) * up
            y = hidden @ dp.T
            return (acc + w[:, None] * y, None)
        out, _ = jax.lax.scan(expert_step, jnp.zeros_like(x), (gate_up_proj, down_proj, combine_w.T))
        return out.reshape(b, s, h)
    x = L0_attn_query
    xn = _layernorm(x, axis=-1)
    x = x + _L0_attn_ref(xn, L0_attn_w_q, L0_attn_b_q, L0_attn_w_k, L0_attn_b_k, L0_attn_w_v, L0_attn_b_v, L0_attn_w_o, L0_attn_b_o) + _L0_ffn_ref(xn, L0_ffn_sim_matrix, L0_ffn_gates, L0_ffn_w_q, L0_ffn_w_k, L0_ffn_w_v, L0_ffn_o_weights)
    xn = _layernorm(x, axis=-1)
    x = x + _L1_attn_ref(xn, L1_attn_Wq, L1_attn_bq, L1_attn_Wk, L1_attn_bk, L1_attn_Wv, L1_attn_bv, L1_attn_Wo, L1_attn_bo) + _L1_ffn_ref(xn, L1_ffn_gate_weight, L1_ffn_gate_up_proj, L1_ffn_down_proj)
    return x

_drawn_inputs = setup_inputs


def setup_inputs(seed=0):
    import zlib

    import numpy as np

    out = dict(_drawn_inputs(seed))
    spreads = {'L0_attn_b_q': (0.0, 2.0),
     'L0_attn_b_k': (0.0, 2.0),
     'L0_attn_b_v': (0.0, 0.8),
     'L0_attn_b_o': (0.0, 0.1),
     'L0_ffn_gates': (0.0, 0.1),
     'L1_attn_bq': (0.0, 0.8),
     'L1_attn_bk': (0.0, 2.0),
     'L1_attn_bv': (0.0, 0.8),
     'L1_attn_bo': (0.0, 0.1)}
    factors = {'L0_attn_w_q': 64.0,
     'L0_attn_w_k': 64.0,
     'L0_attn_w_v': 32.686,
     'L0_attn_w_o': 8.0,
     'L1_attn_Wq': 8.0,
     'L1_attn_Wk': 8.0,
     'L1_attn_Wv': 8.0,
     'L1_attn_Wo': 6.739,
     'L1_ffn_gate_weight': 4.262,
     'L1_ffn_gate_up_proj': 3.699,
     'L1_ffn_down_proj': 3.7}
    for name, (base, spread) in spreads.items():
        noise = np.random.default_rng([zlib.crc32(name.encode()), seed]).standard_normal(out[name].shape)
        drawn = base * np.exp(spread * noise) if base else spread * noise
        out[name] = jnp.asarray(drawn.astype(out[name].dtype))
    for name, factor in factors.items():
        out[name] = (out[name] * factor).astype(out[name].dtype)
    return out
```

```python
from contextlib import ExitStack

import numpy as np
import concourse.bass as bass
from concourse import mybir

ALU = mybir.AluOpType
ACT = mybir.ActivationFunctionType
AX = mybir.AxisListType.X
F32 = mybir.dt.float32
F32R = mybir.dt.float32r
BF16 = mybir.dt.bfloat16

P = 128
EPS = 1e-5
FLT_MAX = 3.4028234663852886e38
MASKED = -1e30


def mm3(pe, out, a, b, start, stop, **kw):
    (a_hi, a_lo), (b_hi, b_lo) = a, b
    pe.matmul(out, a_hi, b_hi, start=start, stop=False, **kw)
    pe.matmul(out, a_hi, b_lo, start=False, stop=False, **kw)
    return pe.matmul(out, a_lo, b_hi, start=False, stop=stop, **kw)


def build(nc, ins, out):
    x_in = ins["x"]
    T, D = x_in.shape
    B = 2
    S = T // B
    NT = T // P
    TS = S // P
    DC = D // P
    NH0 = ins["w_o0"].shape[0] * 2
    PAIRS = NH0 // 2
    E0, H0 = 32, 64
    EH = E0 * H0 // P
    NH1 = 16
    HD1 = D // NH1
    E1 = ins["w_gate_up"].shape[0]
    HALVES = ins["w_gate_up"].shape[1]
    SCALE0 = float(P) ** -0.5
    SCALE1 = float(HD1) ** -0.5
    SCORES = sum((q + 1) * P for q in range(TS))

    P_AT = [sum((j + 1) * P for j in range(q)) for q in range(TS)]
    Q_ORDER = [3, 2, 0, 1]
    T_GROUPS = [[0], [1, 3], [2]]
    T_AT, at = {}, 0
    for group in T_GROUPS:
        for kt in group:
            T_AT[kt] = at
            at += S - kt * P
    T_SPAN = [(T_AT[g[0]], sum(S - kt * P for kt in g)) for g in T_GROUPS]

    whole = ExitStack()

    def psum(name):
        return whole.enter_context(nc.psum_tensor(name, [P, 512], F32))

    banks = [psum(f"bank{n}") for n in range(8)]

    def sbuf(stack, name, shape, dt=F32):
        return stack.enter_context(nc.sbuf_tensor(name, shape, dt))

    def sem(name):
        return whole.enter_context(nc.semaphore(name))

    def wait_apart(eng, *waits):
        held = [(signal, v if isinstance(v, int) else eng.to_reg(v)) for signal, v in waits]
        eng.wait_ge(consts_done, 1)
        for signal, v in held:
            eng.wait_ge(signal, v)

    xs = sbuf(whole, "x_rows", [P, NT, D])
    acc = sbuf(whole, "added_T", [P, DC, T])
    xt_hi = sbuf(whole, "xnorm_T_hi", [P, DC, T], F32R)
    xt_lo = sbuf(whole, "xnorm_T_lo", [P, DC, T], F32R)
    ident = sbuf(whole, "ident", [P, P])
    ident_bf = sbuf(whole, "ident_bf", [P, P], BF16)
    mask_bf = sbuf(whole, "mask_bf", [P, P], BF16)
    ones = sbuf(whole, "ones", [P, P])
    zeros_bf = sbuf(whole, "zeros_bf", [P, 512], BF16)
    small = sbuf(whole, "biases", list(ins["biases"].shape))
    BQ0, BK0, BV0, BO0 = 0, NH0, 2 * NH0, 3 * NH0
    BQ1 = 3 * NH0 + DC
    BK1, BV1, BO1 = BQ1 + DC, BQ1 + 2 * DC, BQ1 + 3 * DC

    def layer_norm(tag):
        st = ExitStack()
        xn = sbuf(st, f"xnorm_{tag}", [P, NT, D])
        stats = sbuf(st, f"stats_{tag}", [P, NT, 6])
        mv = sbuf(st, f"mean_var_{tag}", [P, NT, 2])
        std = sbuf(st, f"std_{tag}", [P, NT, 2])
        stats_done = sem(f"stats_done_{tag}")
        var_done = sem(f"var_done_{tag}")
        std_done = sem(f"std_done_{tag}")
        rstd_done = sem(f"rstd_done_{tag}")
        rows_done = sem(f"rows_done_{tag}")
        turned = sem(f"turned_{tag}")
        hi_done = sem(f"xt_hi_done_{tag}")
        lo_done = sem(f"xt_lo_done_{tag}")

        def dve_part(dve, x_ready):
            for t in range(NT):
                x_ready(dve, t)
                dve.bn_stats(stats[:, t, :], xs[:, t, :]).then_inc(stats_done, 1)
            for t in range(NT):
                dve.wait_ge(stats_done, t + 1)
                dve.bn_aggr(mv[:, t, :], stats[:, t, :]).then_inc(var_done, 1)
            dve.wait_ge(var_done, NT)
            dve.tensor_scalar(std[:, :, 0], mv[:, :, 1], EPS, None, ALU.add).then_inc(var_done, 1)
            dve.wait_ge(std_done, 1)
            dve.reciprocal(std[:, :, 1], std[:, :, 0]).then_inc(rstd_done, 1)
            dve.wait_ge(rstd_done, 1)
            for t in range(NT):
                dve.tensor_scalar(xn[:, t, :], xs[:, t, :], mv[:, t, 0:1], std[:, t, 1:2],
                                  ALU.subtract, ALU.mult).then_inc(rows_done, 1)
            for n in range(2 * DC):
                dve.wait_ge(hi_done, n + 1)
                c, b = n // 2, n % 2
                at = slice(b * S, (b + 1) * S)
                dve.tensor_tensor(xt_lo[:, c, at], banks[n][:, :], xt_hi[:, c, at].bitcast(F32),
                                  ALU.subtract).then_inc(lo_done, 1)

        def act_part(act):
            act.wait_ge(var_done, NT + 1)
            act.activation(std[:, :, 0], std[:, :, 0], ACT.Sqrt).then_inc(std_done, 1)
            for n in range(2 * DC):
                act.wait_ge(turned, n + 1)
                c, b = n // 2, n % 2
                act.activation(xt_hi[:, c, b * S:(b + 1) * S], banks[n][:, :], ACT.Copy).then_inc(hi_done, 1)

        def pe_part(pe):
            for n in range(2 * DC):
                c, b = n // 2, n % 2
                for j in range(TS):
                    t = b * TS + j
                    pe.wait_ge(rows_done, t + 1)
                    mm = pe.transpose(banks[n][:, j * P:(j + 1) * P], xn[:, t, c * P:(c + 1) * P], ident[:, :])
                mm.then_inc(turned, 1)

        return st, xn, rows_done, hi_done, lo_done, dve_part, act_part, pe_part

    loaded_x = [sem(f"loaded_x{t}") for t in range(2)]
    loaded_const = sem("loaded_const")
    loaded_sim = sem("loaded_sim")
    loaded_ident = sem("loaded_ident")
    loaded_sel = sem("loaded_sel")
    loaded_ev = [sem(f"loaded_ev{t}") for t in range(2)]
    loaded_eo = [sem(f"loaded_eo{t}") for t in range(2)]
    ln0 = layer_norm("0")
    st1, xn, rows_done, hi_done, lo_done, ln_dve, ln_act, ln_pe = ln0
    with st1:
        sm = sbuf(st1, "sim", [P, DC, E0])
        gates = sbuf(st1, "gates", [B, E0])
        sr = sbuf(st1, "seq_rep", [P, DC, B])
        sq = sbuf(st1, "squares", [P, DC, B + E0])
        below = sbuf(st1, "below", [B, E0, E0])
        sel_half = sbuf(st1, "sel_half", [E0, P])
        sel_tile = sbuf(st1, "sel_tile", [E0, EH])
        same_h = sbuf(st1, "same_h", [P, H0])
        mask = sbuf(st1, "after", [P, P])
        g = sbuf(st1, "gating", [B, 16, E0])
        gs = sbuf(st1, "gating_scalars", [B, 8])
        cmp1 = sbuf(st1, "rank_gt", [B, E0, E0])
        cmp2 = sbuf(st1, "rank_eq", [B, E0, E0])
        r_T = sbuf(st1, "routing_T", [E0, B])
        r_spread = sbuf(st1, "routing_spread", [E0, EH, B])
        r_col = sbuf(st1, "routing_col", [P, EH, B])
        spread = sbuf(st1, "spread", [P, EH, B * H0])
        ev = sbuf(st1, "expert_v", [P, EH, D])
        eo = sbuf(st1, "expert_o", [P, EH, D])
        wv_hi = sbuf(st1, "mixed_v_hi", [P, DC, P], F32R)
        wv_lo = sbuf(st1, "mixed_v_lo", [P, DC, P], F32R)
        wo_hi = sbuf(st1, "mixed_o_hi", [P, D], F32R)
        wo_lo = sbuf(st1, "mixed_o_lo", [P, D], F32R)
        c_hi = sbuf(st1, "combined_hi", [P, T], F32R)
        c_lo = sbuf(st1, "combined_lo", [P, T], F32R)

        consts_done = sem("consts_done")
        rep_done = sem("rep_done")
        gate_step = sem("gate_step")
        sr_done = sem("sr_done")
        norms_done = sem("norms_done")
        gate_act = sem("gate_act")
        r_turned = sem("r_turned")
        r_sp_done = sem("r_sp_done")
        r_col_done = sem("r_col_done")
        spread_done = sem("spread_done")
        mixed = sem("mixed")
        mixed_hi = sem("mixed_hi")
        mixed_lo = sem("mixed_lo")
        comb = sem("comb")
        comb_hi = sem("comb_hi")
        comb_lo = sem("comb_lo")
        ffn_ready = sem("ffn_ready")
        ffn_acc = sem("ffn_acc")

        with nc.Block() as block:
            @block.sync
            def _(sp):
                for n in range(2):
                    half = slice(n * TS, (n + 1) * TS)
                    sp.dma_start(xs[:, half, :], x_in[n * S:(n + 1) * S, :].rearrange("(t p) d -> p t d", p=P))\
                      .then_inc(loaded_x[n], 16)
                sp.dma_start(ident[:, :], ins["ident"]).then_inc(loaded_ident, 16)
                sp.dma_start(small[:, :], ins["biases"]).then_inc(loaded_const, 16)
                sp.dma_start(sm[:, :, :], ins["sim"].rearrange("(c p) e -> p c e", p=P)).then_inc(loaded_sim, 16)
                sp.dma_start(gates[:, :], ins["gates"]).then_inc(loaded_sim, 16)
                for tile, name in ((below, "below"), (sel_half, "sel_half"), (sel_tile, "sel_tile"),
                                   (same_h, "same_h"), (mask, "after")):
                    sp.dma_start(tile[:], ins[name]).then_inc(loaded_sel, 16)
                for n in range(2):
                    h = slice(n * EH // 2, (n + 1) * EH // 2)
                    sp.dma_start(ev[:, h, :], ins["expert_v"].rearrange("(t p) d -> p t d", p=P)[:, h, :])\
                      .then_inc(loaded_ev[n], 16)
                for n in range(2):
                    h = slice(n * EH // 2, (n + 1) * EH // 2)
                    sp.dma_start(eo[:, h, :], ins["expert_o"].rearrange("(t p) d -> p t d", p=P)[:, h, :])\
                      .then_inc(loaded_eo[n], 16)

            @block.gpsimd
            def _(pool):
                pool.memset(ones[:, :], 1.0).then_inc(consts_done, 1)
                pool.memset(zeros_bf[:, :], 0.0).then_inc(consts_done, 1)
                pool.memset(c_hi[:, :].bitcast(F32), 0.0).then_inc(consts_done, 1)
                pool.memset(c_lo[:, :].bitcast(F32), 0.0).then_inc(consts_done, 1)
                pool.wait_ge(loaded_ident, 16)
                pool.tensor_scalar(ident_bf[:, :], ident[:, :], 1.0, 1.0, ALU.mult, ALU.mult)\
                    .then_inc(consts_done, 1)
                pool.wait_ge(loaded_sel, 80)
                pool.tensor_scalar(mask_bf[:, :], mask[:, :], MASKED, 1.0, ALU.mult, ALU.mult)\
                    .then_inc(consts_done, 1)

            @block.scalar
            def _(act):
                ln_act(act)
                act.wait_ge(gate_step, 2)
                act.activation(g[:, 2, :], g[:, 1, :], ACT.Sqrt).then_inc(gate_act, 1)
                act.activation(gs[:, 1:2], gs[:, 0:1], ACT.Sqrt).then_inc(gate_act, 1)
                act.wait_ge(loaded_sim, 32)
                act.activation(g[:, 3, :], gates[:, :], ACT.Exp, scale=-1.0).then_inc(gate_act, 1)
                act.wait_ge(gate_step, 20)
                act.activation(g[:, 14, :], g[:, 13, :], ACT.Exp, bias=gs[:, 4:5], scale=1.0,
                               accum_out=gs[:, 5:6]).then_inc(gate_act, 1)
                act.wait_ge(mixed, 1)
                act.activation(wv_hi[:, :, :], banks[2][:, 0:D].rearrange("p (c m) -> p c m", c=DC), ACT.Copy)\
                    .then_inc(mixed_hi, 1)
                act.wait_ge(mixed, 2)
                act.activation(wo_hi[:, :], banks[3][:, 0:D], ACT.Copy).then_inc(mixed_hi, 1)
                for b in range(B):
                    act.wait_ge(comb, b + 1)
                    act.wait_ge(consts_done, 4)
                    act.activation(c_hi[b * H0:(b + 1) * H0, b * S:(b + 1) * S], banks[b][b * H0:(b + 1) * H0, :],
                                   ACT.Copy).then_inc(comb_hi, 1)

            @block.vector
            def _(dve):
                ln_dve(dve, lambda e, t: e.wait_ge(loaded_x[t // TS], 16))
                dve.wait_ge(rep_done, 1)
                dve.tensor_scalar(sr[:, :, :], banks[4][:, 0:DC * B].rearrange("p (c b) -> p c b", c=DC),
                                  1.0 / S, None, ALU.mult).then_inc(sr_done, 1)
                dve.wait_ge(sr_done, 1)
                dve.tensor_tensor(sq[:, :, 0:B], sr[:, :, :], sr[:, :, :], ALU.mult).then_inc(sr_done, 1)
                dve.wait_ge(loaded_sim, 32)
                dve.tensor_tensor(sq[:, :, B:], sm[:, :, :], sm[:, :, :], ALU.mult).then_inc(sr_done, 1)
                steps = [0]

                def link(ins_):
                    steps[0] += 1
                    ins_.then_inc(gate_step, 1)
                    dve.wait_ge(gate_step, steps[0])

                dve.wait_ge(norms_done, 1)
                nrm = banks[5]
                link(dve.tensor_copy(g[:, 1, :], nrm[0:B, E0:2 * E0]))
                link(dve.tensor_copy(gs[:, 0:1], nrm[0:B, 2 * E0:2 * E0 + 1]))
                dve.wait_ge(gate_act, 3)
                link(dve.reciprocal(g[:, 4, :], g[:, 2, :]))
                link(dve.reciprocal(gs[:, 2:3], gs[:, 1:2]))
                link(dve.tensor_scalar(g[:, 5, :], g[:, 3, :], 1.0, None, ALU.add))
                link(dve.reciprocal(g[:, 6, :], g[:, 5, :]))
                link(dve.scalar_tensor_tensor(g[:, 7, :], nrm[0:B, 0:E0], gs[:, 2:3], g[:, 4, :],
                                              ALU.mult, ALU.mult))
                link(dve.tensor_tensor(g[:, 8, :], g[:, 7, :], g[:, 6, :], ALU.subtract))
                link(dve.tensor_scalar(g[:, 9, :], g[:, 8, :], 0.0, None, ALU.max))
                link(dve.tensor_scalar(g[:, 10, :], g[:, 9, :], 0.0, None, ALU.is_gt))
                link(dve.tensor_reduce(gs[:, 3:4], g[:, 10, :], AX, ALU.max))
                row = g[:, 8:9, :].to_broadcast([B, E0, E0])
                col = g[:, 8, :].rearrange("b (e o) -> b e o", o=1).to_broadcast([B, E0, E0])
                link(dve.tensor_tensor(cmp1[:, :, :], row, col, ALU.is_gt))
                link(dve.tensor_tensor(cmp2[:, :, :], row, col, ALU.is_equal))
                dve.wait_ge(loaded_sel, 80)
                link(dve.tensor_tensor(cmp2[:, :, :], cmp2[:, :, :], below[:, :, :], ALU.mult))
                link(dve.tensor_tensor(cmp1[:, :, :], cmp1[:, :, :], cmp2[:, :, :], ALU.add))
                link(dve.tensor_reduce(g[:, 11, :], cmp1[:, :, :], AX, ALU.add))
                link(dve.tensor_scalar(g[:, 12, :], g[:, 11, :], E0 / 2, gs[:, 3:4], ALU.is_lt, ALU.is_gt))
                link(dve.tensor_tensor(g[:, 12, :], g[:, 10, :], g[:, 12, :], ALU.max))
                link(dve.tensor_scalar(g[:, 0, :], g[:, 12, :], FLT_MAX, FLT_MAX, ALU.mult, ALU.subtract))
                dve.tensor_tensor(g[:, 13, :], g[:, 9, :], g[:, 0, :], ALU.add).then_inc(r_sp_done, 1)
                dve.wait_ge(r_sp_done, 1)
                link(dve.tensor_reduce(gs[:, 4:5], g[:, 13, :], AX, ALU.max, negate=True))
                dve.wait_ge(gate_act, 4)
                link(dve.reciprocal(gs[:, 6:7], gs[:, 5:6]))
                link(dve.scalar_tensor_tensor(g[:, 15, :], g[:, 14, :], gs[:, 6:7], g[:, 12, :],
                                              ALU.mult, ALU.mult))
                dve.wait_ge(r_turned, 1)
                dve.tensor_copy(r_T[:, :], banks[4][0:E0, 0:B]).then_inc(r_sp_done, 1)
                dve.wait_ge(r_sp_done, 2)
                dve.wait_ge(loaded_sel, 80)
                dve.tensor_tensor(r_spread[:, :, :],
                                  r_T[:, :].rearrange("e (o b) -> e o b", o=1).to_broadcast([E0, EH, B]),
                                  sel_tile[:, :].rearrange("e (t o) -> e t o", o=1).to_broadcast([E0, EH, B]),
                                  ALU.mult).then_inc(r_sp_done, 1)
                dve.wait_ge(r_col_done, 1)
                dve.tensor_copy(r_col[:, :, :], banks[5][:, 0:EH * B].rearrange("p (t b) -> p t b", b=B))\
                   .then_inc(r_sp_done, 1)
                dve.wait_ge(r_sp_done, 4)
                tb = EH * B
                dve.tensor_tensor(spread[:, :, :].rearrange("p t (b h) -> p (t b) h", b=B),
                                  same_h[:, :].rearrange("p (o h) -> p o h", o=1).to_broadcast([P, tb, H0]),
                                  r_col[:, :, :].rearrange("p t (b o) -> p (t b) o", o=1)
                                  .to_broadcast([P, tb, H0]), ALU.mult).then_inc(spread_done, 1)
                dve.wait_ge(mixed_hi, 1)
                dve.tensor_tensor(wv_lo[:, :, :], banks[2][:, 0:D].rearrange("p (c m) -> p c m", c=DC),
                                  wv_hi[:, :, :].bitcast(F32), ALU.subtract).then_inc(mixed_lo, 1)
                dve.wait_ge(mixed_hi, 2)
                dve.tensor_tensor(wo_lo[:, :], banks[3][:, 0:D], wo_hi[:, :].bitcast(F32), ALU.subtract)\
                   .then_inc(mixed_lo, 1)
                for b in range(B):
                    dve.wait_ge(comb_hi, b + 1)
                    rows, cols = slice(b * H0, (b + 1) * H0), slice(b * S, (b + 1) * S)
                    dve.tensor_tensor(c_lo[rows, cols], banks[b][rows, :], c_hi[rows, cols].bitcast(F32),
                                      ALU.subtract).then_inc(comb_lo, 1)
                dve.wait_ge(loaded_const, 16)
                for n in range(2 * DC):
                    c, b = n // 2, n % 2
                    dve.wait_ge(ffn_ready, n + 1)
                    dve.tensor_scalar(acc[:, c, b * S:(b + 1) * S], banks[4 + n][:, :],
                                      small[:, BO0 + c:BO0 + c + 1], None, ALU.add).then_inc(ffn_acc, 1)

            @block.tensor
            def _(pe):
                pe.wait_ge(loaded_ident, 16)
                pe.wait_ge(consts_done, 2)
                ln_pe(pe)
                for c in range(DC):
                    for b in range(B):
                        for j in range(TS):
                            mm = pe.matmul(banks[4][:, c * B + b:c * B + b + 1],
                                           xn[:, b * TS + j, c * P:(c + 1) * P], ones[:, 0:1],
                                           start=(j == 0), stop=(j == TS - 1))
                mm.then_inc(rep_done, 1)
                pe.wait_ge(sr_done, 3)
                pe.wait_ge(loaded_sim, 32)
                for c in range(DC):
                    pe.matmul(banks[5][0:B, 0:E0], sr[:, c, :], sm[:, c, :], start=(c == 0), stop=(c == DC - 1))
                for c in range(DC):
                    pe.matmul(banks[5][0:B, E0:2 * E0], ones[:, 0:B], sq[:, c, B:], start=(c == 0),
                              stop=(c == DC - 1))
                for c in range(DC):
                    mm = pe.matmul(banks[5][0:B, 2 * E0:2 * E0 + 1], sq[:, c, 0:B], ones[:, 0:1],
                                   start=(c == 0), stop=(c == DC - 1))
                mm.then_inc(norms_done, 1)
                pe.wait_ge(gate_step, 22)
                pe.transpose(banks[4][0:E0, 0:B], g[:, 15, :], ident[0:B, 0:B]).then_inc(r_turned, 1)
                pe.wait_ge(r_sp_done, 3)
                pe.wait_ge(loaded_sel, 80)
                pe.matmul(banks[5][:, 0:EH * B], sel_half[:, :], r_spread[:, :, :].rearrange("e t b -> e (t b)"),
                          start=True, stop=True).then_inc(r_col_done, 1)
                pe.wait_ge(spread_done, 1)
                pe.wait_ge(lo_done, 2 * DC)
                for c in range(DC):
                    for t in range(EH):
                        if c == 0 and t % (EH // 2) == 0:
                            pe.wait_ge(loaded_ev[t // (EH // 2)], 16)
                        mm = pe.matmul(banks[2][:, c * P:(c + 1) * P], ev[:, t, c * P:(c + 1) * P],
                                       spread[:, t, :], start=(t == 0), stop=(t == EH - 1))
                mm.then_inc(mixed, 1)
                for t in range(EH):
                    if t % (EH // 2) == 0:
                        pe.wait_ge(loaded_eo[t // (EH // 2)], 16)
                    mm = pe.matmul(banks[3][:, 0:D], spread[:, t, :], eo[:, t, :], start=(t == 0),
                                   stop=(t == EH - 1))
                mm.then_inc(mixed, 1)
                pe.wait_ge(mixed_lo, 1)
                for b in range(B):
                    for c in range(DC):
                        cols = slice(b * S, (b + 1) * S)
                        mm = mm3(pe, banks[b][:, :], (wv_hi[:, c, :], wv_lo[:, c, :]),
                                 (xt_hi[:, c, cols], xt_lo[:, c, cols]), c == 0, c == DC - 1)
                    mm.then_inc(comb, 1)
                pe.wait_ge(mixed_lo, 2)
                pe.wait_ge(comb_lo, 2)
                for n in range(2 * DC):
                    c, b = n // 2, n % 2
                    cols, rows = slice(b * S, (b + 1) * S), slice(c * P, (c + 1) * P)
                    mm3(pe, banks[4 + n][:, :], (wo_hi[:, rows], wo_lo[:, rows]),
                        (c_hi[:, cols], c_lo[:, cols]), True, True).then_inc(ffn_ready, 1)


    SCORE_BANK = {3: banks[0][:, 0:S], 2: banks[1][:, P:P + 3 * P], 0: banks[1][:, 0:P], 1: banks[2][:, 0:2 * P]}
    T_BANK = [banks[3], banks[4], banks[3]]

    class Attention:

        def __init__(self, tag, stack, scale):
            self.scale = scale
            self.probs = sbuf(stack, f"probs_{tag}", [P, 2, SCORES])
            self.pt_hi = sbuf(stack, f"probs_T_hi_{tag}", [P, SCORES], F32R)
            self.pt_lo = sbuf(stack, f"probs_T_lo_{tag}", [P, SCORES], F32R)
            self.row_max = sbuf(stack, f"row_max_{tag}", [P, 2, TS])
            self.neg_max = sbuf(stack, f"neg_max_{tag}", [P, 2, TS])
            self.row_sum = sbuf(stack, f"row_sum_{tag}", [P, 2, TS])
            self.recip = sbuf(stack, f"recip_{tag}", [P, 2, TS])
            self.scores_ready = sem(f"scores_ready_{tag}")
            self.max_done = sem(f"max_done_{tag}")
            self.neg_ready = sem(f"neg_ready_{tag}")
            self.probs_ready = sem(f"probs_ready_{tag}")
            self.recip_ready = sem(f"recip_ready_{tag}")
            self.norm_done = sem(f"norm_done_{tag}")
            self.t_ready = sem(f"t_ready_{tag}")
            self.t_high = sem(f"t_high_{tag}")
            self.t_low = sem(f"t_low_{tag}")

        def scores(self, pe, U, u, product):
            if u:
                pe.wait_ge(self.probs_ready, 4 * U)
            for n, group in enumerate(([3], [2, 0], [1])):
                for q in group:
                    region = SCORE_BANK[q]
                    product(pe, region, q)
                    mm = pe.matmul(region[:, q * P:(q + 1) * P], ident_bf[:, :], mask_bf[:, :],
                                   start=False, stop=True)
                mm.then_inc(self.scores_ready, 1)

        def turn(self, pe, U, u, n):
            if n == 0:
                pe.wait_ge(self.norm_done, 4 * U + 4)
            if n == 2:
                pe.wait_ge(self.t_low, 3 * U + 1)
            at = 0
            for kt in T_GROUPS[n]:
                for q in range(kt, TS):
                    mm = pe.transpose(T_BANK[n][:, at:at + P],
                                      self.probs[:, u % 2, P_AT[q] + kt * P:P_AT[q] + (kt + 1) * P], ident[:, :])
                    at += P
            mm.then_inc(self.t_ready, 1)

        def pt(self, kt):
            at = slice(T_AT[kt], T_AT[kt] + S - kt * P)
            return self.pt_hi[:, at], self.pt_lo[:, at]

        def exp(self, act, U, u, q):
            act.wait_ge(self.neg_ready, 2 * U + (1 if q == 3 else 2))
            act.activation(self.probs[:, u % 2, P_AT[q]:P_AT[q] + (q + 1) * P], SCORE_BANK[q], ACT.Exp,
                           bias=self.neg_max[:, u % 2, q:q + 1], scale=self.scale,
                           accum_out=self.row_sum[:, u % 2, q:q + 1]).then_inc(self.probs_ready, 1)

        def turned_high(self, act, U, n):
            at, w = T_SPAN[n]
            act.wait_ge(self.t_ready, 3 * U + n + 1)
            act.activation(self.pt_hi[:, at:at + w], T_BANK[n][:, 0:w], ACT.Copy).then_inc(self.t_high, 1)

        def maxima(self, dve, U, u):
            for n, q in enumerate(Q_ORDER):
                dve.wait_ge(self.scores_ready, 3 * U + (1, 2, 2, 3)[n])
                dve.tensor_reduce(self.row_max[:, u % 2, q:q + 1], SCORE_BANK[q], AX, ALU.max)\
                   .then_inc(self.max_done, 1)
                if n in (0, 3):
                    cols = slice(3, 4) if n == 0 else slice(0, 3)
                    dve.wait_ge(self.max_done, 4 * U + n + 1)
                    dve.tensor_scalar(self.neg_max[:, u % 2, cols], self.row_max[:, u % 2, cols], -self.scale,
                                      None, ALU.mult).then_inc(self.neg_ready, 1)

        def turned_low(self, dve, U, n):
            at, w = T_SPAN[n]
            dve.wait_ge(self.t_high, 3 * U + n + 1)
            dve.tensor_tensor(self.pt_lo[:, at:at + w], T_BANK[n][:, 0:w],
                              self.pt_hi[:, at:at + w].bitcast(F32), ALU.subtract).then_inc(self.t_low, 1)

        def reciprocals(self, dve, U, u):
            dve.wait_ge(self.probs_ready, 4 * U + 4)
            dve.reciprocal(self.recip[:, u % 2, :], self.row_sum[:, u % 2, :]).then_inc(self.recip_ready, 1)

        def normalise(self, pool, U, u):
            wait_apart(pool, (self.recip_ready, U + 1))
            for q in Q_ORDER:
                row = self.probs[:, u % 2, P_AT[q]:P_AT[q] + (q + 1) * P]
                pool.tensor_scalar(row, row, self.recip[:, u % 2, q:q + 1], 1.0, ALU.mult, ALU.mult)\
                    .then_inc(self.norm_done, 1)

    UNITS = 4
    RING0 = 12
    RING = 16
    with ExitStack() as st2:
        att = Attention("0", st2, SCALE0)
        qk_raw = sbuf(st2, "qk_raw", [P, 2, DC, 2, P])
        v_raw = sbuf(st2, "v_raw", [P, DC, 2 * P])
        o_raw = sbuf(st2, "o_raw", [P, 2, D])
        qk_w = [sbuf(st2, f"qk_w_{x}", [P, 2, DC, 2, P], F32R) for x in ("hi", "lo")]
        v_w = [sbuf(st2, f"v_w_{x}", [P, DC, 2 * P], F32R) for x in ("hi", "lo")]
        o_w = [sbuf(st2, f"o_w_{x}", [P, 2, D], F32R) for x in ("hi", "lo")]
        qk_T = [sbuf(st2, f"qk_T_{x}", [P, 2, UNITS, S], F32R) for x in ("hi", "lo")]
        v_rows = [sbuf(st2, f"v_rows_{x}", [P, B, TS, 2 * P], F32R) for x in ("hi", "lo")]
        attn_T = [sbuf(st2, f"attn_T_{x}", [P, 2, S], F32R) for x in ("hi", "lo")]
        O_BANK, R_BANK = banks[5], banks[6:8]

        qk_loaded = [sem(f"qk_loaded{h}") for h in range(2)]
        v_loaded = sem("v_loaded")
        o_loaded = sem("o_loaded")
        qk_split = [sem(f"qk_split{h}") for h in range(2)]
        v_split = sem("v_split")
        o_split = sem("o_split")
        ring_full = sem("ring_full")
        ring_high = sem("ring_high")
        ring_free = sem("ring_free")
        o_ready = sem("o_ready")
        o_high = sem("o_high")
        o_low = sem("o_low")
        QK_USE = [0, 2, 4, 10]
        V_USE = [6, 12]
        OUT_USE = [8, 14]
        OUT_USE_LAST = [0, 2]
        HIGHS = 12

        def pair_of(ap, j):
            return ap[j] if isinstance(j, int) else ap[bass.ds(j, 1)].rearrange("o p n -> (o p) n")

        with nc.Block() as block:
            @block.sync
            def _(sp):
                def load_qk(j, wait):
                    for h in range(2):
                        if wait is not None:
                            sp.wait_ge(qk_split[h], wait)
                        sp.dma_start(qk_raw[:, h].rearrange("p c k n -> p (c k n)"),
                                     pair_of(ins["w_qk0"][h], j)).then_inc(qk_loaded[h], 16)

                def load_v(j, wait):
                    if wait is not None:
                        sp.wait_ge(v_split, wait)
                    sp.dma_start(v_raw[:, :, :].rearrange("p c n -> p (c n)"), pair_of(ins["w_v0"], j))\
                      .then_inc(v_loaded, 16)

                def load_o(j, wait):
                    if wait is not None:
                        sp.wait_ge(o_split, wait)
                    sp.dma_start(o_raw[:, :, :].rearrange("p h n -> p (h n)"), pair_of(ins["w_o0"], j))\
                      .then_inc(o_loaded, 16)

                load_qk(0, None)
                load_v(0, None)
                load_qk(1, 2)
                load_v(1, 2)
                load_o(0, None)
                load_qk(2, 4)
                with sp.Fori(2, PAIRS - 1) as m:
                    load_v(m, 2 * m)
                    load_o(m - 1, 2 * m - 2)
                    load_qk(m + 1, 2 * m + 2)
                load_v(PAIRS - 1, 2 * PAIRS - 2)
                load_o(PAIRS - 2, 2 * PAIRS - 4)
                load_o(PAIRS - 1, 2 * PAIRS - 2)

            @block.gpsimd
            def _(pool):
                def split(raw, parts, loaded, done, j, used):
                    waits = [(loaded, 16 * (j + 1))]
                    if used is not None:
                        waits.append((ring_full, used))
                    wait_apart(pool, *waits)
                    pool.tensor_scalar(parts[0], raw, 1.0, 1.0, ALU.mult, ALU.mult).then_inc(done, 1)
                    pool.wait_ge(done, 2 * j + 1)
                    pool.tensor_tensor(parts[1], raw, parts[0].bitcast(F32), ALU.subtract).then_inc(done, 1)

                def split_qk(h, j, used):
                    split(qk_raw[:, h].rearrange("p c k n -> p (c k n)"),
                          [w[:, h].rearrange("p c k n -> p (c k n)") for w in qk_w], qk_loaded[h], qk_split[h], j,
                          used)

                def split_v(j, used):
                    split(v_raw[:, :, :], [w[:, :, :] for w in v_w], v_loaded, v_split, j, used)

                def iteration(i, project, weights):
                    used = RING0 + RING * i
                    if project:
                        split_v(i + 1, used)
                    split(o_raw[:, :, :], [w[:, :, :] for w in o_w], o_loaded, o_split, i, used)
                    for u in range(UNITS):
                        att.normalise(pool, UNITS * i + u, u)
                        if weights and u >= 2:
                            split_qk(u - 2, i + 2, used + QK_USE[u] + 2)

                split_qk(0, 0, None)
                split_qk(1, 0, None)
                split_v(0, None)
                split_qk(0, 1, 6)
                split_qk(1, 1, 8)
                with pool.Fori(0, PAIRS - 2) as i:
                    iteration(i, True, True)
                iteration(PAIRS - 2, True, False)
                iteration(PAIRS - 1, False, False)

            @block.tensor
            def _(pe):
                def take(r):
                    n = r if isinstance(r, int) else 2
                    if n >= 2:
                        pe.wait_ge(ring_free, r - 1)

                def project_qk(u, j, r, k):
                    h, b = u % 2, u // 2
                    if k == 0:
                        pe.wait_ge(qk_split[h], 2 * j + 2)
                    take(r + k)
                    for c in range(DC):
                        cols = slice(b * S, (b + 1) * S)
                        mm = mm3(pe, R_BANK[k][:, :], [w[:, h, c, k, :] for w in qk_w],
                                 (xt_hi[:, c, cols], xt_lo[:, c, cols]), c == 0, c == DC - 1)
                    mm.then_inc(ring_full, 1)

                def project_v(b, j, r):
                    pe.wait_ge(v_split, 2 * j + 2)
                    for k in range(2):
                        take(r + k)
                        for n in range(2):
                            t = b * TS + 2 * k + n
                            rows = slice(t * P, (t + 1) * P)
                            for c in range(DC):
                                mm = mm3(pe, R_BANK[k][:, n * 2 * P:(n + 1) * 2 * P],
                                         (xt_hi[:, c, rows], xt_lo[:, c, rows]), [w[:, c, :] for w in v_w],
                                         c == 0, c == DC - 1)
                        mm.then_inc(ring_full, 1)

                def project_out(b, i, r):
                    pe.wait_ge(o_split, 2 * i + 2)
                    pe.wait_ge(o_low, UNITS * i + 2 * b + 2)
                    for c in range(DC):
                        take(r + c)
                        for h in range(2):
                            mm = mm3(pe, R_BANK[c][:, :], [w[:, h, c * P:(c + 1) * P] for w in o_w],
                                     [a[:, h, :] for a in attn_T], h == 0, h == 1)
                        mm.then_inc(ring_full, 1)

                def weigh_v(U, u):
                    h, b = u % 2, u // 2
                    if u:
                        pe.wait_ge(o_low, U)
                    for kt in range(TS):
                        need = {0: 1, 1: 2, 3: 2, 2: 3}[kt]
                        pe.wait_ge(att.t_low, 3 * U + need)
                        mm = mm3(pe, O_BANK[:, kt * P:S], [v[:, b, kt, h * P:(h + 1) * P] for v in v_rows],
                                 att.pt(kt), kt == 0, kt == TS - 1)
                    mm.then_inc(o_ready, 1)

                def iteration(i, project):
                    r = RING0 + RING * i
                    outs = OUT_USE if project else OUT_USE_LAST
                    for u in range(UNITS):
                        U = UNITS * i + u

                        def product(pe_, region, q):
                            q_T = [x[:, 0, u, q * P:(q + 1) * P] for x in qk_T]
                            k_T = [x[:, 1, u, 0:(q + 1) * P] for x in qk_T]
                            mm3(pe_, region, q_T, k_T, True, False)

                        att.scores(pe, U, u, product)
                        if u:
                            att.turn(pe, U - 1, u - 1, 0)
                            att.turn(pe, U - 1, u - 1, 1)
                        if project:
                            project_qk(u, i + 1, r + QK_USE[u], 0)
                        if u:
                            att.turn(pe, U - 1, u - 1, 2)
                        if project:
                            project_qk(u, i + 1, r + QK_USE[u], 1)
                        if u:
                            weigh_v(U - 1, u - 1)
                        if u == 2:
                            if project:
                                project_v(0, i + 1, r + V_USE[0])
                            project_out(0, i, r + outs[0])
                    U = UNITS * i + 3
                    for n in range(3):
                        att.turn(pe, U, 3, n)
                    weigh_v(U, 3)
                    if project:
                        project_v(1, i + 1, r + V_USE[1])
                    project_out(1, i, r + outs[1])

                for u in range(UNITS):
                    for k in range(2):
                        project_qk(u, 0, 2 * u, k)
                for b in range(B):
                    project_v(b, 0, 8 + 2 * b)
                with pe.Fori(0, PAIRS - 1) as i:
                    iteration(i, True)
                iteration(PAIRS - 1, False)

            def bias_col(at, i, h):
                return small[:, bass.ds(2 * i + (at + h), 1)] if not isinstance(i, int) \
                    else small[:, at + 2 * i + h:at + 2 * i + h + 1]

            def v_dest(parts, b, k):
                return parts[:, b, 2 * k:2 * k + 2, :].rearrange("p t n -> p (t n)")

            @block.scalar
            def _(act):
                def high_qk(u, j, r, k):
                    wait_apart(act, (ring_full, r + k + 1))
                    act.activation(qk_T[0][:, k, u, :], R_BANK[k][:, :], ACT.Identity,
                                   bias=bias_col((BQ0, BK0)[k], j, u % 2)).then_inc(ring_high, 1)

                def high_v(b, r):
                    for k in range(2):
                        act.wait_ge(ring_full, r + k + 1)
                        act.activation(v_dest(v_rows[0], b, k), R_BANK[k][:, :], ACT.Copy).then_inc(ring_high, 1)

                def high_out(U, u, i):
                    wait_apart(act, (o_ready, U + 1))
                    act.activation(attn_T[0][:, u % 2, :], O_BANK[:, :], ACT.Identity,
                                   bias=bias_col(BV0, i, u % 2)).then_inc(o_high, 1)

                def iteration(i, project):
                    r = RING0 + RING * i
                    for u in range(UNITS):
                        U = UNITS * i + u
                        if u:
                            att.turned_high(act, U - 1, 0)
                            att.turned_high(act, U - 1, 1)
                        att.exp(act, U, u, 3)
                        if project:
                            high_qk(u, i + 1, r + QK_USE[u], 0)
                        if u:
                            att.turned_high(act, U - 1, 2)
                        att.exp(act, U, u, 2)
                        att.exp(act, U, u, 0)
                        if project:
                            high_qk(u, i + 1, r + QK_USE[u], 1)
                        att.exp(act, U, u, 1)
                        if u:
                            high_out(U - 1, u - 1, i)
                        if u == 2 and project:
                            high_v(0, r + V_USE[0])
                    U = UNITS * i + 3
                    for n in range(3):
                        att.turned_high(act, U, n)
                    high_out(U, 3, i)
                    if project:
                        high_v(1, r + V_USE[1])

                for u in range(UNITS):
                    for k in range(2):
                        high_qk(u, 0, 2 * u, k)
                for b in range(B):
                    high_v(b, 8 + 2 * b)
                with act.Fori(0, PAIRS - 1) as i:
                    iteration(i, True)
                iteration(PAIRS - 1, False)

            @block.vector
            def _(dve):
                def low_qk(u, j, n, k):
                    dve.wait_ge(ring_high, n + 1)
                    dve.scalar_tensor_tensor(qk_T[1][:, k, u, :], R_BANK[k][:, :],
                                             bias_col((BQ0, BK0)[k], j, u % 2),
                                             qk_T[0][:, k, u, :].bitcast(F32), ALU.add, ALU.subtract)\
                       .then_inc(ring_free, 1)

                def low_v(b, n):
                    for k in range(2):
                        dve.wait_ge(ring_high, n + k + 1)
                        dve.tensor_tensor(v_dest(v_rows[1], b, k), R_BANK[k][:, :],
                                          v_dest(v_rows[0], b, k).bitcast(F32), ALU.subtract)\
                           .then_inc(ring_free, 1)

                def low_out(U, u, i):
                    dve.wait_ge(o_high, U + 1)
                    dve.scalar_tensor_tensor(attn_T[1][:, u % 2, :], O_BANK[:, :], bias_col(BV0, i, u % 2),
                                             attn_T[0][:, u % 2, :].bitcast(F32), ALU.add, ALU.subtract)\
                       .then_inc(o_low, 1)

                def add_out(b, r):
                    for c in range(DC):
                        dve.wait_ge(ring_full, r + c + 1)
                        at = acc[:, c, b * S:(b + 1) * S]
                        dve.tensor_tensor(at, R_BANK[c][:, :], at, ALU.add).then_inc(ring_free, 1)

                def iteration(i, project):
                    r = RING0 + RING * i
                    n = HIGHS + HIGHS * i
                    outs = OUT_USE if project else OUT_USE_LAST
                    for u in range(UNITS):
                        U = UNITS * i + u
                        before = (0, 2, 4, 8)[u]
                        if u:
                            att.turned_low(dve, U - 1, 0)
                            att.turned_low(dve, U - 1, 1)
                        att.maxima(dve, U, u)
                        if project:
                            low_qk(u, i + 1, n + before, 0)
                        if u:
                            att.turned_low(dve, U - 1, 2)
                        if project:
                            low_qk(u, i + 1, n + before + 1, 1)
                        att.reciprocals(dve, U, u)
                        if u:
                            low_out(U - 1, u - 1, i)
                        if u == 2:
                            if project:
                                low_v(0, n + 6)
                            add_out(0, r + outs[0])
                    U = UNITS * i + 3
                    for k in range(3):
                        att.turned_low(dve, U, k)
                    low_out(U, 3, i)
                    if project:
                        low_v(1, n + 10)
                    add_out(1, r + outs[1])

                for u in range(UNITS):
                    for k in range(2):
                        low_qk(u, 0, 2 * u + k, k)
                for b in range(B):
                    low_v(b, 8 + 2 * b)
                with dve.Fori(0, PAIRS - 1) as i:
                    iteration(i, True)
                iteration(PAIRS - 1, False)

    scratch = nc.dram_tensor("head_rows", (5, D, T), F32, kind="Internal").ap()
    alibi_scratch = nc.dram_tensor("alibi_rows", (NH1, 2, T), F32, kind="Internal").ap()
    late = ExitStack()
    v1 = sbuf(late, "v1", [P, 2, NT, D], F32R)
    w_bc = sbuf(late, "expert_weight", [P, E1, T])
    wqkv_hi = sbuf(late, "w_qkvo1_hi", [P, DC, 4 * D], F32R)
    wqkv_lo = sbuf(late, "w_qkvo1_lo", [P, DC, 4 * D], F32R)
    with ExitStack() as st3:
        raw = sbuf(st3, "w_qkvo1", [P, DC, 4 * D])
        qk1 = [sbuf(st3, f"qk1_{x}", [P, 2, DC, T], F32R) for x in ("hi", "lo")]
        al = sbuf(st3, "alibi", [NH1, T])
        al_hi = sbuf(st3, "alibi_hi", [NH1, T], F32R)
        al_lo = sbuf(st3, "alibi_lo", [NH1, T], F32R)
        rw = sbuf(st3, "router", [P, DC, E1])
        before8 = sbuf(st3, "before8", [P, E1, E1])
        sel8 = sbuf(st3, "sel8", [E1, E1, P])
        lg = sbuf(st3, "router_work", [P, 6, NT, E1])
        ls = sbuf(st3, "router_scalars", [P, 4, NT])
        gt8 = sbuf(st3, "rank8_gt", [P, NT, E1, E1])
        eq8 = sbuf(st3, "rank8_eq", [P, NT, E1, E1])
        w_T = sbuf(st3, "expert_weight_T", [E1, T])

        loaded1 = sem("loaded1")
        loaded_raw1 = sem("loaded_raw1")
        acc_turned = sem("acc_turned")
        added = sem("added")
        split1 = sem("split1")
        al_split = sem("alibi_split")
        routed = sem("routed")
        route_step = sem("route_step")
        route_exp = sem("route_exp")
        w_turned = sem("w_turned")
        w_T_done = sem("w_T_done")
        bc_ready = sem("bc_ready")
        bc_act = sem("bc_act")
        bc_dve = sem("bc_dve")
        ring1_full = sem("ring1_full")
        ring1_high = sem("ring1_high")
        ring1_free = sem("ring1_free")
        stored_rows = sem("stored_rows")

        stn, xn, rows_done, hi_done, lo_done, ln_dve, ln_act, ln_pe = layer_norm("1")
        with stn, nc.Block() as block:
            @block.sync
            def _(sp):
                sp.dma_start(raw[:, :, :], ins["w_qkv1"].rearrange("(c p) n -> p c n", p=P)).then_inc(loaded_raw1, 16)
                sp.dma_start(al[:, :], ins["alibi"]).then_inc(loaded1, 16)
                sp.dma_start(rw[:, :, :], ins["router"].rearrange("(c p) e -> p c e", p=P)).then_inc(loaded1, 16)
                sp.dma_start(before8[:, :, :], ins["before8"]).then_inc(loaded1, 16)
                sp.dma_start(sel8[:, :, :], ins["sel8"]).then_inc(loaded1, 16)
                sp.wait_ge(al_split, 2)
                sp.dma_start(alibi_scratch[:, 0, :], al_hi[:, :].bitcast(F32)).then_inc(stored_rows, 16)
                sp.dma_start(alibi_scratch[:, 1, :], al_lo[:, :].bitcast(F32)).then_inc(stored_rows, 16)
                for k in range(2):
                    for m in range(DC):
                        sp.wait_ge(ring1_free, 4 * k + 2 * m + 2)
                        rows = slice(m * P, (m + 1) * P)
                        for part, which in ((0, 0), (1, 1), (2, 0)) if k == 0 else ((3, 0), (4, 1)):
                            sp.dma_start(scratch[part, rows, :], qk1[which][:, k, m, :].bitcast(F32))\
                              .then_inc(stored_rows, 16)
                sp.wait_ge(stored_rows, 16 * (2 + 5 * DC))

            @block.gpsimd
            def _(pool):
                pool.wait_ge(loaded_raw1, 16)
                for c in range(DC):
                    pool.tensor_scalar(wqkv_hi[:, c, :], raw[:, c, :], 1.0, 1.0, ALU.mult, ALU.mult)\
                        .then_inc(split1, 1)
                pool.wait_ge(loaded1, 64)
                pool.tensor_scalar(al_hi[:, :], al[:, :], 1.0, 1.0, ALU.mult, ALU.mult).then_inc(al_split, 1)
                pool.wait_ge(al_split, 1)
                pool.tensor_tensor(al_lo[:, :], al[:, :], al_hi[:, :].bitcast(F32), ALU.subtract)\
                    .then_inc(al_split, 1)
                pool.wait_ge(split1, DC)
                for c in range(DC):
                    pool.tensor_tensor(wqkv_lo[:, c, :], raw[:, c, :], wqkv_hi[:, c, :].bitcast(F32), ALU.subtract)\
                        .then_inc(split1, 1)

            @block.scalar
            def _(act):
                ln_act(act)
                for n in range(8):
                    k, m, b = n // 4, n // 2 % 2, n % 2
                    act.wait_ge(ring1_full, n + 1)
                    act.activation(qk1[0][:, k, m, b * S:(b + 1) * S], banks[6 + n % 2][:, :], ACT.Identity,
                                   bias=small[:, (BQ1, BK1)[k] + m:(BQ1, BK1)[k] + m + 1]).then_inc(ring1_high, 1)
                for n in range(4):
                    act.wait_ge(ring1_full, 9 + n)
                    act.activation(v1[:, 0, 2 * n:2 * n + 2, :], banks[6 + n % 2][:, :].rearrange(
                        "p (t d) -> p t d", d=D), ACT.Copy).then_inc(ring1_high, 1)
                act.wait_ge(route_step, 3)
                act.activation(lg[:, 2, :, :], lg[:, 1, :, :], ACT.Exp).then_inc(route_exp, 1)
                for n in range(0, 2 * E1, 2):
                    act.wait_ge(bc_ready, n + 1)
                    act.activation(w_bc[:, n // 2, 0:S], banks[n % 4][:, :], ACT.Copy).then_inc(bc_act, 1)

            @block.vector
            def _(dve):
                for n in range(4):
                    dve.wait_ge(acc_turned, n + 1)
                    rows = xs[:, 2 * n:2 * n + 2, :]
                    dve.tensor_tensor(rows, banks[4 + n][:, :].rearrange("p (t d) -> p t d", d=D), rows, ALU.add)\
                       .then_inc(added, 1)
                ln_dve(dve, lambda e, t: e.wait_ge(added, t // 2 + 1))
                for n in range(8):
                    k, m, b = n // 4, n // 2 % 2, n % 2
                    dve.wait_ge(ring1_high, n + 1)
                    at = slice(b * S, (b + 1) * S)
                    dve.scalar_tensor_tensor(qk1[1][:, k, m, at], banks[6 + n % 2][:, :],
                                             small[:, (BQ1, BK1)[k] + m:(BQ1, BK1)[k] + m + 1],
                                             qk1[0][:, k, m, at].bitcast(F32), ALU.add, ALU.subtract)\
                       .then_inc(ring1_free, 1)
                for n in range(4):
                    dve.wait_ge(ring1_high, 9 + n)
                    dve.tensor_tensor(v1[:, 1, 2 * n:2 * n + 2, :], banks[6 + n % 2][:, :].rearrange(
                        "p (t d) -> p t d", d=D), v1[:, 0, 2 * n:2 * n + 2, :].bitcast(F32), ALU.subtract)\
                       .then_inc(ring1_free, 1)
                steps = [0]

                def link(ins_):
                    steps[0] += 1
                    ins_.then_inc(route_step, 1)
                    dve.wait_ge(route_step, steps[0])

                def per_expert(col):
                    return ls[:, col, :].rearrange("p (t o) -> p t o", o=1).to_broadcast([P, NT, E1])

                dve.wait_ge(routed, 1)
                link(dve.tensor_copy(lg[:, 0, :, :], banks[4][:, 0:NT * E1].rearrange("p (t e) -> p t e", e=E1)))
                link(dve.tensor_reduce(ls[:, 0, :], lg[:, 0, :, :], AX, ALU.max))
                link(dve.tensor_tensor(lg[:, 1, :, :], lg[:, 0, :, :], per_expert(0), ALU.subtract))
                dve.wait_ge(route_exp, 1)
                link(dve.tensor_reduce(ls[:, 1, :], lg[:, 2, :, :], AX, ALU.add))
                link(dve.reciprocal(ls[:, 2, :], ls[:, 1, :]))
                link(dve.tensor_tensor(lg[:, 3, :, :], lg[:, 2, :, :], per_expert(2), ALU.mult))
                four = [P, NT, E1, E1]
                row = lg[:, 3, :, :].rearrange("p t (o j) -> p t o j", o=1).to_broadcast(four)
                col = lg[:, 3, :, :].rearrange("p t (e o) -> p t e o", o=1).to_broadcast(four)
                link(dve.tensor_tensor(gt8[:, :, :, :], row, col, ALU.is_gt))
                link(dve.tensor_tensor(eq8[:, :, :, :], row, col, ALU.is_equal))
                dve.wait_ge(loaded1, 64)
                eq = eq8[:, :, :, :].rearrange("p t e j -> p t (e j)")
                link(dve.tensor_tensor(eq, eq, before8[:, :, :].rearrange("p (o e) j -> p o (e j)", o=1)
                                       .to_broadcast([P, NT, E1 * E1]), ALU.mult))
                link(dve.tensor_tensor(gt8[:, :, :, :], gt8[:, :, :, :], eq8[:, :, :, :], ALU.add))
                link(dve.tensor_reduce(lg[:, 4, :, :], gt8[:, :, :, :], AX, ALU.add))
                link(dve.scalar_tensor_tensor(lg[:, 5, :, :].rearrange("p t e -> p (t e)"),
                                              lg[:, 4, :, :].rearrange("p t e -> p (t e)"), 2.0,
                                              lg[:, 3, :, :].rearrange("p t e -> p (t e)"), ALU.is_lt, ALU.mult))
                link(dve.tensor_reduce(ls[:, 3, :], lg[:, 5, :, :], AX, ALU.add))
                link(dve.reciprocal(ls[:, 0, :], ls[:, 3, :]))
                link(dve.tensor_tensor(lg[:, 0, :, :], lg[:, 5, :, :], per_expert(0), ALU.mult))
                for n in range(2):
                    dve.wait_ge(w_turned, n + 1)
                    dve.tensor_copy(w_T[:, n * S:(n + 1) * S], banks[4 + n][0:E1, :]).then_inc(w_T_done, 1)
                for n in range(1, 2 * E1, 2):
                    dve.wait_ge(bc_ready, n + 1)
                    dve.tensor_copy(w_bc[:, n // 2, S:T], banks[n % 4][:, :]).then_inc(bc_dve, 1)

            @block.tensor
            def _(pe):
                for t in range(NT):
                    for c in range(DC):
                        at = (t % 2) * D + c * P
                        mm = pe.transpose(banks[4 + t // 2][:, at:at + P], acc[:, c, t * P:(t + 1) * P], ident[:, :])
                    if t % 2:
                        mm.then_inc(acc_turned, 1)
                ln_pe(pe)
                pe.wait_ge(lo_done, 2 * DC)
                pe.wait_ge(loaded1, 64)
                for t in range(NT):
                    n = 0
                    for c in range(DC):
                        for part in (xt_hi, xt_lo):
                            mm = pe.matmul(banks[4][:, t * E1:(t + 1) * E1],
                                           part[:, c, t * P:(t + 1) * P].bitcast(F32), rw[:, c, :],
                                           start=(n == 0), stop=(n == 2 * DC - 1))
                            n += 1
                mm.then_inc(routed, 1)
                pe.wait_ge(split1, 2 * DC)
                for n in range(8):
                    k, m, b = n // 4, n // 2 % 2, n % 2
                    if n >= 2:
                        pe.wait_ge(ring1_free, n - 1)
                    w = slice(k * D + m * P, k * D + (m + 1) * P)
                    cols = slice(b * S, (b + 1) * S)
                    for c in range(DC):
                        mm = mm3(pe, banks[6 + n % 2][:, :], (wqkv_hi[:, c, w], wqkv_lo[:, c, w]),
                                 (xt_hi[:, c, cols], xt_lo[:, c, cols]), c == 0, c == DC - 1)
                    mm.then_inc(ring1_full, 1)
                for n in range(4):
                    pe.wait_ge(ring1_free, 8 + n - 1)
                    for t in (2 * n, 2 * n + 1):
                        rows = slice(t * P, (t + 1) * P)
                        for c in range(DC):
                            mm = mm3(pe, banks[6 + n % 2][:, (t % 2) * D:(t % 2 + 1) * D],
                                     (xt_hi[:, c, rows], xt_lo[:, c, rows]),
                                     (wqkv_hi[:, c, 2 * D:3 * D], wqkv_lo[:, c, 2 * D:3 * D]), c == 0, c == DC - 1)
                    mm.then_inc(ring1_full, 1)
                pe.wait_ge(route_step, 15)
                for t in range(NT):
                    mm = pe.transpose(banks[4 + t // TS][0:E1, (t % TS) * P:(t % TS + 1) * P], lg[:, 0, t, :],
                                      ident[:, :])
                    if t % TS == TS - 1:
                        mm.then_inc(w_turned, 1)
                pe.wait_ge(w_T_done, 2)
                for n in range(2 * E1):
                    if n >= 4:
                        pe.wait_ge((bc_act, bc_dve)[n % 2], (n - 4) // 2 + 1)
                    pe.matmul(banks[n % 4][:, :], sel8[:, n // 2, :], w_T[:, (n % 2) * S:(n % 2 + 1) * S],
                              start=True, stop=True).then_inc(bc_ready, 1)

    GROUPS = D // P
    GROUP_PAIRS = P // HD1 // 2
    KR = 4 * HD1 + 2
    a1_hi = sbuf(late, "attn1_T_hi", [P, GROUPS, T], F32R)
    a1_lo = sbuf(late, "attn1_T_lo", [P, GROUPS, T], F32R)
    with ExitStack() as st4:
        att = Attention("1", st4, SCALE1)
        q4 = sbuf(st4, "q_rows", [KR, 2, T], F32R)
        k4 = sbuf(st4, "k_rows", [KR, 2, T], F32R)
        PAD = 2 * HD1
        vz = sbuf(st4, "v_placed", [P, 2, 2 * NT, PAD + P], F32R)
        none = sbuf(st4, "none", [P, 2 * NT, HD1])
        rows_loaded = [sem(f"rows_loaded{h}") for h in range(2)]
        q4_ones = sem("q4_ones")
        cleared = sem("cleared")
        placed = sem("placed")
        pv_done = sem("pv_done")
        o1_ready = sem("o1_ready")
        o1_high = sem("o1_high")
        o1_low = sem("o1_low")
        O_BANKS = banks[5:7]

        with nc.Block() as block:
            @block.sync
            def _(sp):
                def load(j, h, wait):
                    if wait is not None:
                        sp.wait_ge(att.scores_ready, wait)
                    at = (2 * j + h) * HD1
                    rows = slice(at, at + HD1) if isinstance(j, int) else bass.ds(at, HD1)
                    for tile, parts in ((q4, (0, 1, 1, 2)), (k4, (3, 4, 3, 4))):
                        for n, part in enumerate(parts):
                            sp.dma_start(tile[n * HD1:(n + 1) * HD1, h, :].bitcast(F32), scratch[part, rows, :])\
                              .then_inc(rows_loaded[h], 16)
                    head = slice(2 * j + h, 2 * j + h + 1) if isinstance(j, int) else bass.ds(2 * j + h, 1)
                    sp.dma_start(k4[4 * HD1:KR, h, :].bitcast(F32),
                                 alibi_scratch[head].rearrange("o k t -> (o k) t")).then_inc(rows_loaded[h], 16)

                for h in range(2):
                    load(0, h, None)
                with sp.Fori(1, NH1 // 2) as j:
                    for h in range(2):
                        load(j, h, 3 * (4 * j - 4 + 2 * h + 2))

            @block.gpsimd
            def _(pool):
                pool.memset(q4[4 * HD1:KR, :, :].bitcast(F32), 1.0).then_inc(q4_ones, 1)
                pool.wait_ge(q4_ones, 1)
                pool.memset(vz[:, :, :, :].bitcast(F32), 0.0).then_inc(cleared, 1)
                pool.memset(none[:, :, :], 0.0).then_inc(cleared, 1)
                pool.wait_ge(cleared, 2)
                for grp in range(GROUPS):
                    if grp:
                        pool.wait_ge(pv_done, (4 * GROUP_PAIRS + B) * grp)
                        pool.memset(vz[:, :, :, P:PAD + P].bitcast(F32), 0.0).then_inc(cleared, 1)
                        pool.wait_ge(cleared, 2 + grp)
                    with pool.Fori(0, GROUP_PAIRS) as i:
                        for h in range(2):
                            at = i * PAD + h * HD1
                            used = 16 * grp + 4 * i
                            pool.wait_ge(pv_done, used + B * (grp + 1) + (2 * h - 2 if grp or h else 0))
                            pool.tensor_copy(vz[:, h, :, bass.ds(at, HD1)], none[:, :, :].bitcast(F32R))\
                                .then_inc(placed, 1)
                            pool.tensor_copy(vz[:, h, :, bass.ds(at + PAD, HD1)],
                                             v1[:, :, :, bass.ds(at + grp * P, HD1)]
                                             .rearrange("p k t d -> p (k t) d")).then_inc(placed, 1)
                            for b in range(B):
                                att.normalise(pool, used + 2 * h + b, 2 * h + b)

            @block.tensor
            def _(pe):
                pe.wait_ge(q4_ones, 1)

                def product_of(u):
                    h, b = u // 2, u % 2

                    def product(pe_, region, q):
                        pe.matmul(region, q4[:, h, b * S + q * P:b * S + (q + 1) * P],
                                  k4[:, h, b * S:b * S + (q + 1) * P], start=True, stop=False)
                    return product

                def weigh_v(grp, i, U, u):
                    h, b = u // 2, u % 2
                    if b == 0:
                        pe.wait_ge(placed, 4 * (GROUP_PAIRS * grp + i) + 2 * h + 2)
                    for kt in range(TS):
                        need = {0: 1, 1: 2, 3: 2, 2: 3}[kt]
                        pe.wait_ge(att.t_low, 3 * U + need)
                        v = [vz[:, h, k * NT + b * TS + kt, PAD:PAD + P] for k in range(2)]
                        mm = mm3(pe, O_BANKS[b][:, kt * P:S], v, att.pt(kt), False, False, skip_group_check=True)
                    mm.then_inc(pv_done, 1)

                for grp in range(GROUPS):
                    if grp:
                        pe.wait_ge(o1_low, B * grp)
                    for b in range(B):
                        pe.matmul(O_BANKS[b][:, :], zeros_bf[:, 0:P], zeros_bf[:, :], start=True, stop=False,
                                  skip_group_check=True).then_inc(pv_done, 1)
                    with pe.Fori(0, GROUP_PAIRS) as i:
                        for u in range(4):
                            U = 4 * (GROUP_PAIRS * grp + i) + u
                            if u % 2 == 0:
                                pe.wait_ge(rows_loaded[u // 2], 9 * 16 * (GROUP_PAIRS * grp + i + 1))
                            att.scores(pe, U, u, product_of(u))
                            if u:
                                for n in range(3):
                                    att.turn(pe, U - 1, u - 1, n)
                                weigh_v(grp, i, U - 1, u - 1)
                        for n in range(3):
                            att.turn(pe, U, 3, n)
                        weigh_v(grp, i, U, 3)
                    for b in range(B):
                        pe.matmul(O_BANKS[b][:, :], zeros_bf[:, 0:P], zeros_bf[:, :], start=False, stop=True,
                                  skip_group_check=True).then_inc(o1_ready, 1)

            @block.scalar
            def _(act):
                for grp in range(GROUPS):
                    with act.Fori(0, GROUP_PAIRS) as i:
                        for u in range(4):
                            U = 4 * (GROUP_PAIRS * grp + i) + u
                            if u:
                                att.turned_high(act, U - 1, 0)
                                att.turned_high(act, U - 1, 1)
                            att.exp(act, U, u, 3)
                            if u:
                                att.turned_high(act, U - 1, 2)
                            for q in (2, 0, 1):
                                att.exp(act, U, u, q)
                        for n in range(3):
                            att.turned_high(act, U, n)
                    for b in range(B):
                        act.wait_ge(o1_ready, B * grp + b + 1)
                        act.activation(a1_hi[:, grp, b * S:(b + 1) * S], O_BANKS[b][:, :], ACT.Identity,
                                       bias=small[:, BV1 + grp:BV1 + grp + 1]).then_inc(o1_high, 1)

            @block.vector
            def _(dve):
                for grp in range(GROUPS):
                    with dve.Fori(0, GROUP_PAIRS) as i:
                        for u in range(4):
                            U = 4 * (GROUP_PAIRS * grp + i) + u
                            if u:
                                att.turned_low(dve, U - 1, 0)
                                att.turned_low(dve, U - 1, 1)
                            att.maxima(dve, U, u)
                            if u:
                                att.turned_low(dve, U - 1, 2)
                            att.reciprocals(dve, U, u)
                        for n in range(3):
                            att.turned_low(dve, U, n)
                    for b in range(B):
                        dve.wait_ge(o1_high, B * grp + b + 1)
                        at = slice(b * S, (b + 1) * S)
                        dve.scalar_tensor_tensor(a1_lo[:, grp, at], O_BANKS[b][:, :], small[:, BV1 + grp:BV1 + grp + 1],
                                                 a1_hi[:, grp, at].bitcast(F32), ALU.add, ALU.subtract)\
                           .then_inc(o1_low, 1)

    HALF = ins["w_down"].shape[3] // D * P
    IC = HALF // P
    with late, ExitStack() as st5:
        w1_raw = sbuf(st5, "w1_raw", [P, DC, 2, HALF])
        w2_raw = sbuf(st5, "w2_raw", [P, IC, D])
        w1 = [sbuf(st5, f"w1_{x}", [P, 2, DC, 2, HALF], F32R) for x in ("hi", "lo")]
        w2 = [sbuf(st5, f"w2_{x}", [P, 2, IC, D], F32R) for x in ("hi", "lo")]
        silu = sbuf(st5, "silu_gate", [P, 2, S])
        gated = sbuf(st5, "gated_up", [P, 2, S])
        weighed = sbuf(st5, "weighed", [P, 2, S])
        hid = [sbuf(st5, f"hidden_{x}", [P, B, IC, S], F32R) for x in ("hi", "lo")]
        w1_loaded = sem("w1_loaded")
        w2_loaded = sem("w2_loaded")
        w1_split = sem("w1_split")
        w2_split = sem("w2_split")
        gu_ready = sem("gu_ready")
        silu_done = sem("silu_done")
        up_done = sem("up_done")
        weigh_done = sem("weigh_done")
        hid_high = sem("hid_high")
        hid_low = sem("hid_low")
        down_done = sem("down_done")
        sums_ready = sem("sums_ready")
        sums_copied = sem("sums_copied")
        out_turned = sem("out_turned")
        out_added = sem("out_added")
        stored = sem("stored")
        Y_BANK = banks[0:4]
        NHALF = E1 * HALVES

        with nc.Block() as block:
            @block.sync
            def _(sp):
                def load(e, hf, j):
                    if not (isinstance(j, int) and j == 0):
                        sp.wait_ge(w1_split, 2 * j)
                        sp.wait_ge(w2_split, 2 * j)
                    at = e if isinstance(e, int) else bass.ds(e, 1)
                    w1_src, w2_src = ins["w_gate_up"][at, hf], ins["w_down"][at, hf]
                    if not isinstance(e, int):
                        w1_src, w2_src = (w.rearrange("o p n -> (o p) n") for w in (w1_src, w2_src))
                    sp.dma_start(w1_raw[:, :, :, :].rearrange("p c k n -> p (c k n)"), w1_src)\
                      .then_inc(w1_loaded, 16)
                    sp.dma_start(w2_raw[:, :, :].rearrange("p c n -> p (c n)"), w2_src).then_inc(w2_loaded, 16)

                for hf in range(2):
                    load(0, hf, hf)
                with sp.Fori(1, E1) as e:
                    for hf in range(2):
                        load(e, hf, 2 * e + hf)
                for n in range(4):
                    sp.wait_ge(out_added, n + 1)
                    sp.dma_start(out[2 * n * P:(2 * n + 2) * P, :].rearrange("(t p) d -> p t d", p=P),
                                 xs[:, 2 * n:2 * n + 2, :]).then_inc(stored, 16)
                sp.wait_ge(stored, 64)

            @block.gpsimd
            def _(pool):
                def split(raw_, parts, loaded, done, j, used):
                    wait_apart(pool, (loaded, 16 * (j + 1)), *used)
                    pool.tensor_scalar(parts[0], raw_, 1.0, 1.0, ALU.mult, ALU.mult).then_inc(done, 1)
                    pool.wait_ge(done, 2 * j + 1)
                    pool.tensor_tensor(parts[1], raw_, parts[0].bitcast(F32), ALU.subtract).then_inc(done, 1)

                def split_w1(slot, j, *used):
                    split(w1_raw[:, :, :, :].rearrange("p c k n -> p (c k n)"),
                          [w[:, slot].rearrange("p c k n -> p (c k n)") for w in w1], w1_loaded, w1_split, j, used)

                def split_w2(slot, j, *used):
                    split(w2_raw[:, :, :], [w[:, slot] for w in w2], w2_loaded, w2_split, j, used)

                def half(e, hf, more, first):
                    j = 2 * e + hf
                    for k in range(2 * IC):
                        s, b = 4 * j + k, k // IC
                        waits = [(up_done, s + 1)]
                        if not (first and k < 2):
                            waits.append((hid_low, s - 1))
                        wait_apart(pool, *waits)
                        weight = (w_bc[:, e, b * S:(b + 1) * S] if isinstance(e, int) else
                                  w_bc[:, bass.ds(e, 1), b * S:(b + 1) * S].rearrange("p o t -> p (o t)"))
                        pool.tensor_tensor(weighed[:, k % 2, :], gated[:, k % 2, :], weight, ALU.mult)\
                            .then_inc(weigh_done, 1)
                        if more and k == 0:
                            split_w1(1 - hf, j + 1, *([] if first else [(gu_ready, 4 * j)]))
                        if more and k == 2:
                            split_w2(1 - hf, j + 1, *([] if first else [(down_done, 2 * j)]))

                split_w1(0, 0)
                split_w2(0, 0)
                half(0, 0, True, True)
                half(0, 1, True, False)
                with pool.Fori(1, E1 - 1) as e:
                    half(e, 0, True, False)
                    half(e, 1, True, False)
                half(E1 - 1, 0, True, False)
                half(E1 - 1, 1, False, False)

            @block.tensor
            def _(pe):
                for n in range(2 * DC):
                    c, b = n // 2, n % 2
                    w = slice(3 * D + c * P, 3 * D + (c + 1) * P)
                    for grp in range(GROUPS):
                        at = slice(b * S, (b + 1) * S)
                        mm3(pe, Y_BANK[n][:, :], (wqkv_hi[:, grp, w], wqkv_lo[:, grp, w]),
                            (a1_hi[:, grp, at], a1_lo[:, grp, at]), grp == 0, False, skip_group_check=True)

                def down(g, hf, b, last=False):
                    pe.wait_ge(hid_low, 2 * g + 2)
                    for c in range(DC):
                        for ic in range(IC):
                            mm = mm3(pe, Y_BANK[2 * c + b][:, :], [w[:, hf, ic, c * P:(c + 1) * P] for w in w2],
                                     [h[:, b, ic, :] for h in hid], False, last and ic == IC - 1,
                                     skip_group_check=True)
                    mm.then_inc(down_done, 1)

                def expert(e, first):
                    for hf in range(2):
                        j = 2 * e + hf
                        pe.wait_ge(w1_split, 2 * j + 2)
                        for b in range(B):
                            g = 2 * j + b
                            for ic in range(IC):
                                s = 2 * g + ic
                                if not (first and hf == 0 and b == 0):
                                    pe.wait_ge(up_done, s - 1)
                                for k in range(2):
                                    for c in range(DC):
                                        at = slice(b * S, (b + 1) * S)
                                        mm = mm3(pe, banks[4 + 2 * ic + k][:, :],
                                                 [w[:, hf, c, k, ic * P:(ic + 1) * P] for w in w1],
                                                 (xt_hi[:, c, at], xt_lo[:, c, at]), c == 0, c == DC - 1)
                                mm.then_inc(gu_ready, 1)
                            if not (first and hf == 0 and b == 0):
                                if b == 1:
                                    pe.wait_ge(w2_split, 2 * j + 2)
                                down(g - 1, hf if b else 1 - hf, 1 - b)

                expert(0, True)
                with pe.Fori(1, E1) as e:
                    expert(e, False)
                down(2 * NHALF - 1, 1, 1, last=True)
                for b in range(B - 1):
                    pass
                pe.matmul(Y_BANK[0][:, :], zeros_bf[:, 0:P], zeros_bf[:, :], start=False, stop=True,
                          skip_group_check=True)
                pe.matmul(Y_BANK[2][:, :], zeros_bf[:, 0:P], zeros_bf[:, :], start=False, stop=True,
                          skip_group_check=True).then_inc(sums_ready, 1)
                pe.wait_ge(sums_copied, 4)
                for t in range(NT):
                    for c in range(DC):
                        at = (t % 2) * D + c * P
                        mm = pe.transpose(banks[4 + t // 2][:, at:at + P], acc[:, c, t * P:(t + 1) * P], ident[:, :])
                    if t % 2:
                        mm.then_inc(out_turned, 1)

            @block.scalar
            def _(act):
                def step(s, k, lag):
                    act.wait_ge(gu_ready, s + 1)
                    act.activation(silu[:, k % 2, :], banks[4 + 2 * (k % 2)][:, :], ACT.Silu).then_inc(silu_done, 1)
                    if lag:
                        high(s - 1, (k - 1) % 4)

                def high(s, k):
                    act.wait_ge(weigh_done, s + 1)
                    act.activation(hid[0][:, k // 2, k % 2, :], weighed[:, k % 2, :], ACT.Copy).then_inc(hid_high, 1)

                for k in range(8):
                    step(k, k % 4, k > 0)
                with act.Fori(1, E1) as e:
                    for k in range(8):
                        step(8 * e + k, k % 4, True)
                high(4 * NHALF - 1, 3)

            @block.vector
            def _(dve):
                def step(s, k, lag):
                    dve.wait_ge(silu_done, s + 1)
                    dve.tensor_tensor(gated[:, k % 2, :], banks[5 + 2 * (k % 2)][:, :], silu[:, k % 2, :], ALU.mult)\
                       .then_inc(up_done, 1)
                    if lag:
                        low(s - 1, (k - 1) % 4)

                def low(s, k):
                    dve.wait_ge(hid_high, s + 1)
                    dve.tensor_tensor(hid[1][:, k // 2, k % 2, :], weighed[:, k % 2, :],
                                      hid[0][:, k // 2, k % 2, :].bitcast(F32), ALU.subtract).then_inc(hid_low, 1)

                for k in range(8):
                    step(k, k % 4, k > 0)
                with dve.Fori(1, E1) as e:
                    for k in range(8):
                        step(8 * e + k, k % 4, True)
                low(4 * NHALF - 1, 3)
                dve.wait_ge(sums_ready, 1)
                for n in range(2 * DC):
                    c, b = n // 2, n % 2
                    dve.tensor_scalar(acc[:, c, b * S:(b + 1) * S], Y_BANK[n][:, :],
                                      small[:, BO1 + c:BO1 + c + 1], None, ALU.add).then_inc(sums_copied, 1)
                for n in range(4):
                    dve.wait_ge(out_turned, n + 1)
                    rows = xs[:, 2 * n:2 * n + 2, :]
                    dve.tensor_tensor(rows, banks[4 + n][:, :].rearrange("p (t d) -> p t d", d=D), rows, ALU.add)\
                       .then_inc(out_added, 1)
    whole.close()


def kernel(**inputs):
    import concourse.bacc as bacc
    from concourse.bass_utils import run_bass_kernel_spmd

    def layout(a):
        return np.ascontiguousarray(a)

    x = np.asarray(inputs["L0_attn_query"])
    B, S, D = x.shape
    DC = D // P
    w_q, w_k, w_v, w_o = (np.asarray(inputs[f"L0_attn_w_{n}"]) for n in "qkvo")
    pairs = w_q.shape[1] // (2 * P)
    qk = np.stack([w_q, w_k]).reshape(2, DC, P, pairs, 2, P).transpose(4, 3, 2, 1, 0, 5)
    v = w_v.reshape(DC, P, pairs, 2 * P).transpose(2, 1, 0, 3)
    o = w_o.reshape(pairs, 2, P, D).transpose(0, 2, 1, 3)

    def columns(name):
        return np.asarray(inputs[name]).reshape(-1, P).T

    biases = np.concatenate([columns(f"L0_attn_b_{n}") for n in "qkvo"]
                            + [columns(f"L1_attn_b{n}") for n in "qkvo"], axis=1)
    e0 = inputs["L0_ffn_sim_matrix"].shape[1]
    e = np.arange(e0)
    p = np.arange(P)
    width = inputs["L0_ffn_w_v"].shape[1]
    gate_up = np.asarray(inputs["L1_ffn_gate_up_proj"])
    down = np.asarray(inputs["L1_ffn_down_proj"])
    e1, two_i, _ = gate_up.shape
    half = two_i // 4
    gu = gate_up.reshape(e1, 2, 2, half, DC, P).transpose(0, 2, 5, 4, 1, 3)
    dn = down.reshape(e1, D, 2, half // P, P).transpose(0, 2, 4, 3, 1)
    nh1 = 16
    start = 2 ** (-2 ** (-(np.log2(nh1) - 3)))
    slopes = np.array([start * start ** i for i in range(nh1)], dtype=np.float32)
    alibi = (-slopes[:, None] * (S - 1 - np.arange(S, dtype=np.float32))[None, :]).astype(np.float32)
    alibi = np.concatenate([alibi] * B, axis=1) * np.float32(np.sqrt(D // nh1))

    arrays = {
        "x": layout(x.reshape(B * S, D)),
        "w_qk0": layout(qk.reshape(2, pairs, P, DC * 2 * P)),
        "w_v0": layout(v.reshape(pairs, P, DC * 2 * P)),
        "w_o0": layout(o.reshape(pairs, P, 2 * D)),
        "biases": layout(biases),
        "sim": layout(inputs["L0_ffn_sim_matrix"]),
        "gates": layout(np.broadcast_to(np.asarray(inputs["L0_ffn_gates"]), (B, e0))),
        "expert_v": layout(np.asarray(inputs["L0_ffn_w_v"]).reshape(e0 * width, D)),
        "expert_o": layout(np.asarray(inputs["L0_ffn_o_weights"]).reshape(e0 * width, D)),
        "w_qkv1": layout(np.concatenate([np.asarray(inputs[f"L1_attn_W{n}"]) for n in "qkvo"], axis=1)),
        "router": layout(np.asarray(inputs["L1_ffn_gate_weight"]).T),
        "w_gate_up": layout(gu.reshape(e1, 2, P, DC * 2 * half)),
        "w_down": layout(dn.reshape(e1, 2, P, (half // P) * D)),
        "ident": np.eye(P, dtype=np.float32),
        "after": (p[None, :] > p[:, None]).astype(np.float32),
        "below": layout(np.broadcast_to(e[None, :] < e[:, None], (B, e0, e0)).astype(np.float32)),
        "sel_half": (e[:, None] % 2 == p[None, :] // width).astype(np.float32),
        "sel_tile": (e[:, None] // 2 == np.arange(e0 * width // P)[None, :]).astype(np.float32),
        "same_h": (p[:, None] % width == np.arange(width)[None, :]).astype(np.float32),
        "alibi": layout(alibi),
        "before8": layout(np.broadcast_to(np.arange(e1)[None, :] < np.arange(e1)[:, None],
                                          (P, e1, e1)).astype(np.float32)),
        "sel8": layout(np.repeat(np.eye(e1, dtype=np.float32)[:, :, None], P, axis=2)),
    }
    nc = bacc.Bacc("TRN2", target_bir_lowering=False, num_devices=1)
    ins = {n: nc.dram_tensor(f"in_{n}", a.shape, mybir.dt.from_np(a.dtype), kind="ExternalInput").ap()
           for n, a in arrays.items()}
    out = nc.dram_tensor("out_x", (B * S, D), F32, kind="ExternalOutput").ap()
    build(nc, ins, out)
    r = run_bass_kernel_spmd(nc, [{f"in_{n}": a for n, a in arrays.items()}], core_ids=[0])
    return r.results[0]["out_x"].reshape(B, S, D)
```

```python
from contextlib import ExitStack

import numpy as np
import concourse.bass as bass
from concourse import mybir

ALU = mybir.AluOpType
ACT = mybir.ActivationFunctionType
AX = mybir.AxisListType.X
F32 = mybir.dt.float32
F32R = mybir.dt.float32r
BF16 = mybir.dt.bfloat16

P = 128
EPS = 1e-5
FLT_MAX = 3.4028234663852886e38
MASKED = -1e30


def mm3(pe, out, a, b, start, stop, **kw):
    (a_hi, a_lo), (b_hi, b_lo) = a, b
    pe.matmul(out, a_hi, b_hi, start=start, stop=False, **kw)
    pe.matmul(out, a_hi, b_lo, start=False, stop=False, **kw)
    return pe.matmul(out, a_lo, b_hi, start=False, stop=stop, **kw)


def build(nc, ins, out):
    x_in = ins["x"]
    T, D = x_in.shape
    B = 2
    S = T // B
    NT = T // P
    TS = S // P
    DC = D // P
    NH0 = ins["w_o0"].shape[0] * 2
    PAIRS = NH0 // 2
    E0, H0 = 32, 64
    EH = E0 * H0 // P
    NH1 = 16
    HD1 = D // NH1
    E1 = ins["w_gate_up"].shape[0]
    HALVES = ins["w_gate_up"].shape[1]
    SCALE0 = float(P) ** -0.5
    SCALE1 = float(HD1) ** -0.5
    SCORES = sum((q + 1) * P for q in range(TS))

    P_AT = [sum((j + 1) * P for j in range(q)) for q in range(TS)]
    Q_ORDER = [3, 2, 0, 1]
    T_GROUPS = [[0], [1, 3], [2]]
    T_AT, at = {}, 0
    for group in T_GROUPS:
        for kt in group:
            T_AT[kt] = at
            at += S - kt * P
    T_SPAN = [(T_AT[g[0]], sum(S - kt * P for kt in g)) for g in T_GROUPS]

    whole = ExitStack()

    def psum(name):
        return whole.enter_context(nc.psum_tensor(name, [P, 512], F32))

    banks = [psum(f"bank{n}") for n in range(8)]

    def sbuf(stack, name, shape, dt=F32):
        return stack.enter_context(nc.sbuf_tensor(name, shape, dt))

    def sem(name):
        return whole.enter_context(nc.semaphore(name))

    def wait_apart(eng, *waits):
        held = [(signal, v if isinstance(v, int) else eng.to_reg(v)) for signal, v in waits]
        eng.wait_ge(consts_done, 1)
        for signal, v in held:
            eng.wait_ge(signal, v)

    xs = sbuf(whole, "x_rows", [P, NT, D])
    acc = sbuf(whole, "added_T", [P, DC, T])
    xt_hi = sbuf(whole, "xnorm_T_hi", [P, DC, T], F32R)
    xt_lo = sbuf(whole, "xnorm_T_lo", [P, DC, T], F32R)
    ident = sbuf(whole, "ident", [P, P])
    ident_bf = sbuf(whole, "ident_bf", [P, P], BF16)
    mask_bf = sbuf(whole, "mask_bf", [P, P], BF16)
    ones = sbuf(whole, "ones", [P, P])
    zeros_bf = sbuf(whole, "zeros_bf", [P, 512], BF16)
    small = sbuf(whole, "biases", list(ins["biases"].shape))
    BQ0, BK0, BV0, BO0 = 0, NH0, 2 * NH0, 3 * NH0
    BQ1 = 3 * NH0 + DC
    BK1, BV1, BO1 = BQ1 + DC, BQ1 + 2 * DC, BQ1 + 3 * DC

    def layer_norm(tag):
        st = ExitStack()
        xn = sbuf(st, f"xnorm_{tag}", [P, NT, D])
        stats = sbuf(st, f"stats_{tag}", [P, NT, 6])
        mv = sbuf(st, f"mean_var_{tag}", [P, NT, 2])
        std = sbuf(st, f"std_{tag}", [P, NT, 2])
        stats_done = sem(f"stats_done_{tag}")
        var_done = sem(f"var_done_{tag}")
        std_done = sem(f"std_done_{tag}")
        rstd_done = sem(f"rstd_done_{tag}")
        rows_done = sem(f"rows_done_{tag}")
        turned = sem(f"turned_{tag}")
        hi_done = sem(f"xt_hi_done_{tag}")
        lo_done = sem(f"xt_lo_done_{tag}")

        def dve_part(dve, x_ready):
            for t in range(NT):
                x_ready(dve, t)
                dve.bn_stats(stats[:, t, :], xs[:, t, :]).then_inc(stats_done, 1)
            for t in range(NT):
                dve.wait_ge(stats_done, t + 1)
                dve.bn_aggr(mv[:, t, :], stats[:, t, :]).then_inc(var_done, 1)
            dve.wait_ge(var_done, NT)
            dve.tensor_scalar(std[:, :, 0], mv[:, :, 1], EPS, None, ALU.add).then_inc(var_done, 1)
            dve.wait_ge(std_done, 1)
            dve.reciprocal(std[:, :, 1], std[:, :, 0]).then_inc(rstd_done, 1)
            dve.wait_ge(rstd_done, 1)
            for t in range(NT):
                dve.tensor_scalar(xn[:, t, :], xs[:, t, :], mv[:, t, 0:1], std[:, t, 1:2],
                                  ALU.subtract, ALU.mult).then_inc(rows_done, 1)
            for n in range(2 * DC):
                dve.wait_ge(hi_done, n + 1)
                c, b = n // 2, n % 2
                at = slice(b * S, (b + 1) * S)
                dve.tensor_tensor(xt_lo[:, c, at], banks[n][:, :], xt_hi[:, c, at].bitcast(F32),
                                  ALU.subtract).then_inc(lo_done, 1)

        def act_part(act):
            act.wait_ge(var_done, NT + 1)
            act.activation(std[:, :, 0], std[:, :, 0], ACT.Sqrt).then_inc(std_done, 1)
            for n in range(2 * DC):
                act.wait_ge(turned, n + 1)
                c, b = n // 2, n % 2
                act.activation(xt_hi[:, c, b * S:(b + 1) * S], banks[n][:, :], ACT.Copy).then_inc(hi_done, 1)

        def pe_part(pe):
            for n in range(2 * DC):
                c, b = n // 2, n % 2
                for j in range(TS):
                    t = b * TS + j
                    pe.wait_ge(rows_done, t + 1)
                    mm = pe.transpose(banks[n][:, j * P:(j + 1) * P], xn[:, t, c * P:(c + 1) * P], ident[:, :])
                mm.then_inc(turned, 1)

        return st, xn, rows_done, hi_done, lo_done, dve_part, act_part, pe_part

    loaded_x = [sem(f"loaded_x{t}") for t in range(2)]
    loaded_const = sem("loaded_const")
    loaded_sim = sem("loaded_sim")
    loaded_ident = sem("loaded_ident")
    loaded_sel = sem("loaded_sel")
    loaded_ev = [sem(f"loaded_ev{t}") for t in range(2)]
    loaded_eo = [sem(f"loaded_eo{t}") for t in range(2)]
    ln0 = layer_norm("0")
    st1, xn, rows_done, hi_done, lo_done, ln_dve, ln_act, ln_pe = ln0
    with st1:
        sm = sbuf(st1, "sim", [P, DC, E0])
        gates = sbuf(st1, "gates", [B, E0])
        sr = sbuf(st1, "seq_rep", [P, DC, B])
        sq = sbuf(st1, "squares", [P, DC, B + E0])
        below = sbuf(st1, "below", [B, E0, E0])
        sel_half = sbuf(st1, "sel_half", [E0, P])
        sel_tile = sbuf(st1, "sel_tile", [E0, EH])
        same_h = sbuf(st1, "same_h", [P, H0])
        mask = sbuf(st1, "after", [P, P])
        g = sbuf(st1, "gating", [B, 16, E0])
        gs = sbuf(st1, "gating_scalars", [B, 8])
        cmp1 = sbuf(st1, "rank_gt", [B, E0, E0])
        cmp2 = sbuf(st1, "rank_eq", [B, E0, E0])
        r_T = sbuf(st1, "routing_T", [E0, B])
        r_spread = sbuf(st1, "routing_spread", [E0, EH, B])
        r_col = sbuf(st1, "routing_col", [P, EH, B])
        spread = sbuf(st1, "spread", [P, EH, B * H0])
        ev = sbuf(st1, "expert_v", [P, EH, D])
        eo = sbuf(st1, "expert_o", [P, EH, D])
        wv_hi = sbuf(st1, "mixed_v_hi", [P, DC, P], F32R)
        wv_lo = sbuf(st1, "mixed_v_lo", [P, DC, P], F32R)
        wo_hi = sbuf(st1, "mixed_o_hi", [P, D], F32R)
        wo_lo = sbuf(st1, "mixed_o_lo", [P, D], F32R)
        c_hi = sbuf(st1, "combined_hi", [P, T], F32R)
        c_lo = sbuf(st1, "combined_lo", [P, T], F32R)

        consts_done = sem("consts_done")
        rep_done = sem("rep_done")
        gate_step = sem("gate_step")
        sr_done = sem("sr_done")
        norms_done = sem("norms_done")
        gate_act = sem("gate_act")
        r_turned = sem("r_turned")
        r_sp_done = sem("r_sp_done")
        r_col_done = sem("r_col_done")
        spread_done = sem("spread_done")
        mixed = sem("mixed")
        mixed_hi = sem("mixed_hi")
        mixed_lo = sem("mixed_lo")
        comb = sem("comb")
        comb_hi = sem("comb_hi")
        comb_lo = sem("comb_lo")
        ffn_ready = sem("ffn_ready")
        ffn_acc = sem("ffn_acc")

        with nc.Block() as block:
            @block.sync
            def _(sp):
                for n in range(2):
                    half = slice(n * TS, (n + 1) * TS)
                    sp.dma_start(xs[:, half, :], x_in[n * S:(n + 1) * S, :].rearrange("(t p) d -> p t d", p=P))\
                      .then_inc(loaded_x[n], 16)
                sp.dma_start(ident[:, :], ins["ident"]).then_inc(loaded_ident, 16)
                sp.dma_start(small[:, :], ins["biases"]).then_inc(loaded_const, 16)
                sp.dma_start(sm[:, :, :], ins["sim"].rearrange("(c p) e -> p c e", p=P)).then_inc(loaded_sim, 16)
                sp.dma_start(gates[:, :], ins["gates"]).then_inc(loaded_sim, 16)
                for tile, name in ((below, "below"), (sel_half, "sel_half"), (sel_tile, "sel_tile"),
                                   (same_h, "same_h"), (mask, "after")):
                    sp.dma_start(tile[:], ins[name]).then_inc(loaded_sel, 16)
                for n in range(2):
                    h = slice(n * EH // 2, (n + 1) * EH // 2)
                    sp.dma_start(ev[:, h, :], ins["expert_v"].rearrange("(t p) d -> p t d", p=P)[:, h, :])\
                      .then_inc(loaded_ev[n], 16)
                for n in range(2):
                    h = slice(n * EH // 2, (n + 1) * EH // 2)
                    sp.dma_start(eo[:, h, :], ins["expert_o"].rearrange("(t p) d -> p t d", p=P)[:, h, :])\
                      .then_inc(loaded_eo[n], 16)

            @block.gpsimd
            def _(pool):
                pool.memset(ones[:, :], 1.0).then_inc(consts_done, 1)
                pool.memset(zeros_bf[:, :], 0.0).then_inc(consts_done, 1)
                pool.memset(c_hi[:, :].bitcast(F32), 0.0).then_inc(consts_done, 1)
                pool.memset(c_lo[:, :].bitcast(F32), 0.0).then_inc(consts_done, 1)
                pool.wait_ge(loaded_ident, 16)
                pool.tensor_scalar(ident_bf[:, :], ident[:, :], 1.0, 1.0, ALU.mult, ALU.mult)\
                    .then_inc(consts_done, 1)
                pool.wait_ge(loaded_sel, 80)
                pool.tensor_scalar(mask_bf[:, :], mask[:, :], MASKED, 1.0, ALU.mult, ALU.mult)\
                    .then_inc(consts_done, 1)

            @block.scalar
            def _(act):
                ln_act(act)
                act.wait_ge(gate_step, 2)
                act.activation(g[:, 2, :], g[:, 1, :], ACT.Sqrt).then_inc(gate_act, 1)
                act.activation(gs[:, 1:2], gs[:, 0:1], ACT.Sqrt).then_inc(gate_act, 1)
                act.wait_ge(loaded_sim, 32)
                act.activation(g[:, 3, :], gates[:, :], ACT.Exp, scale=-1.0).then_inc(gate_act, 1)
                act.wait_ge(gate_step, 20)
                act.activation(g[:, 14, :], g[:, 13, :], ACT.Exp, bias=gs[:, 4:5], scale=1.0,
                               accum_out=gs[:, 5:6]).then_inc(gate_act, 1)
                act.wait_ge(mixed, 1)
                act.activation(wv_hi[:, :, :], banks[2][:, 0:D].rearrange("p (c m) -> p c m", c=DC), ACT.Copy)\
                    .then_inc(mixed_hi, 1)
                act.wait_ge(mixed, 2)
                act.activation(wo_hi[:, :], banks[3][:, 0:D], ACT.Copy).then_inc(mixed_hi, 1)
                for b in range(B):
                    act.wait_ge(comb, b + 1)
                    act.wait_ge(consts_done, 4)
                    act.activation(c_hi[b * H0:(b + 1) * H0, b * S:(b + 1) * S], banks[b][b * H0:(b + 1) * H0, :],
                                   ACT.Copy).then_inc(comb_hi, 1)

            @block.vector
            def _(dve):
                ln_dve(dve, lambda e, t: e.wait_ge(loaded_x[t // TS], 16))
                dve.wait_ge(loaded_const, 16)
                for at, n, by in ((BQ0, NH0, SCALE0), (BQ1, DC, SCALE1)):
                    dve.tensor_scalar(small[:, at:at + n], small[:, at:at + n], by, None, ALU.mult)
                dve.wait_ge(rep_done, 1)
                dve.tensor_scalar(sr[:, :, :], banks[4][:, 0:DC * B].rearrange("p (c b) -> p c b", c=DC),
                                  1.0 / S, None, ALU.mult).then_inc(sr_done, 1)
                dve.wait_ge(sr_done, 1)
                dve.tensor_tensor(sq[:, :, 0:B], sr[:, :, :], sr[:, :, :], ALU.mult).then_inc(sr_done, 1)
                dve.wait_ge(loaded_sim, 32)
                dve.tensor_tensor(sq[:, :, B:], sm[:, :, :], sm[:, :, :], ALU.mult).then_inc(sr_done, 1)
                steps = [0]

                def link(ins_):
                    steps[0] += 1
                    ins_.then_inc(gate_step, 1)
                    dve.wait_ge(gate_step, steps[0])

                dve.wait_ge(norms_done, 1)
                nrm = banks[5]
                link(dve.tensor_copy(g[:, 1, :], nrm[0:B, E0:2 * E0]))
                link(dve.tensor_copy(gs[:, 0:1], nrm[0:B, 2 * E0:2 * E0 + 1]))
                dve.wait_ge(gate_act, 3)
                link(dve.reciprocal(g[:, 4, :], g[:, 2, :]))
                link(dve.reciprocal(gs[:, 2:3], gs[:, 1:2]))
                link(dve.tensor_scalar(g[:, 5, :], g[:, 3, :], 1.0, None, ALU.add))
                link(dve.reciprocal(g[:, 6, :], g[:, 5, :]))
                link(dve.scalar_tensor_tensor(g[:, 7, :], nrm[0:B, 0:E0], gs[:, 2:3], g[:, 4, :],
                                              ALU.mult, ALU.mult))
                link(dve.tensor_tensor(g[:, 8, :], g[:, 7, :], g[:, 6, :], ALU.subtract))
                link(dve.tensor_scalar(g[:, 9, :], g[:, 8, :], 0.0, None, ALU.max))
                link(dve.tensor_scalar(g[:, 10, :], g[:, 9, :], 0.0, None, ALU.is_gt))
                link(dve.tensor_reduce(gs[:, 3:4], g[:, 10, :], AX, ALU.max))
                row = g[:, 8:9, :].to_broadcast([B, E0, E0])
                col = g[:, 8, :].rearrange("b (e o) -> b e o", o=1).to_broadcast([B, E0, E0])
                link(dve.tensor_tensor(cmp1[:, :, :], row, col, ALU.is_gt))
                link(dve.tensor_tensor(cmp2[:, :, :], row, col, ALU.is_equal))
                dve.wait_ge(loaded_sel, 80)
                link(dve.tensor_tensor(cmp2[:, :, :], cmp2[:, :, :], below[:, :, :], ALU.mult))
                link(dve.tensor_tensor(cmp1[:, :, :], cmp1[:, :, :], cmp2[:, :, :], ALU.add))
                link(dve.tensor_reduce(g[:, 11, :], cmp1[:, :, :], AX, ALU.add))
                link(dve.tensor_scalar(g[:, 12, :], g[:, 11, :], E0 / 2, gs[:, 3:4], ALU.is_lt, ALU.is_gt))
                link(dve.tensor_tensor(g[:, 12, :], g[:, 10, :], g[:, 12, :], ALU.max))
                link(dve.tensor_scalar(g[:, 0, :], g[:, 12, :], FLT_MAX, FLT_MAX, ALU.mult, ALU.subtract))
                dve.tensor_tensor(g[:, 13, :], g[:, 9, :], g[:, 0, :], ALU.add).then_inc(r_sp_done, 1)
                dve.wait_ge(r_sp_done, 1)
                link(dve.tensor_reduce(gs[:, 4:5], g[:, 13, :], AX, ALU.max, negate=True))
                dve.wait_ge(gate_act, 4)
                link(dve.reciprocal(gs[:, 6:7], gs[:, 5:6]))
                link(dve.scalar_tensor_tensor(g[:, 15, :], g[:, 14, :], gs[:, 6:7], g[:, 12, :],
                                              ALU.mult, ALU.mult))
                dve.wait_ge(r_turned, 1)
                dve.tensor_copy(r_T[:, :], banks[4][0:E0, 0:B]).then_inc(r_sp_done, 1)
                dve.wait_ge(r_sp_done, 2)
                dve.wait_ge(loaded_sel, 80)
                dve.tensor_tensor(r_spread[:, :, :],
                                  r_T[:, :].rearrange("e (o b) -> e o b", o=1).to_broadcast([E0, EH, B]),
                                  sel_tile[:, :].rearrange("e (t o) -> e t o", o=1).to_broadcast([E0, EH, B]),
                                  ALU.mult).then_inc(r_sp_done, 1)
                dve.wait_ge(r_col_done, 1)
                dve.tensor_copy(r_col[:, :, :], banks[5][:, 0:EH * B].rearrange("p (t b) -> p t b", b=B))\
                   .then_inc(r_sp_done, 1)
                dve.wait_ge(r_sp_done, 4)
                tb = EH * B
                dve.tensor_tensor(spread[:, :, :].rearrange("p t (b h) -> p (t b) h", b=B),
                                  same_h[:, :].rearrange("p (o h) -> p o h", o=1).to_broadcast([P, tb, H0]),
                                  r_col[:, :, :].rearrange("p t (b o) -> p (t b) o", o=1)
                                  .to_broadcast([P, tb, H0]), ALU.mult).then_inc(spread_done, 1)
                dve.wait_ge(mixed_hi, 1)
                dve.tensor_tensor(wv_lo[:, :, :], banks[2][:, 0:D].rearrange("p (c m) -> p c m", c=DC),
                                  wv_hi[:, :, :].bitcast(F32), ALU.subtract).then_inc(mixed_lo, 1)
                dve.wait_ge(mixed_hi, 2)
                dve.tensor_tensor(wo_lo[:, :], banks[3][:, 0:D], wo_hi[:, :].bitcast(F32), ALU.subtract)\
                   .then_inc(mixed_lo, 1)
                for b in range(B):
                    dve.wait_ge(comb_hi, b + 1)
                    rows, cols = slice(b * H0, (b + 1) * H0), slice(b * S, (b + 1) * S)
                    dve.tensor_tensor(c_lo[rows, cols], banks[b][rows, :], c_hi[rows, cols].bitcast(F32),
                                      ALU.subtract).then_inc(comb_lo, 1)
                for n in range(2 * DC):
                    c, b = n // 2, n % 2
                    dve.wait_ge(ffn_ready, n + 1)
                    dve.tensor_scalar(acc[:, c, b * S:(b + 1) * S], banks[4 + n][:, :],
                                      small[:, BO0 + c:BO0 + c + 1], None, ALU.add).then_inc(ffn_acc, 1)

            @block.tensor
            def _(pe):
                pe.wait_ge(loaded_ident, 16)
                pe.wait_ge(consts_done, 2)
                ln_pe(pe)
                for c in range(DC):
                    for b in range(B):
                        for j in range(TS):
                            mm = pe.matmul(banks[4][:, c * B + b:c * B + b + 1],
                                           xn[:, b * TS + j, c * P:(c + 1) * P], ones[:, 0:1],
                                           start=(j == 0), stop=(j == TS - 1))
                mm.then_inc(rep_done, 1)
                pe.wait_ge(sr_done, 3)
                pe.wait_ge(loaded_sim, 32)
                for c in range(DC):
                    pe.matmul(banks[5][0:B, 0:E0], sr[:, c, :], sm[:, c, :], start=(c == 0), stop=(c == DC - 1))
                for c in range(DC):
                    pe.matmul(banks[5][0:B, E0:2 * E0], ones[:, 0:B], sq[:, c, B:], start=(c == 0),
                              stop=(c == DC - 1))
                for c in range(DC):
                    mm = pe.matmul(banks[5][0:B, 2 * E0:2 * E0 + 1], sq[:, c, 0:B], ones[:, 0:1],
                                   start=(c == 0), stop=(c == DC - 1))
                mm.then_inc(norms_done, 1)
                pe.wait_ge(gate_step, 22)
                pe.transpose(banks[4][0:E0, 0:B], g[:, 15, :], ident[0:B, 0:B]).then_inc(r_turned, 1)
                pe.wait_ge(r_sp_done, 3)
                pe.wait_ge(loaded_sel, 80)
                pe.matmul(banks[5][:, 0:EH * B], sel_half[:, :], r_spread[:, :, :].rearrange("e t b -> e (t b)"),
                          start=True, stop=True).then_inc(r_col_done, 1)
                pe.wait_ge(spread_done, 1)
                pe.wait_ge(lo_done, 2 * DC)
                for c in range(DC):
                    for t in range(EH):
                        if c == 0 and t % (EH // 2) == 0:
                            pe.wait_ge(loaded_ev[t // (EH // 2)], 16)
                        mm = pe.matmul(banks[2][:, c * P:(c + 1) * P], ev[:, t, c * P:(c + 1) * P],
                                       spread[:, t, :], start=(t == 0), stop=(t == EH - 1))
                mm.then_inc(mixed, 1)
                for t in range(EH):
                    if t % (EH // 2) == 0:
                        pe.wait_ge(loaded_eo[t // (EH // 2)], 16)
                    mm = pe.matmul(banks[3][:, 0:D], spread[:, t, :], eo[:, t, :], start=(t == 0),
                                   stop=(t == EH - 1))
                mm.then_inc(mixed, 1)
                pe.wait_ge(mixed_lo, 1)
                for b in range(B):
                    for c in range(DC):
                        cols = slice(b * S, (b + 1) * S)
                        mm = mm3(pe, banks[b][:, :], (wv_hi[:, c, :], wv_lo[:, c, :]),
                                 (xt_hi[:, c, cols], xt_lo[:, c, cols]), c == 0, c == DC - 1)
                    mm.then_inc(comb, 1)
                pe.wait_ge(mixed_lo, 2)
                pe.wait_ge(comb_lo, 2)
                for n in range(2 * DC):
                    c, b = n // 2, n % 2
                    cols, rows = slice(b * S, (b + 1) * S), slice(c * P, (c + 1) * P)
                    mm3(pe, banks[4 + n][:, :], (wo_hi[:, rows], wo_lo[:, rows]),
                        (c_hi[:, cols], c_lo[:, cols]), True, True).then_inc(ffn_ready, 1)


    SCORE_BANK = {3: banks[0][:, 0:S], 2: banks[1][:, P:P + 3 * P], 0: banks[1][:, 0:P], 1: banks[2][:, 0:2 * P]}

    class Attention:

        def __init__(self, tag, stack, t_bank, slots):
            self.t_bank, self.slots = t_bank, slots
            self.probs = sbuf(stack, f"probs_{tag}", [P, 2, SCORES])
            self.pt_hi = sbuf(stack, f"probs_T_hi_{tag}", [P, slots, SCORES], F32R)
            self.pt_lo = sbuf(stack, f"probs_T_lo_{tag}", [P, slots, SCORES], F32R)
            self.neg_max = sbuf(stack, f"neg_max_{tag}", [P, 2, TS])
            self.row_sum = sbuf(stack, f"row_sum_{tag}", [P, 2, TS])
            self.recip = sbuf(stack, f"recip_{tag}", [P, 2, TS])
            self.scores_ready = sem(f"scores_ready_{tag}")
            self.max_ready = sem(f"max_ready_{tag}")
            self.probs_ready = sem(f"probs_ready_{tag}")
            self.recip_ready = sem(f"recip_ready_{tag}")
            self.norm_done = sem(f"norm_done_{tag}")
            self.t_ready = sem(f"t_ready_{tag}")
            self.t_high = sem(f"t_high_{tag}")
            self.t_low = sem(f"t_low_{tag}")

        def scores(self, pe, U, product):
            for n, group in enumerate(([3], [2, 0], [1])):
                if not (isinstance(U, int) and U == 0):
                    pe.wait_ge(self.probs_ready, 4 * U + (1, 3, 4)[n] - 4)
                for q in group:
                    region = SCORE_BANK[q]
                    product(pe, region, q)
                    mm = pe.matmul(region[:, q * P:(q + 1) * P], ident_bf[:, :], mask_bf[:, :],
                                   start=False, stop=True)
                mm.then_inc(self.scores_ready, 1)

        def turn(self, pe, U, u, n):
            if n == 0:
                pe.wait_ge(self.norm_done, 4 * U + 4)
            if n == 2 and self.t_bank[2] is self.t_bank[0]:
                pe.wait_ge(self.t_low, 3 * U + 1)
            at = 0
            for kt in T_GROUPS[n]:
                for q in range(kt, TS):
                    mm = pe.transpose(self.t_bank[n][:, at:at + P],
                                      self.probs[:, u % 2, P_AT[q] + kt * P:P_AT[q] + (kt + 1) * P], ident[:, :])
                    at += P
            mm.then_inc(self.t_ready, 1)

        def wait_pt(self, pe, U, kt):
            pe.wait_ge(self.t_low, 3 * U + {0: 1, 1: 2, 3: 2, 2: 3}[kt])

        def pt(self, u, kt):
            at = slice(T_AT[kt], T_AT[kt] + S - kt * P)
            return self.pt_hi[:, u % self.slots, at], self.pt_lo[:, u % self.slots, at]

        def exps(self, act, U, u):
            for n, q in enumerate(Q_ORDER):
                act.wait_ge(self.max_ready, 4 * U + (1, 3, 3, 4)[n])
                act.activation(self.probs[:, u % 2, P_AT[q]:P_AT[q] + (q + 1) * P], SCORE_BANK[q], ACT.Exp,
                               bias=self.neg_max[:, u % 2, q:q + 1], scale=1.0,
                               accum_out=self.row_sum[:, u % 2, q:q + 1]).then_inc(self.probs_ready, 1)

        def turned_high(self, act, U, u, n):
            at, w = T_SPAN[n]
            act.wait_ge(self.t_ready, 3 * U + n + 1)
            act.activation(self.pt_hi[:, u % self.slots, at:at + w], self.t_bank[n][:, 0:w], ACT.Copy)\
               .then_inc(self.t_high, 1)

        def maxima(self, dve, U, u):
            for n, q in enumerate(Q_ORDER):
                dve.wait_ge(self.scores_ready, 3 * U + (1, 2, 2, 3)[n])
                dve.tensor_reduce(self.neg_max[:, u % 2, q:q + 1], SCORE_BANK[q], AX, ALU.max, negate=True)\
                   .then_inc(self.max_ready, 1)

        def reciprocals(self, dve, U, u):
            for n in (1, 0):
                dve.wait_ge(self.probs_ready, 4 * U + (4 - 2 * n))
                dve.reciprocal(self.recip[:, u % 2, 2 * n:2 * n + 2], self.row_sum[:, u % 2, 2 * n:2 * n + 2])\
                   .then_inc(self.recip_ready, 1)

        def turned_low(self, dve, U, u, n):
            at, w = T_SPAN[n]
            dve.wait_ge(self.t_high, 3 * U + n + 1)
            dve.tensor_tensor(self.pt_lo[:, u % self.slots, at:at + w], self.t_bank[n][:, 0:w],
                              self.pt_hi[:, u % self.slots, at:at + w].bitcast(F32), ALU.subtract)\
               .then_inc(self.t_low, 1)

        def normalise(self, pool, U, u):
            for n, q in enumerate(Q_ORDER):
                if n % 2 == 0:
                    wait_apart(pool, (self.recip_ready, 2 * U + n // 2 + 1))
                row = self.probs[:, u % 2, P_AT[q]:P_AT[q] + (q + 1) * P]
                pool.tensor_scalar(row, row, self.recip[:, u % 2, q:q + 1], 1.0, ALU.mult, ALU.mult)\
                    .then_inc(self.norm_done, 1)

    UNITS = 4
    RING = 16
    RING0 = 10
    with ExitStack() as st2:
        att = Attention("0", st2, [banks[3], banks[4], banks[3]], 1)
        qk_raw = sbuf(st2, "qk_raw", [P, 2, DC, 2, P])
        v_raw = sbuf(st2, "v_raw", [P, DC, 2 * P])
        o_raw = sbuf(st2, "o_raw", [P, 2, D])
        qk_w = [sbuf(st2, f"qk_w_{x}", [P, 2, DC, 2, P], F32R) for x in ("hi", "lo")]
        v_w = [sbuf(st2, f"v_w_{x}", [P, DC, 2 * P], F32R) for x in ("hi", "lo")]
        o_w = [sbuf(st2, f"o_w_{x}", [P, 2, D], F32R) for x in ("hi", "lo")]
        qk_T = [sbuf(st2, f"qk_T_{x}", [P, 2, UNITS, S], F32R) for x in ("hi", "lo")]
        v_rows = [sbuf(st2, f"v_rows_{x}", [P, B, TS, 2 * P], F32R) for x in ("hi", "lo")]
        attn_T = [sbuf(st2, f"attn_T_{x}", [P, 2, S], F32R) for x in ("hi", "lo")]
        O_BANK, R_BANK = banks[5], banks[6:8]

        qk_loaded = [sem(f"qk_loaded{h}") for h in range(2)]
        v_loaded = sem("v_loaded")
        o_loaded = sem("o_loaded")
        qk_split = [sem(f"qk_split{h}") for h in range(2)]
        v_split = sem("v_split")
        o_split = sem("o_split")
        ring_full = sem("ring_full")
        ring_high = sem("ring_high")
        ring_free = sem("ring_free")
        o_ready = sem("o_ready")
        o_high = sem("o_high")
        o_low = sem("o_low")
        QK_USE = [2, 4, 10, 12]
        V_USE = [6, 14]
        OUT_USE = [8, 0]
        OUT_USE_LAST = [2, 0]
        HIGHS = 12
        QK_HIGH = [0, 2, 6, 8]
        V_HIGH = [4, 10]

        def pair_of(ap, j):
            return ap[j] if isinstance(j, int) else ap[bass.ds(j, 1)].rearrange("o p n -> (o p) n")

        with nc.Block() as block:
            @block.sync
            def _(sp):
                def load_qk(h, j):
                    if not isinstance(j, int) or j:
                        wait_apart(sp, (qk_split[h], 3 * j))
                    sp.dma_start(qk_raw[:, h].rearrange("p c k n -> p (c k n)"), pair_of(ins["w_qk0"][h], j))\
                      .then_inc(qk_loaded[h], 16)

                def load_v(j):
                    if not isinstance(j, int) or j:
                        wait_apart(sp, (v_split, 2 * j))
                    sp.dma_start(v_raw[:, :, :].rearrange("p c n -> p (c n)"), pair_of(ins["w_v0"], j))\
                      .then_inc(v_loaded, 16)

                def load_o(j):
                    if not isinstance(j, int) or j:
                        wait_apart(sp, (o_split, 2 * j))
                    sp.dma_start(o_raw[:, :, :].rearrange("p h n -> p (h n)"), pair_of(ins["w_o0"], j))\
                      .then_inc(o_loaded, 16)

                load_qk(0, 0)
                load_qk(1, 0)
                load_v(0)
                load_o(0)
                load_qk(0, 1)
                load_qk(1, 1)
                load_v(1)
                load_qk(0, 2)
                with sp.Fori(0, PAIRS - 3) as i:
                    load_qk(1, i + 2)
                    load_v(i + 2)
                    load_o(i + 1)
                    load_qk(0, i + 3)
                load_qk(1, PAIRS - 1)
                load_v(PAIRS - 1)
                load_o(PAIRS - 2)
                load_o(PAIRS - 1)

            @block.gpsimd
            def _(pool):
                def split(raw, parts, done, n):
                    pool.tensor_scalar(parts[0], raw, 1.0, 1.0, ALU.mult, ALU.mult).then_inc(done, 1)
                    pool.wait_ge(done, n + 1)
                    pool.tensor_tensor(parts[1], raw, parts[0].bitcast(F32), ALU.subtract).then_inc(done, 1)

                def split_qk(h, j, used):
                    wait_apart(pool, (qk_loaded[h], 16 * (j + 1)), *([] if used is None else [(ring_full, used)]))
                    for c in range(DC):
                        mul = pool.tensor_scalar(qk_raw[:, h, c, 0, :], qk_raw[:, h, c, 0, :], SCALE0, 1.0,
                                                 ALU.mult, ALU.mult)
                    mul.then_inc(qk_split[h], 1)
                    wait_apart(pool, (qk_split[h], 3 * j + 1))
                    split(qk_raw[:, h].rearrange("p c k n -> p (c k n)"),
                          [w[:, h].rearrange("p c k n -> p (c k n)") for w in qk_w], qk_split[h], 3 * j + 1)

                def split_v(j, used):
                    wait_apart(pool, (v_loaded, 16 * (j + 1)), *([] if used is None else [(ring_full, used)]))
                    split(v_raw[:, :, :], [w[:, :, :] for w in v_w], v_split, 2 * j)

                def split_o(j, used):
                    wait_apart(pool, (o_loaded, 16 * (j + 1)), (ring_full, used))
                    split(o_raw[:, :, :], [w[:, :, :] for w in o_w], o_split, 2 * j)

                def iteration(i, first=False, project=True, more=True):
                    r = RING0 + RING * i
                    for u in range(UNITS):
                        if u == 0 and project:
                            split_qk(1, i + 1, r - 2)
                            split_v(i + 1, r + 2 if first else r)
                        if project or u < UNITS - 1:
                            att.normalise(pool, UNITS * i + u + 1, u + 1)
                        if u == 0:
                            split_o(i, r + 2)
                        if u == 3 and more:
                            split_qk(0, i + 2, r + QK_USE[2] + 2)

                split_qk(0, 0, None)
                split_qk(1, 0, None)
                split_v(0, None)
                att.normalise(pool, 0, 0)
                split_qk(0, 1, 6)
                iteration(0, first=True)
                with pool.Fori(1, PAIRS - 2) as i:
                    iteration(i)
                iteration(PAIRS - 2, more=False)
                iteration(PAIRS - 1, project=False, more=False)

            @block.tensor
            def _(pe):
                def take(r):
                    if not isinstance(r, int) or r >= 2:
                        pe.wait_ge(ring_free, r - 1)

                def project_qk(u, j, r, k):
                    h, b = u % 2, u // 2
                    if k == 0:
                        pe.wait_ge(qk_split[h], 3 * j + 3)
                    take(r + k)
                    for c in range(DC):
                        cols = slice(b * S, (b + 1) * S)
                        mm = mm3(pe, R_BANK[k][:, :], [w[:, h, c, k, :] for w in qk_w],
                                 (xt_hi[:, c, cols], xt_lo[:, c, cols]), c == 0, c == DC - 1)
                    mm.then_inc(ring_full, 1)

                def project_v(b, j, r):
                    pe.wait_ge(v_split, 2 * j + 2)
                    for k in range(2):
                        take(r + k)
                        for n in range(2):
                            t = b * TS + 2 * k + n
                            rows = slice(t * P, (t + 1) * P)
                            for c in range(DC):
                                mm = mm3(pe, R_BANK[k][:, n * 2 * P:(n + 1) * 2 * P],
                                         (xt_hi[:, c, rows], xt_lo[:, c, rows]), [w[:, c, :] for w in v_w],
                                         c == 0, c == DC - 1)
                        mm.then_inc(ring_full, 1)

                def project_out(b, i, r):
                    pe.wait_ge(o_split, 2 * i + 2)
                    pe.wait_ge(o_low, UNITS * i + 2 * b + 2)
                    for c in range(DC):
                        take(r + c)
                        for h in range(2):
                            mm = mm3(pe, R_BANK[c][:, :], [w[:, h, c * P:(c + 1) * P] for w in o_w],
                                     [a[:, h, :] for a in attn_T], h == 0, h == 1)
                        mm.then_inc(ring_full, 1)

                def score(U, u):
                    def product(pe_, region, q):
                        q_T = [x[:, 0, u, q * P:(q + 1) * P] for x in qk_T]
                        k_T = [x[:, 1, u, 0:(q + 1) * P] for x in qk_T]
                        mm3(pe_, region, q_T, k_T, True, False)

                    att.scores(pe, U, product)

                def weigh_v(U, u):
                    h, b = u % 2, u // 2
                    if not isinstance(U, int) or U:
                        pe.wait_ge(o_low, U)
                    for kt in range(TS):
                        att.wait_pt(pe, U, kt)
                        mm = mm3(pe, O_BANK[:, kt * P:S], [v[:, b, kt, h * P:(h + 1) * P] for v in v_rows],
                                 att.pt(u, kt), kt == 0, kt == TS - 1)
                    mm.then_inc(o_ready, 1)

                def iteration(i, first=False, project=True):
                    r = RING0 + RING * i
                    outs = OUT_USE if project else OUT_USE_LAST
                    for u in range(UNITS):
                        U = UNITS * i + u
                        if project or u < UNITS - 1:
                            score(U + 1, (u + 1) % UNITS)
                        if u == 0 and not first:
                            project_out(1, i - 1, r + outs[1])
                        if u == 2:
                            project_out(0, i, r + outs[0])
                        if u % 2 and project:
                            project_qk(u, i + 1, r + QK_USE[u], 0)
                        att.turn(pe, U, u, 0)
                        att.turn(pe, U, u, 1)
                        if project:
                            project_qk(u, i + 1, r + QK_USE[u], u % 2)
                        att.turn(pe, U, u, 2)
                        if u % 2 == 0 and project:
                            project_qk(u, i + 1, r + QK_USE[u], 1)
                        weigh_v(U, u)
                        if u % 2 and project:
                            project_v(u // 2, i + 1, r + V_USE[u // 2])

                for u in range(UNITS):
                    for k in range(2):
                        project_qk(u, 0, 2 * u, k)
                    if u == 0:
                        pe.wait_ge(ring_free, 2)
                        score(0, 0)
                for b in range(B):
                    project_v(b, 0, 8 + 2 * b)
                iteration(0, first=True)
                with pe.Fori(1, PAIRS - 1) as i:
                    iteration(i)
                iteration(PAIRS - 1, project=False)
                project_out(1, PAIRS - 1, RING0 + RING * (PAIRS - 1) + 4)

            def bias_col(at, i, h):
                return small[:, bass.ds(2 * i + (at + h), 1)] if not isinstance(i, int) \
                    else small[:, at + 2 * i + h:at + 2 * i + h + 1]

            def v_dest(parts, b, k):
                return parts[:, b, 2 * k:2 * k + 2, :].rearrange("p t n -> p (t n)")

            @block.scalar
            def _(act):
                def high_qk(u, j, r, k):
                    wait_apart(act, (ring_full, r + k + 1))
                    act.activation(qk_T[0][:, k, u, :], R_BANK[k][:, :], ACT.Identity,
                                   bias=bias_col((BQ0, BK0)[k], j, u % 2)).then_inc(ring_high, 1)

                def high_v(b, r):
                    for k in range(2):
                        act.wait_ge(ring_full, r + k + 1)
                        act.activation(v_dest(v_rows[0], b, k), R_BANK[k][:, :], ACT.Copy).then_inc(ring_high, 1)

                def high_out(U, u, i):
                    wait_apart(act, (o_ready, U + 1))
                    act.activation(attn_T[0][:, u % 2, :], O_BANK[:, :], ACT.Identity,
                                   bias=bias_col(BV0, i, u % 2)).then_inc(o_high, 1)

                def iteration(i, first=False, project=True):
                    r = RING0 + RING * i
                    for u in range(UNITS):
                        U = UNITS * i + u
                        if project or u < UNITS - 1:
                            att.exps(act, U + 1, u + 1)
                        if u % 2 and project:
                            high_qk(u, i + 1, r + QK_USE[u], 0)
                        att.turned_high(act, U, u, 0)
                        att.turned_high(act, U, u, 1)
                        if project:
                            high_qk(u, i + 1, r + QK_USE[u], u % 2)
                        att.turned_high(act, U, u, 2)
                        if u % 2 == 0 and project:
                            high_qk(u, i + 1, r + QK_USE[u], 1)
                        high_out(U, u, i)
                        if u % 2 and project:
                            high_v(u // 2, r + V_USE[u // 2])

                for u in range(UNITS):
                    for k in range(2):
                        high_qk(u, 0, 2 * u, k)
                    if u == 0:
                        att.exps(act, 0, 0)
                for b in range(B):
                    high_v(b, 8 + 2 * b)
                iteration(0, first=True)
                with act.Fori(1, PAIRS - 1) as i:
                    iteration(i)
                iteration(PAIRS - 1, project=False)

            @block.vector
            def _(dve):
                def low_qk(u, j, n, k):
                    dve.wait_ge(ring_high, n + 1)
                    dve.scalar_tensor_tensor(qk_T[1][:, k, u, :], R_BANK[k][:, :],
                                             bias_col((BQ0, BK0)[k], j, u % 2),
                                             qk_T[0][:, k, u, :].bitcast(F32), ALU.add, ALU.subtract)\
                       .then_inc(ring_free, 1)

                def low_v(b, n):
                    for k in range(2):
                        dve.wait_ge(ring_high, n + k + 1)
                        dve.tensor_tensor(v_dest(v_rows[1], b, k), R_BANK[k][:, :],
                                          v_dest(v_rows[0], b, k).bitcast(F32), ALU.subtract)\
                           .then_inc(ring_free, 1)

                def low_out(U, u, i):
                    dve.wait_ge(o_high, U + 1)
                    dve.scalar_tensor_tensor(attn_T[1][:, u % 2, :], O_BANK[:, :], bias_col(BV0, i, u % 2),
                                             attn_T[0][:, u % 2, :].bitcast(F32), ALU.add, ALU.subtract)\
                       .then_inc(o_low, 1)

                def add_out(b, r):
                    for c in range(DC):
                        dve.wait_ge(ring_full, r + c + 1)
                        at = acc[:, c, b * S:(b + 1) * S]
                        dve.tensor_tensor(at, R_BANK[c][:, :], at, ALU.add).then_inc(ring_free, 1)

                def iteration(i, first=False, project=True):
                    r = RING0 + RING * i
                    n = HIGHS + HIGHS * i
                    outs = OUT_USE if project else OUT_USE_LAST
                    for u in range(UNITS):
                        U = UNITS * i + u
                        if project or u < UNITS - 1:
                            att.maxima(dve, U + 1, u + 1)
                        if u == 0 and not first:
                            add_out(1, r + outs[1])
                        if u == 2:
                            add_out(0, r + outs[0])
                        if u % 2 and project:
                            low_qk(u, i + 1, n + QK_HIGH[u], 0)
                        if project or u < UNITS - 1:
                            att.reciprocals(dve, U + 1, u + 1)
                        att.turned_low(dve, U, u, 0)
                        att.turned_low(dve, U, u, 1)
                        if project:
                            low_qk(u, i + 1, n + QK_HIGH[u] + u % 2, u % 2)
                        att.turned_low(dve, U, u, 2)
                        if u % 2 == 0 and project:
                            low_qk(u, i + 1, n + QK_HIGH[u] + 1, 1)
                        low_out(U, u, i)
                        if u % 2 and project:
                            low_v(u // 2, n + V_HIGH[u // 2])

                for u in range(UNITS):
                    for k in range(2):
                        low_qk(u, 0, 2 * u + k, k)
                    if u == 0:
                        att.maxima(dve, 0, 0)
                for b in range(B):
                    low_v(b, 8 + 2 * b)
                    if b == 0:
                        att.reciprocals(dve, 0, 0)
                iteration(0, first=True)
                with dve.Fori(1, PAIRS - 1) as i:
                    iteration(i)
                iteration(PAIRS - 1, project=False)
                add_out(1, RING0 + RING * (PAIRS - 1) + 4)

    scratch = nc.dram_tensor("head_rows", (5, D, T), F32, kind="Internal").ap()
    alibi_scratch = nc.dram_tensor("alibi_rows", (NH1, 2, T), F32, kind="Internal").ap()
    late = ExitStack()
    v1 = sbuf(late, "v1", [P, 2, NT, D], F32R)
    w_bc = sbuf(late, "expert_weight", [P, E1, T])
    wqkv_hi = sbuf(late, "w_qkvo1_hi", [P, DC, 4 * D], F32R)
    wqkv_lo = sbuf(late, "w_qkvo1_lo", [P, DC, 4 * D], F32R)
    with ExitStack() as st3:
        raw = sbuf(st3, "w_qkvo1", [P, DC, 4 * D])
        qk1 = [sbuf(st3, f"qk1_{x}", [P, 2, DC, T], F32R) for x in ("hi", "lo")]
        al = sbuf(st3, "alibi", [NH1, T])
        al_hi = sbuf(st3, "alibi_hi", [NH1, T], F32R)
        al_lo = sbuf(st3, "alibi_lo", [NH1, T], F32R)
        rw = sbuf(st3, "router", [P, DC, E1])
        before8 = sbuf(st3, "before8", [P, E1, E1])
        sel8 = sbuf(st3, "sel8", [E1, E1, P])
        lg = sbuf(st3, "router_work", [P, 6, NT, E1])
        ls = sbuf(st3, "router_scalars", [P, 4, NT])
        gt8 = sbuf(st3, "rank8_gt", [P, NT, E1, E1])
        eq8 = sbuf(st3, "rank8_eq", [P, NT, E1, E1])
        w_T = sbuf(st3, "expert_weight_T", [E1, T])

        loaded1 = sem("loaded1")
        loaded_raw1 = sem("loaded_raw1")
        acc_turned = sem("acc_turned")
        added = sem("added")
        scaled1 = sem("scaled1")
        split1 = sem("split1")
        al_split = sem("alibi_split")
        routed = sem("routed")
        route_step = sem("route_step")
        route_exp = sem("route_exp")
        w_turned = sem("w_turned")
        w_T_done = sem("w_T_done")
        bc_ready = sem("bc_ready")
        bc_act = sem("bc_act")
        bc_dve = sem("bc_dve")
        ring1_full = sem("ring1_full")
        ring1_high = sem("ring1_high")
        ring1_free = sem("ring1_free")
        stored_rows = sem("stored_rows")

        stn, xn, rows_done, hi_done, lo_done, ln_dve, ln_act, ln_pe = layer_norm("1")
        with stn, nc.Block() as block:
            @block.sync
            def _(sp):
                sp.dma_start(raw[:, :, :], ins["w_qkv1"].rearrange("(c p) n -> p c n", p=P)).then_inc(loaded_raw1, 16)
                sp.dma_start(al[:, :], ins["alibi"]).then_inc(loaded1, 16)
                sp.dma_start(rw[:, :, :], ins["router"].rearrange("(c p) e -> p c e", p=P)).then_inc(loaded1, 16)
                sp.dma_start(before8[:, :, :], ins["before8"]).then_inc(loaded1, 16)
                sp.dma_start(sel8[:, :, :], ins["sel8"]).then_inc(loaded1, 16)
                sp.wait_ge(al_split, 2)
                sp.dma_start(alibi_scratch[:, 0, :], al_hi[:, :].bitcast(F32)).then_inc(stored_rows, 16)
                sp.dma_start(alibi_scratch[:, 1, :], al_lo[:, :].bitcast(F32)).then_inc(stored_rows, 16)
                for k in range(2):
                    for m in range(DC):
                        sp.wait_ge(ring1_free, 4 * k + 2 * m + 2)
                        rows = slice(m * P, (m + 1) * P)
                        for part, which in ((0, 0), (1, 1), (2, 0)) if k == 0 else ((3, 0), (4, 1)):
                            sp.dma_start(scratch[part, rows, :], qk1[which][:, k, m, :].bitcast(F32))\
                              .then_inc(stored_rows, 16)
                sp.wait_ge(stored_rows, 16 * (2 + 5 * DC))

            @block.gpsimd
            def _(pool):
                pool.wait_ge(loaded_raw1, 16)
                for c in range(DC):
                    pool.tensor_scalar(raw[:, c, 0:D], raw[:, c, 0:D], SCALE1, 1.0, ALU.mult, ALU.mult)\
                        .then_inc(scaled1, 1)
                pool.wait_ge(scaled1, DC)
                for c in range(DC):
                    pool.tensor_scalar(wqkv_hi[:, c, :], raw[:, c, :], 1.0, 1.0, ALU.mult, ALU.mult)\
                        .then_inc(split1, 1)
                pool.wait_ge(loaded1, 64)
                pool.tensor_scalar(al_hi[:, :], al[:, :], 1.0, 1.0, ALU.mult, ALU.mult).then_inc(al_split, 1)
                pool.wait_ge(al_split, 1)
                pool.tensor_tensor(al_lo[:, :], al[:, :], al_hi[:, :].bitcast(F32), ALU.subtract)\
                    .then_inc(al_split, 1)
                pool.wait_ge(split1, DC)
                for c in range(DC):
                    pool.tensor_tensor(wqkv_lo[:, c, :], raw[:, c, :], wqkv_hi[:, c, :].bitcast(F32), ALU.subtract)\
                        .then_inc(split1, 1)

            @block.scalar
            def _(act):
                ln_act(act)
                for n in range(8):
                    k, m, b = n // 4, n // 2 % 2, n % 2
                    act.wait_ge(ring1_full, n + 1)
                    act.activation(qk1[0][:, k, m, b * S:(b + 1) * S], banks[6 + n % 2][:, :], ACT.Identity,
                                   bias=small[:, (BQ1, BK1)[k] + m:(BQ1, BK1)[k] + m + 1]).then_inc(ring1_high, 1)
                for n in range(4):
                    act.wait_ge(ring1_full, 9 + n)
                    act.activation(v1[:, 0, 2 * n:2 * n + 2, :], banks[6 + n % 2][:, :].rearrange(
                        "p (t d) -> p t d", d=D), ACT.Copy).then_inc(ring1_high, 1)
                act.wait_ge(route_step, 3)
                act.activation(lg[:, 2, :, :], lg[:, 1, :, :], ACT.Exp).then_inc(route_exp, 1)
                for n in range(0, 2 * E1, 2):
                    act.wait_ge(bc_ready, n + 1)
                    act.activation(w_bc[:, n // 2, 0:S], banks[n % 4][:, :], ACT.Copy).then_inc(bc_act, 1)

            @block.vector
            def _(dve):
                for n in range(4):
                    dve.wait_ge(acc_turned, n + 1)
                    rows = xs[:, 2 * n:2 * n + 2, :]
                    dve.tensor_tensor(rows, banks[4 + n][:, :].rearrange("p (t d) -> p t d", d=D), rows, ALU.add)\
                       .then_inc(added, 1)
                ln_dve(dve, lambda e, t: e.wait_ge(added, t // 2 + 1))
                for n in range(8):
                    k, m, b = n // 4, n // 2 % 2, n % 2
                    dve.wait_ge(ring1_high, n + 1)
                    at = slice(b * S, (b + 1) * S)
                    dve.scalar_tensor_tensor(qk1[1][:, k, m, at], banks[6 + n % 2][:, :],
                                             small[:, (BQ1, BK1)[k] + m:(BQ1, BK1)[k] + m + 1],
                                             qk1[0][:, k, m, at].bitcast(F32), ALU.add, ALU.subtract)\
                       .then_inc(ring1_free, 1)
                for n in range(4):
                    dve.wait_ge(ring1_high, 9 + n)
                    dve.tensor_tensor(v1[:, 1, 2 * n:2 * n + 2, :], banks[6 + n % 2][:, :].rearrange(
                        "p (t d) -> p t d", d=D), v1[:, 0, 2 * n:2 * n + 2, :].bitcast(F32), ALU.subtract)\
                       .then_inc(ring1_free, 1)
                steps = [0]

                def link(ins_):
                    steps[0] += 1
                    ins_.then_inc(route_step, 1)
                    dve.wait_ge(route_step, steps[0])

                def per_expert(col):
                    return ls[:, col, :].rearrange("p (t o) -> p t o", o=1).to_broadcast([P, NT, E1])

                dve.wait_ge(routed, 1)
                link(dve.tensor_copy(lg[:, 0, :, :], banks[4][:, 0:NT * E1].rearrange("p (t e) -> p t e", e=E1)))
                link(dve.tensor_reduce(ls[:, 0, :], lg[:, 0, :, :], AX, ALU.max))
                link(dve.tensor_tensor(lg[:, 1, :, :], lg[:, 0, :, :], per_expert(0), ALU.subtract))
                dve.wait_ge(route_exp, 1)
                link(dve.tensor_reduce(ls[:, 1, :], lg[:, 2, :, :], AX, ALU.add))
                link(dve.reciprocal(ls[:, 2, :], ls[:, 1, :]))
                link(dve.tensor_tensor(lg[:, 3, :, :], lg[:, 2, :, :], per_expert(2), ALU.mult))
                four = [P, NT, E1, E1]
                row = lg[:, 3, :, :].rearrange("p t (o j) -> p t o j", o=1).to_broadcast(four)
                col = lg[:, 3, :, :].rearrange("p t (e o) -> p t e o", o=1).to_broadcast(four)
                link(dve.tensor_tensor(gt8[:, :, :, :], row, col, ALU.is_gt))
                link(dve.tensor_tensor(eq8[:, :, :, :], row, col, ALU.is_equal))
                dve.wait_ge(loaded1, 64)
                eq = eq8[:, :, :, :].rearrange("p t e j -> p t (e j)")
                link(dve.tensor_tensor(eq, eq, before8[:, :, :].rearrange("p (o e) j -> p o (e j)", o=1)
                                       .to_broadcast([P, NT, E1 * E1]), ALU.mult))
                link(dve.tensor_tensor(gt8[:, :, :, :], gt8[:, :, :, :], eq8[:, :, :, :], ALU.add))
                link(dve.tensor_reduce(lg[:, 4, :, :], gt8[:, :, :, :], AX, ALU.add))
                link(dve.scalar_tensor_tensor(lg[:, 5, :, :].rearrange("p t e -> p (t e)"),
                                              lg[:, 4, :, :].rearrange("p t e -> p (t e)"), 2.0,
                                              lg[:, 3, :, :].rearrange("p t e -> p (t e)"), ALU.is_lt, ALU.mult))
                link(dve.tensor_reduce(ls[:, 3, :], lg[:, 5, :, :], AX, ALU.add))
                link(dve.reciprocal(ls[:, 0, :], ls[:, 3, :]))
                link(dve.tensor_tensor(lg[:, 0, :, :], lg[:, 5, :, :], per_expert(0), ALU.mult))
                for n in range(2):
                    dve.wait_ge(w_turned, n + 1)
                    dve.tensor_copy(w_T[:, n * S:(n + 1) * S], banks[4 + n][0:E1, :]).then_inc(w_T_done, 1)
                for n in range(1, 2 * E1, 2):
                    dve.wait_ge(bc_ready, n + 1)
                    dve.tensor_copy(w_bc[:, n // 2, S:T], banks[n % 4][:, :]).then_inc(bc_dve, 1)

            @block.tensor
            def _(pe):
                for t in range(NT):
                    for c in range(DC):
                        at = (t % 2) * D + c * P
                        mm = pe.transpose(banks[4 + t // 2][:, at:at + P], acc[:, c, t * P:(t + 1) * P], ident[:, :])
                    if t % 2:
                        mm.then_inc(acc_turned, 1)
                ln_pe(pe)
                pe.wait_ge(lo_done, 2 * DC)
                pe.wait_ge(loaded1, 64)
                for t in range(NT):
                    n = 0
                    for c in range(DC):
                        for part in (xt_hi, xt_lo):
                            mm = pe.matmul(banks[4][:, t * E1:(t + 1) * E1],
                                           part[:, c, t * P:(t + 1) * P].bitcast(F32), rw[:, c, :],
                                           start=(n == 0), stop=(n == 2 * DC - 1))
                            n += 1
                mm.then_inc(routed, 1)
                pe.wait_ge(split1, 2 * DC)
                for n in range(8):
                    k, m, b = n // 4, n // 2 % 2, n % 2
                    if n >= 2:
                        pe.wait_ge(ring1_free, n - 1)
                    w = slice(k * D + m * P, k * D + (m + 1) * P)
                    cols = slice(b * S, (b + 1) * S)
                    for c in range(DC):
                        mm = mm3(pe, banks[6 + n % 2][:, :], (wqkv_hi[:, c, w], wqkv_lo[:, c, w]),
                                 (xt_hi[:, c, cols], xt_lo[:, c, cols]), c == 0, c == DC - 1)
                    mm.then_inc(ring1_full, 1)
                for n in range(4):
                    pe.wait_ge(ring1_free, 8 + n - 1)
                    for t in (2 * n, 2 * n + 1):
                        rows = slice(t * P, (t + 1) * P)
                        for c in range(DC):
                            mm = mm3(pe, banks[6 + n % 2][:, (t % 2) * D:(t % 2 + 1) * D],
                                     (xt_hi[:, c, rows], xt_lo[:, c, rows]),
                                     (wqkv_hi[:, c, 2 * D:3 * D], wqkv_lo[:, c, 2 * D:3 * D]), c == 0, c == DC - 1)
                    mm.then_inc(ring1_full, 1)
                pe.wait_ge(route_step, 15)
                for t in range(NT):
                    mm = pe.transpose(banks[4 + t // TS][0:E1, (t % TS) * P:(t % TS + 1) * P], lg[:, 0, t, :],
                                      ident[:, :])
                    if t % TS == TS - 1:
                        mm.then_inc(w_turned, 1)
                pe.wait_ge(w_T_done, 2)
                for n in range(2 * E1):
                    if n >= 4:
                        pe.wait_ge((bc_act, bc_dve)[n % 2], (n - 4) // 2 + 1)
                    pe.matmul(banks[n % 4][:, :], sel8[:, n // 2, :], w_T[:, (n % 2) * S:(n % 2 + 1) * S],
                              start=True, stop=True).then_inc(bc_ready, 1)

    GROUPS = D // P
    GROUP_PAIRS = P // HD1 // 2
    PAIR = 2 * HD1
    KR = 4 * HD1 + 2
    a1_hi = sbuf(late, "attn1_T_hi", [P, GROUPS, T], F32R)
    a1_lo = sbuf(late, "attn1_T_lo", [P, GROUPS, T], F32R)
    with ExitStack() as st4:
        att = Attention("1", st4, [banks[3], banks[4], banks[7]], 2)
        q4 = sbuf(st4, "q_rows", [KR, 2, T], F32R)
        k4 = sbuf(st4, "k_rows", [KR, 2, T], F32R)
        vz = sbuf(st4, "v_placed", [P, 2, 2 * NT, P], F32R)
        none = sbuf(st4, "none", [P, 2 * NT, HD1])
        rows_loaded = [sem(f"rows_loaded{h}") for h in range(2)]
        q4_ones = sem("q4_ones")
        cleared = sem("cleared")
        placed = sem("placed")
        pv_done = sem("pv_done")
        o1_ready = sem("o1_ready")
        o1_high = sem("o1_high")
        o1_low = sem("o1_low")
        O_BANKS = banks[5:7]
        LAST = GROUPS * GROUP_PAIRS - 1

        def each_pair(eng, body):
            for grp in range(GROUPS):
                first = GROUP_PAIRS * grp
                body(grp, 0, first)
                with eng.Fori(1, GROUP_PAIRS - 1) as i:
                    body(grp, i, i + first)
                body(grp, GROUP_PAIRS - 1, first + GROUP_PAIRS - 1)

        def span(at):
            return slice(at, at + HD1) if isinstance(at, int) else bass.ds(at, HD1)

        def is_(value, number):
            return isinstance(value, int) and value == number

        with nc.Block() as block:
            @block.sync
            def _(sp):
                def load(j, h, wait):
                    rows = span((2 * j + h) * HD1)
                    head = slice(2 * j + h, 2 * j + h + 1) if isinstance(j, int) else bass.ds(2 * j + h, 1)
                    alibi_rows = alibi_scratch[head].rearrange("o k t -> (o k) t")
                    if wait is not None:
                        sp.wait_ge(att.scores_ready, wait)
                    for tile, parts in ((q4, (0, 1, 1, 2)), (k4, (3, 4, 3, 4))):
                        for n, part in enumerate(parts):
                            sp.dma_start(tile[n * HD1:(n + 1) * HD1, h, :].bitcast(F32), scratch[part, rows, :])\
                              .then_inc(rows_loaded[h], 16)
                    sp.dma_start(k4[4 * HD1:KR, h, :].bitcast(F32), alibi_rows).then_inc(rows_loaded[h], 16)

                for h in range(2):
                    load(0, h, None)
                with sp.Fori(1, NH1 // 2) as j:
                    for h in range(2):
                        load(j, h, 3 * (4 * j - 4 + 2 * h + 2))

            @block.gpsimd
            def _(pool):
                pool.memset(q4[4 * HD1:KR, :, :].bitcast(F32), 1.0).then_inc(q4_ones, 1)
                pool.wait_ge(q4_ones, 1)
                pool.memset(vz[:, :, :, :].bitcast(F32), 0.0).then_inc(cleared, 1)
                pool.memset(none[:, :, :], 0.0).then_inc(cleared, 1)
                pool.wait_ge(cleared, 2)

                def place(i, J, h):
                    if not is_(J, 0):
                        pool.wait_ge(pv_done, 4 * J + 2 * h - 2)
                    was = ((i if not is_(i, 0) else GROUP_PAIRS) - 1) * PAIR + h * HD1
                    at, source = i * PAIR + h * HD1, (2 * J + h) * HD1
                    pool.tensor_copy(vz[:, h, :, span(was)], none[:, :, :].bitcast(F32R)).then_inc(placed, 1)
                    pool.tensor_copy(vz[:, h, :, span(at)], v1[:, :, :, span(source)].rearrange(
                        "p k t d -> p (k t) d")).then_inc(placed, 1)

                def pair(grp, i, J):
                    for u in range(4):
                        if u < 2:
                            place(i, J, u)
                        if not (is_(J, LAST) and u == 3):
                            att.normalise(pool, 4 * J + u + 1, u + 1)

                att.normalise(pool, 0, 0)
                each_pair(pool, pair)

            @block.tensor
            def _(pe):
                pe.wait_ge(q4_ones, 1)

                def score(J, u):
                    h, b = u % 4 // 2, u % 2
                    if b == 0:
                        pe.wait_ge(rows_loaded[h], 9 * 16 * (J + u // 4) + 9 * 16)

                    def product(pe_, region, q):
                        pe.matmul(region, q4[:, h, b * S + q * P:b * S + (q + 1) * P],
                                  k4[:, h, b * S:b * S + (q + 1) * P], start=True, stop=False)

                    att.scores(pe, 4 * J + u, product)

                def weigh_v(J, u):
                    h, b = u // 2, u % 2
                    if b == 0:
                        pe.wait_ge(placed, 4 * J + 2 * h + 2)
                    for kt in range(TS):
                        att.wait_pt(pe, 4 * J + u, kt)
                        v = [vz[:, h, k * NT + b * TS + kt, :] for k in range(2)]
                        mm = mm3(pe, O_BANKS[b][:, kt * P:S], v, att.pt(u, kt), False, False, skip_group_check=True)
                    mm.then_inc(pv_done, 1)

                def zeros(b, start, stop):
                    return pe.matmul(O_BANKS[b][:, :], zeros_bf[:, 0:P], zeros_bf[:, :], start=start, stop=stop,
                                     skip_group_check=True)

                def pair(grp, i, J):
                    for u in range(4):
                        if not (is_(J, LAST) and u == 3):
                            score(J, u + 1)
                        if u:
                            if is_(i, 0) and u == 1:
                                if grp:
                                    pe.wait_ge(o1_low, B * grp)
                                for b in range(B):
                                    zeros(b, True, False)
                            weigh_v(J, u - 1)
                        elif not is_(i, 0):
                            weigh_v(J - 1, 3)
                        for n in range(3):
                            att.turn(pe, 4 * J + u, u, n)
                    if is_(i, GROUP_PAIRS - 1):
                        weigh_v(J, 3)
                        for b in range(B):
                            zeros(b, False, True).then_inc(o1_ready, 1)

                score(0, 0)
                each_pair(pe, pair)

            @block.scalar
            def _(act):
                def pair(grp, i, J):
                    for u in range(4):
                        if not (is_(J, LAST) and u == 3):
                            att.exps(act, 4 * J + u + 1, u + 1)
                        for n in range(3):
                            att.turned_high(act, 4 * J + u, u, n)
                    if is_(i, GROUP_PAIRS - 1):
                        for b in range(B):
                            act.wait_ge(o1_ready, B * grp + b + 1)
                            act.activation(a1_hi[:, grp, b * S:(b + 1) * S], O_BANKS[b][:, :], ACT.Identity,
                                           bias=small[:, BV1 + grp:BV1 + grp + 1]).then_inc(o1_high, 1)

                att.exps(act, 0, 0)
                each_pair(act, pair)

            @block.vector
            def _(dve):
                def pair(grp, i, J):
                    for u in range(4):
                        if not (is_(J, LAST) and u == 3):
                            att.maxima(dve, 4 * J + u + 1, u + 1)
                            att.reciprocals(dve, 4 * J + u + 1, u + 1)
                        for n in range(3):
                            att.turned_low(dve, 4 * J + u, u, n)
                    if is_(i, GROUP_PAIRS - 1):
                        for b in range(B):
                            dve.wait_ge(o1_high, B * grp + b + 1)
                            at = slice(b * S, (b + 1) * S)
                            dve.scalar_tensor_tensor(a1_lo[:, grp, at], O_BANKS[b][:, :],
                                                     small[:, BV1 + grp:BV1 + grp + 1],
                                                     a1_hi[:, grp, at].bitcast(F32), ALU.add, ALU.subtract)\
                               .then_inc(o1_low, 1)

                att.maxima(dve, 0, 0)
                att.reciprocals(dve, 0, 0)
                each_pair(dve, pair)

    HALF = ins["w_down"].shape[3] // D * P
    IC = HALF // P
    with late, ExitStack() as st5:
        w1_raw = sbuf(st5, "w1_raw", [P, DC, 2, HALF])
        w2_raw = sbuf(st5, "w2_raw", [P, IC, D])
        w1 = [sbuf(st5, f"w1_{x}", [P, 2, DC, 2, HALF], F32R) for x in ("hi", "lo")]
        w2 = [sbuf(st5, f"w2_{x}", [P, 2, IC, D], F32R) for x in ("hi", "lo")]
        silu = sbuf(st5, "silu_gate", [P, 2, S])
        gated = sbuf(st5, "gated_up", [P, 2, S])
        weighed = sbuf(st5, "weighed", [P, 2, S])
        hid = [sbuf(st5, f"hidden_{x}", [P, B, IC, S], F32R) for x in ("hi", "lo")]
        w1_loaded = sem("w1_loaded")
        w2_loaded = sem("w2_loaded")
        w1_split = sem("w1_split")
        w2_split = sem("w2_split")
        gu_ready = sem("gu_ready")
        silu_done = sem("silu_done")
        up_done = sem("up_done")
        weigh_done = sem("weigh_done")
        hid_high = sem("hid_high")
        hid_low = sem("hid_low")
        down_done = sem("down_done")
        sums_ready = sem("sums_ready")
        sums_copied = sem("sums_copied")
        out_turned = sem("out_turned")
        out_added = sem("out_added")
        stored = sem("stored")
        Y_BANK = banks[0:4]
        NHALF = E1 * HALVES

        with nc.Block() as block:
            @block.sync
            def _(sp):
                def load(e, hf, j):
                    if not (isinstance(j, int) and j == 0):
                        sp.wait_ge(w1_split, 2 * j)
                        sp.wait_ge(w2_split, 2 * j)
                    at = e if isinstance(e, int) else bass.ds(e, 1)
                    w1_src, w2_src = ins["w_gate_up"][at, hf], ins["w_down"][at, hf]
                    if not isinstance(e, int):
                        w1_src, w2_src = (w.rearrange("o p n -> (o p) n") for w in (w1_src, w2_src))
                    sp.dma_start(w1_raw[:, :, :, :].rearrange("p c k n -> p (c k n)"), w1_src)\
                      .then_inc(w1_loaded, 16)
                    sp.dma_start(w2_raw[:, :, :].rearrange("p c n -> p (c n)"), w2_src).then_inc(w2_loaded, 16)

                for hf in range(2):
                    load(0, hf, hf)
                with sp.Fori(1, E1) as e:
                    for hf in range(2):
                        load(e, hf, 2 * e + hf)
                for n in range(4):
                    sp.wait_ge(out_added, n + 1)
                    sp.dma_start(out[2 * n * P:(2 * n + 2) * P, :].rearrange("(t p) d -> p t d", p=P),
                                 xs[:, 2 * n:2 * n + 2, :]).then_inc(stored, 16)
                sp.wait_ge(stored, 64)

            @block.gpsimd
            def _(pool):
                def split(raw_, parts, loaded, done, j, used):
                    wait_apart(pool, (loaded, 16 * (j + 1)), *used)
                    pool.tensor_scalar(parts[0], raw_, 1.0, 1.0, ALU.mult, ALU.mult).then_inc(done, 1)
                    pool.wait_ge(done, 2 * j + 1)
                    pool.tensor_tensor(parts[1], raw_, parts[0].bitcast(F32), ALU.subtract).then_inc(done, 1)

                def split_w1(slot, j, *used):
                    split(w1_raw[:, :, :, :].rearrange("p c k n -> p (c k n)"),
                          [w[:, slot].rearrange("p c k n -> p (c k n)") for w in w1], w1_loaded, w1_split, j, used)

                def split_w2(slot, j, *used):
                    split(w2_raw[:, :, :], [w[:, slot] for w in w2], w2_loaded, w2_split, j, used)

                def half(e, hf, more, first):
                    j = 2 * e + hf
                    for k in range(2 * IC):
                        s, b = 4 * j + k, k // IC
                        waits = [(up_done, s + 1)]
                        if not (first and k < 2):
                            waits.append((hid_low, s - 1))
                        wait_apart(pool, *waits)
                        weight = (w_bc[:, e, b * S:(b + 1) * S] if isinstance(e, int) else
                                  w_bc[:, bass.ds(e, 1), b * S:(b + 1) * S].rearrange("p o t -> p (o t)"))
                        pool.tensor_tensor(weighed[:, k % 2, :], gated[:, k % 2, :], weight, ALU.mult)\
                            .then_inc(weigh_done, 1)
                        if more and k == 0:
                            split_w1(1 - hf, j + 1, *([] if first else [(gu_ready, 4 * j)]))
                        if more and k == 2:
                            split_w2(1 - hf, j + 1, *([] if first else [(down_done, 2 * j)]))

                split_w1(0, 0)
                split_w2(0, 0)
                half(0, 0, True, True)
                half(0, 1, True, False)
                with pool.Fori(1, E1 - 1) as e:
                    half(e, 0, True, False)
                    half(e, 1, True, False)
                half(E1 - 1, 0, True, False)
                half(E1 - 1, 1, False, False)

            @block.tensor
            def _(pe):
                for n in range(2 * DC):
                    c, b = n // 2, n % 2
                    w = slice(3 * D + c * P, 3 * D + (c + 1) * P)
                    for grp in range(GROUPS):
                        at = slice(b * S, (b + 1) * S)
                        mm3(pe, Y_BANK[n][:, :], (wqkv_hi[:, grp, w], wqkv_lo[:, grp, w]),
                            (a1_hi[:, grp, at], a1_lo[:, grp, at]), grp == 0, False, skip_group_check=True)

                def down(g, hf, b, last=False):
                    pe.wait_ge(hid_low, 2 * g + 2)
                    for c in range(DC):
                        for ic in range(IC):
                            mm = mm3(pe, Y_BANK[2 * c + b][:, :], [w[:, hf, ic, c * P:(c + 1) * P] for w in w2],
                                     [h[:, b, ic, :] for h in hid], False, last and ic == IC - 1,
                                     skip_group_check=True)
                    mm.then_inc(down_done, 1)

                def expert(e, first):
                    for hf in range(2):
                        j = 2 * e + hf
                        pe.wait_ge(w1_split, 2 * j + 2)
                        for b in range(B):
                            g = 2 * j + b
                            for ic in range(IC):
                                s = 2 * g + ic
                                if not (first and hf == 0 and b == 0):
                                    pe.wait_ge(up_done, s - 1)
                                for k in range(2):
                                    for c in range(DC):
                                        at = slice(b * S, (b + 1) * S)
                                        mm = mm3(pe, banks[4 + 2 * ic + k][:, :],
                                                 [w[:, hf, c, k, ic * P:(ic + 1) * P] for w in w1],
                                                 (xt_hi[:, c, at], xt_lo[:, c, at]), c == 0, c == DC - 1)
                                mm.then_inc(gu_ready, 1)
                            if not (first and hf == 0 and b == 0):
                                if b == 1:
                                    pe.wait_ge(w2_split, 2 * j + 2)
                                down(g - 1, hf if b else 1 - hf, 1 - b)

                expert(0, True)
                with pe.Fori(1, E1) as e:
                    expert(e, False)
                down(2 * NHALF - 1, 1, 1, last=True)
                pe.matmul(Y_BANK[0][:, :], zeros_bf[:, 0:P], zeros_bf[:, :], start=False, stop=True,
                          skip_group_check=True)
                pe.matmul(Y_BANK[2][:, :], zeros_bf[:, 0:P], zeros_bf[:, :], start=False, stop=True,
                          skip_group_check=True).then_inc(sums_ready, 1)
                pe.wait_ge(sums_copied, 4)
                for t in range(NT):
                    for c in range(DC):
                        at = (t % 2) * D + c * P
                        mm = pe.transpose(banks[4 + t // 2][:, at:at + P], acc[:, c, t * P:(t + 1) * P], ident[:, :])
                    if t % 2:
                        mm.then_inc(out_turned, 1)

            @block.scalar
            def _(act):
                def step(s, k, lag):
                    act.wait_ge(gu_ready, s + 1)
                    act.activation(silu[:, k % 2, :], banks[4 + 2 * (k % 2)][:, :], ACT.Silu).then_inc(silu_done, 1)
                    if lag:
                        high(s - 1, (k - 1) % 4)

                def high(s, k):
                    act.wait_ge(weigh_done, s + 1)
                    act.activation(hid[0][:, k // 2, k % 2, :], weighed[:, k % 2, :], ACT.Copy).then_inc(hid_high, 1)

                for k in range(8):
                    step(k, k % 4, k > 0)
                with act.Fori(1, E1) as e:
                    for k in range(8):
                        step(8 * e + k, k % 4, True)
                high(4 * NHALF - 1, 3)

            @block.vector
            def _(dve):
                def step(s, k, lag):
                    dve.wait_ge(silu_done, s + 1)
                    dve.tensor_tensor(gated[:, k % 2, :], banks[5 + 2 * (k % 2)][:, :], silu[:, k % 2, :], ALU.mult)\
                       .then_inc(up_done, 1)
                    if lag:
                        low(s - 1, (k - 1) % 4)

                def low(s, k):
                    dve.wait_ge(hid_high, s + 1)
                    dve.tensor_tensor(hid[1][:, k // 2, k % 2, :], weighed[:, k % 2, :],
                                      hid[0][:, k // 2, k % 2, :].bitcast(F32), ALU.subtract).then_inc(hid_low, 1)

                for k in range(8):
                    step(k, k % 4, k > 0)
                with dve.Fori(1, E1) as e:
                    for k in range(8):
                        step(8 * e + k, k % 4, True)
                low(4 * NHALF - 1, 3)
                dve.wait_ge(sums_ready, 1)
                for n in range(2 * DC):
                    c, b = n // 2, n % 2
                    dve.tensor_scalar(acc[:, c, b * S:(b + 1) * S], Y_BANK[n][:, :],
                                      small[:, BO1 + c:BO1 + c + 1], None, ALU.add).then_inc(sums_copied, 1)
                for n in range(4):
                    dve.wait_ge(out_turned, n + 1)
                    rows = xs[:, 2 * n:2 * n + 2, :]
                    dve.tensor_tensor(rows, banks[4 + n][:, :].rearrange("p (t d) -> p t d", d=D), rows, ALU.add)\
                       .then_inc(out_added, 1)
    whole.close()


def kernel(**inputs):
    import concourse.bacc as bacc
    from concourse.bass_utils import run_bass_kernel_spmd

    def layout(a):
        return np.ascontiguousarray(a)

    x = np.asarray(inputs["L0_attn_query"])
    B, S, D = x.shape
    DC = D // P
    w_q, w_k, w_v, w_o = (np.asarray(inputs[f"L0_attn_w_{n}"]) for n in "qkvo")
    pairs = w_q.shape[1] // (2 * P)
    qk = np.stack([w_q, w_k]).reshape(2, DC, P, pairs, 2, P).transpose(4, 3, 2, 1, 0, 5)
    v = w_v.reshape(DC, P, pairs, 2 * P).transpose(2, 1, 0, 3)
    o = w_o.reshape(pairs, 2, P, D).transpose(0, 2, 1, 3)

    def columns(name):
        return np.asarray(inputs[name]).reshape(-1, P).T

    biases = np.concatenate([columns(f"L0_attn_b_{n}") for n in "qkvo"]
                            + [columns(f"L1_attn_b{n}") for n in "qkvo"], axis=1)
    e0 = inputs["L0_ffn_sim_matrix"].shape[1]
    e = np.arange(e0)
    p = np.arange(P)
    width = inputs["L0_ffn_w_v"].shape[1]
    gate_up = np.asarray(inputs["L1_ffn_gate_up_proj"])
    down = np.asarray(inputs["L1_ffn_down_proj"])
    e1, two_i, _ = gate_up.shape
    half = two_i // 4
    gu = gate_up.reshape(e1, 2, 2, half, DC, P).transpose(0, 2, 5, 4, 1, 3)
    dn = down.reshape(e1, D, 2, half // P, P).transpose(0, 2, 4, 3, 1)
    nh1 = 16
    start = 2 ** (-2 ** (-(np.log2(nh1) - 3)))
    slopes = np.array([start * start ** i for i in range(nh1)], dtype=np.float32)
    alibi = (-slopes[:, None] * (S - 1 - np.arange(S, dtype=np.float32))[None, :]).astype(np.float32)
    alibi = np.concatenate([alibi] * B, axis=1)

    arrays = {
        "x": layout(x.reshape(B * S, D)),
        "w_qk0": layout(qk.reshape(2, pairs, P, DC * 2 * P)),
        "w_v0": layout(v.reshape(pairs, P, DC * 2 * P)),
        "w_o0": layout(o.reshape(pairs, P, 2 * D)),
        "biases": layout(biases),
        "sim": layout(inputs["L0_ffn_sim_matrix"]),
        "gates": layout(np.broadcast_to(np.asarray(inputs["L0_ffn_gates"]), (B, e0))),
        "expert_v": layout(np.asarray(inputs["L0_ffn_w_v"]).reshape(e0 * width, D)),
        "expert_o": layout(np.asarray(inputs["L0_ffn_o_weights"]).reshape(e0 * width, D)),
        "w_qkv1": layout(np.concatenate([np.asarray(inputs[f"L1_attn_W{n}"]) for n in "qkvo"], axis=1)),
        "router": layout(np.asarray(inputs["L1_ffn_gate_weight"]).T),
        "w_gate_up": layout(gu.reshape(e1, 2, P, DC * 2 * half)),
        "w_down": layout(dn.reshape(e1, 2, P, (half // P) * D)),
        "ident": np.eye(P, dtype=np.float32),
        "after": (p[None, :] > p[:, None]).astype(np.float32),
        "below": layout(np.broadcast_to(e[None, :] < e[:, None], (B, e0, e0)).astype(np.float32)),
        "sel_half": (e[:, None] % 2 == p[None, :] // width).astype(np.float32),
        "sel_tile": (e[:, None] // 2 == np.arange(e0 * width // P)[None, :]).astype(np.float32),
        "same_h": (p[:, None] % width == np.arange(width)[None, :]).astype(np.float32),
        "alibi": layout(alibi),
        "before8": layout(np.broadcast_to(np.arange(e1)[None, :] < np.arange(e1)[:, None],
                                          (P, e1, e1)).astype(np.float32)),
        "sel8": layout(np.repeat(np.eye(e1, dtype=np.float32)[:, :, None], P, axis=2)),
    }
    nc = bacc.Bacc("TRN2", target_bir_lowering=False, num_devices=1)
    ins = {n: nc.dram_tensor(f"in_{n}", a.shape, mybir.dt.from_np(a.dtype), kind="ExternalInput").ap()
           for n, a in arrays.items()}
    out = nc.dram_tensor("out_x", (B * S, D), F32, kind="ExternalOutput").ap()
    build(nc, ins, out)
    r = run_bass_kernel_spmd(nc, [{f"in_{n}": a for n, a in arrays.items()}], core_ids=[0])
    return r.results[0]["out_x"].reshape(B, S, D)
```

```python
from contextlib import ExitStack

import numpy as np
import concourse.bass as bass
from concourse import mybir

ALU = mybir.AluOpType
ACT = mybir.ActivationFunctionType
AX = mybir.AxisListType.X
F32 = mybir.dt.float32
F32R = mybir.dt.float32r
BF16 = mybir.dt.bfloat16

P = 128
EPS = 1e-5
FLT_MAX = 3.4028234663852886e38
MASKED = -1e30


def mm3(pe, out, a, b, start, stop, **kw):
    (a_hi, a_lo), (b_hi, b_lo) = a, b
    pe.matmul(out, a_hi, b_hi, start=start, stop=False, **kw)
    pe.matmul(out, a_hi, b_lo, start=False, stop=False, **kw)
    return pe.matmul(out, a_lo, b_hi, start=False, stop=stop, **kw)


def build(nc, ins, out):
    x_in = ins["x"]
    T, D = x_in.shape
    B = 2
    S = T // B
    NT = T // P
    TS = S // P
    DC = D // P
    NH0 = ins["w_o0"].shape[0] * 2
    PAIRS = NH0 // 2
    E0, H0 = 32, 64
    EH = E0 * H0 // P
    NH1 = 16
    HD1 = D // NH1
    E1 = ins["w_gate_up"].shape[0]
    HALVES = ins["w_gate_up"].shape[1]
    SCALE0 = float(P) ** -0.5
    SCALE1 = float(HD1) ** -0.5
    SCORES = sum((q + 1) * P for q in range(TS))

    P_AT = [sum((j + 1) * P for j in range(q)) for q in range(TS)]
    Q_ORDER = [3, 2, 0, 1]
    T_GROUPS = [[0], [1, 3], [2]]
    T_AT, at = {}, 0
    for group in T_GROUPS:
        for kt in group:
            T_AT[kt] = at
            at += S - kt * P
    T_SPAN = [(T_AT[g[0]], sum(S - kt * P for kt in g)) for g in T_GROUPS]

    whole = ExitStack()

    def psum(name):
        return whole.enter_context(nc.psum_tensor(name, [P, 512], F32))

    banks = [psum(f"bank{n}") for n in range(8)]

    def sbuf(stack, name, shape, dt=F32):
        return stack.enter_context(nc.sbuf_tensor(name, shape, dt))

    def sem(name):
        return whole.enter_context(nc.semaphore(name))

    def wait_apart(eng, *waits):
        held = [(signal, v if isinstance(v, int) else eng.to_reg(v)) for signal, v in waits]
        eng.wait_ge(consts_done, 1)
        for signal, v in held:
            eng.wait_ge(signal, v)

    consts_done = sem("consts_done")

    xs = sbuf(whole, "x_rows", [P, NT, D])
    out_bias = sbuf(whole, "out_bias", [P, 2, D])
    xt_hi = sbuf(whole, "xnorm_T_hi", [P, DC, T], F32R)
    xt_lo = sbuf(whole, "xnorm_T_lo", [P, DC, T], F32R)
    ident = sbuf(whole, "ident", [P, P])
    ident_bf = sbuf(whole, "ident_bf", [P, P], BF16)
    mask_bf = sbuf(whole, "mask_bf", [P, P], BF16)
    ones = sbuf(whole, "ones", [P, P])
    zeros_bf = sbuf(whole, "zeros_bf", [P, 512], BF16)
    small = sbuf(whole, "biases", list(ins["biases"].shape))
    BQ0, BK0, BV0 = 0, NH0, 2 * NH0
    BQ1, BK1, BV1 = 3 * NH0, 3 * NH0 + DC, 3 * NH0 + 2 * DC

    def layer_norm(tag):
        st = ExitStack()
        xn = sbuf(st, f"xnorm_{tag}", [P, NT, D])
        stats = sbuf(st, f"stats_{tag}", [P, NT, 6])
        mv = sbuf(st, f"mean_var_{tag}", [P, NT, 2])
        std = sbuf(st, f"std_{tag}", [P, NT, 2])
        stats_done = sem(f"stats_done_{tag}")
        var_done = sem(f"var_done_{tag}")
        std_done = sem(f"std_done_{tag}")
        rstd_done = sem(f"rstd_done_{tag}")
        rows_done = sem(f"rows_done_{tag}")
        turned = sem(f"turned_{tag}")
        hi_done = sem(f"xt_hi_done_{tag}")
        lo_done = sem(f"xt_lo_done_{tag}")

        def dve_part(dve, x_ready):
            for t in range(NT):
                x_ready(dve, t)
                dve.bn_stats(stats[:, t, :], xs[:, t, :]).then_inc(stats_done, 1)
            for t in range(NT):
                dve.wait_ge(stats_done, t + 1)
                dve.bn_aggr(mv[:, t, :], stats[:, t, :]).then_inc(var_done, 1)
            dve.wait_ge(var_done, NT)
            dve.tensor_scalar(std[:, :, 0], mv[:, :, 1], EPS, None, ALU.add).then_inc(var_done, 1)
            dve.wait_ge(std_done, 1)
            dve.reciprocal(std[:, :, 1], std[:, :, 0]).then_inc(rstd_done, 1)
            dve.wait_ge(rstd_done, 1)
            for t in range(NT):
                dve.tensor_scalar(xn[:, t, :], xs[:, t, :], mv[:, t, 0:1], std[:, t, 1:2],
                                  ALU.subtract, ALU.mult).then_inc(rows_done, 1)
            for n in range(2 * DC):
                dve.wait_ge(hi_done, n + 1)
                c, b = n // 2, n % 2
                at = slice(b * S, (b + 1) * S)
                dve.tensor_tensor(xt_lo[:, c, at], banks[n][:, :], xt_hi[:, c, at].bitcast(F32),
                                  ALU.subtract).then_inc(lo_done, 1)

        def act_part(act):
            act.wait_ge(var_done, NT + 1)
            act.activation(std[:, :, 0], std[:, :, 0], ACT.Sqrt).then_inc(std_done, 1)
            for n in range(2 * DC):
                act.wait_ge(turned, n + 1)
                c, b = n // 2, n % 2
                act.activation(xt_hi[:, c, b * S:(b + 1) * S], banks[n][:, :], ACT.Copy).then_inc(hi_done, 1)

        def pe_part(pe):
            for n in range(2 * DC):
                c, b = n // 2, n % 2
                for j in range(TS):
                    t = b * TS + j
                    pe.wait_ge(rows_done, t + 1)
                    mm = pe.transpose(banks[n][:, j * P:(j + 1) * P], xn[:, t, c * P:(c + 1) * P], ident[:, :])
                mm.then_inc(turned, 1)

        return st, xn, rows_done, hi_done, lo_done, dve_part, act_part, pe_part

    SCORE_BANK = {3: banks[0][:, 0:S], 2: banks[1][:, P:P + 3 * P], 0: banks[1][:, 0:P], 1: banks[2][:, 0:2 * P]}

    class Attention:

        def __init__(self, tag, stack, t_bank, probs, pt_lo):
            self.t_bank, self.slots = t_bank, len(pt_lo)
            self.probs = probs
            self.pt_hi = [sbuf(stack, f"probs_T_hi{k}_{tag}", [P, SCORES], F32R) for k in range(self.slots)]
            self.pt_lo = pt_lo
            self.neg_max = sbuf(stack, f"neg_max_{tag}", [P, 2, TS])
            self.row_sum = sbuf(stack, f"row_sum_{tag}", [P, 2, TS])
            self.recip = sbuf(stack, f"recip_{tag}", [P, 2, TS])
            self.scores_ready = sem(f"scores_ready_{tag}")
            self.max_ready = sem(f"max_ready_{tag}")
            self.probs_ready = sem(f"probs_ready_{tag}")
            self.recip_ready = sem(f"recip_ready_{tag}")
            self.norm_done = sem(f"norm_done_{tag}")
            self.t_ready = sem(f"t_ready_{tag}")
            self.t_high = sem(f"t_high_{tag}")
            self.t_low = sem(f"t_low_{tag}")

        def scores(self, pe, U, product):
            for n, group in enumerate(([3], [2, 0], [1])):
                if not (isinstance(U, int) and U == 0):
                    pe.wait_ge(self.probs_ready, 4 * U + (1, 3, 4)[n] - 4)
                for q in group:
                    region = SCORE_BANK[q]
                    product(pe, region, q)
                    mm = pe.matmul(region[:, q * P:(q + 1) * P], ident_bf[:, :], mask_bf[:, :],
                                   start=False, stop=True)
                mm.then_inc(self.scores_ready, 1)

        def turn(self, pe, U, u, n):
            if n == 0:
                pe.wait_ge(self.norm_done, 4 * U + 4)
            if n == 2 and self.t_bank[2] is self.t_bank[0]:
                pe.wait_ge(self.t_low, 3 * U + 1)
            at = 0
            for kt in T_GROUPS[n]:
                for q in range(kt, TS):
                    mm = pe.transpose(self.t_bank[n][:, at:at + P],
                                      self.probs[u % 2][:, P_AT[q] + kt * P:P_AT[q] + (kt + 1) * P], ident[:, :])
                    at += P
            mm.then_inc(self.t_ready, 1)

        def wait_pt(self, pe, U, kt):
            pe.wait_ge(self.t_low, 3 * U + {0: 1, 1: 2, 3: 2, 2: 3}[kt])

        def pt(self, u, kt):
            at = slice(T_AT[kt], T_AT[kt] + S - kt * P)
            return self.pt_hi[u % self.slots][:, at], self.pt_lo[u % self.slots][:, at]

        def exps(self, act, U, u):
            for n, q in enumerate(Q_ORDER):
                act.wait_ge(self.max_ready, 4 * U + (1, 3, 3, 4)[n])
                act.activation(self.probs[u % 2][:, P_AT[q]:P_AT[q] + (q + 1) * P], SCORE_BANK[q], ACT.Exp,
                               bias=self.neg_max[:, u % 2, q:q + 1], scale=1.0,
                               accum_out=self.row_sum[:, u % 2, q:q + 1]).then_inc(self.probs_ready, 1)

        def turned_high(self, act, U, u, n):
            at, w = T_SPAN[n]
            act.wait_ge(self.t_ready, 3 * U + n + 1)
            act.activation(self.pt_hi[u % self.slots][:, at:at + w], self.t_bank[n][:, 0:w], ACT.Copy)\
               .then_inc(self.t_high, 1)

        def maxima(self, dve, U, u):
            for n, q in enumerate(Q_ORDER):
                dve.wait_ge(self.scores_ready, 3 * U + (1, 2, 2, 3)[n])
                dve.tensor_reduce(self.neg_max[:, u % 2, q:q + 1], SCORE_BANK[q], AX, ALU.max, negate=True)\
                   .then_inc(self.max_ready, 1)

        def reciprocals(self, dve, U, u):
            for n in (1, 0):
                dve.wait_ge(self.probs_ready, 4 * U + (4 - 2 * n))
                dve.reciprocal(self.recip[:, u % 2, 2 * n:2 * n + 2], self.row_sum[:, u % 2, 2 * n:2 * n + 2])\
                   .then_inc(self.recip_ready, 1)

        def turned_low(self, dve, U, u, n):
            at, w = T_SPAN[n]
            dve.wait_ge(self.t_high, 3 * U + n + 1)
            dve.tensor_tensor(self.pt_lo[u % self.slots][:, at:at + w], self.t_bank[n][:, 0:w],
                              self.pt_hi[u % self.slots][:, at:at + w].bitcast(F32), ALU.subtract)\
               .then_inc(self.t_low, 1)

        def normalise(self, pool, U, u):
            for n, q in enumerate(Q_ORDER):
                if n % 2 == 0:
                    wait_apart(pool, (self.recip_ready, 2 * U + n // 2 + 1))
                row = self.probs[u % 2][:, P_AT[q]:P_AT[q] + (q + 1) * P]
                pool.tensor_scalar(row, row, self.recip[:, u % 2, q:q + 1], 1.0, ALU.mult, ALU.mult)\
                    .then_inc(self.norm_done, 1)

    UNITS = 4
    RING = 16
    RING0 = 10
    late = ExitStack()
    loaded1 = sem("loaded1")
    loaded_raw1 = sem("loaded_raw1")
    raw = sbuf(late, "w_qkvo1", [P, DC, 4 * D])
    al = sbuf(late, "alibi", [P, NH1 * T // P])
    rw = sbuf(late, "router", [P, DC, E1])
    before8 = sbuf(late, "before8", [P, E1, E1])
    al_hi = sbuf(late, "alibi_hi", [P, NH1 * T // P], F32R)
    al_lo = sbuf(late, "alibi_lo", [P, NH1 * T // P], F32R)
    rw_hi = sbuf(late, "router_hi", [P, DC, E1], F32R)
    rw_lo = sbuf(late, "router_lo", [P, DC, E1], F32R)
    wqkv_hi = sbuf(late, "w_qkvo1_hi", [P, DC, 4 * D], F32R)
    wqkv_lo = sbuf(late, "w_qkvo1_lo", [P, DC, 4 * D], F32R)
    scaled1 = sem("scaled1")
    split1 = sem("split1")
    rw_split = sem("rw_split")
    al_split = sem("alibi_split")
    sel_done = sem("sel_done")
    sel16 = sbuf(late, "sel16", [2 * E1, E1, P], F32R)
    st2 = ExitStack()
    att = Attention("0", st2, [banks[3], banks[4], banks[3]],
                    [sbuf(st2, f"probs{k}", [P, SCORES]) for k in range(2)],
                    [sbuf(st2, "probs_T_lo", [P, SCORES], F32R)])
    qk_raw = sbuf(st2, "qk_raw", [P, 2, DC, 2, P])
    v_raw = sbuf(st2, "v_raw", [P, DC, 2 * P])
    o_raw = sbuf(st2, "o_raw", [P, 2, D])
    qk_w = [sbuf(st2, f"qk_w_{x}", [P, 2, DC, 2, P], F32R) for x in ("hi", "lo")]
    v_w = [sbuf(st2, f"v_w_{x}", [P, DC, 2 * P], F32R) for x in ("hi", "lo")]
    o_w = [sbuf(st2, f"o_w_{x}", [P, 2, D], F32R) for x in ("hi", "lo")]
    qk_T = [sbuf(st2, f"qk_T_{x}", [P, 2, UNITS, S], F32R) for x in ("hi", "lo")]
    v_rows = [sbuf(st2, f"v_rows_{x}", [P, B, TS, 2 * P], F32R) for x in ("hi", "lo")]
    attn_T = [sbuf(st2, f"attn_T_{x}", [P, 2, S], F32R) for x in ("hi", "lo")]
    O_BANK, R_BANK = banks[5], banks[6:8]

    qk_loaded = [sem(f"qk_loaded{h}") for h in range(2)]
    v_loaded = sem("v_loaded")
    o_loaded = sem("o_loaded")
    qk_split = [sem(f"qk_split{h}") for h in range(2)]
    v_split = sem("v_split")
    o_split = sem("o_split")
    ring_full = sem("ring_full")
    ring_high = sem("ring_high")
    ring_free = sem("ring_free")
    o_ready = sem("o_ready")
    o_high = sem("o_high")
    o_low = sem("o_low")
    QK_USE = [2, 4, 10, 12]
    V_USE = [6, 14]
    OUT_USE = [8, 0]
    OUT_USE_LAST = [2, 0]
    HIGHS = 12
    QK_HIGH = [0, 2, 6, 8]
    V_HIGH = [4, 10]

    def pair_of(ap, j):
        return ap[j] if isinstance(j, int) else ap[bass.ds(j, 1)].rearrange("o p n -> (o p) n")

    def load_qk(sp, h, j):
        if not isinstance(j, int) or j:
            wait_apart(sp, (qk_split[h], 3 * j))
        sp.dma_start(qk_raw[:, h].rearrange("p c k n -> p (c k n)"), pair_of(ins["w_qk0"][h], j))\
          .then_inc(qk_loaded[h], 16)

    def load_v(sp, j):
        if not isinstance(j, int) or j:
            wait_apart(sp, (v_split, 2 * j))
        sp.dma_start(v_raw[:, :, :].rearrange("p c n -> p (c n)"), pair_of(ins["w_v0"], j))\
          .then_inc(v_loaded, 16)

    def load_o(sp, j):
        if not isinstance(j, int) or j:
            wait_apart(sp, (o_split, 2 * j))
        sp.dma_start(o_raw[:, :, :].rearrange("p h n -> p (h n)"), pair_of(ins["w_o0"], j))\
          .then_inc(o_loaded, 16)

    def split(pool, raw, parts, done, n):
        pool.tensor_scalar(parts[0], raw, 1.0, 1.0, ALU.mult, ALU.mult).then_inc(done, 1)
        pool.wait_ge(done, n + 1)
        pool.tensor_tensor(parts[1], raw, parts[0].bitcast(F32), ALU.subtract).then_inc(done, 1)

    def split_qk(pool, h, j, used):
        wait_apart(pool, (qk_loaded[h], 16 * (j + 1)), *([] if used is None else [(ring_full, used)]))
        for c in range(DC):
            mul = pool.tensor_scalar(qk_raw[:, h, c, 0, :], qk_raw[:, h, c, 0, :], SCALE0, 1.0,
                                     ALU.mult, ALU.mult)
        mul.then_inc(qk_split[h], 1)
        wait_apart(pool, (qk_split[h], 3 * j + 1))
        split(pool, qk_raw[:, h].rearrange("p c k n -> p (c k n)"),
              [w[:, h].rearrange("p c k n -> p (c k n)") for w in qk_w], qk_split[h], 3 * j + 1)

    def split_v(pool, j, used):
        wait_apart(pool, (v_loaded, 16 * (j + 1)), *([] if used is None else [(ring_full, used)]))
        split(pool, v_raw[:, :, :], [w[:, :, :] for w in v_w], v_split, 2 * j)

    def split_o(pool, j, used):
        wait_apart(pool, (o_loaded, 16 * (j + 1)), (ring_full, used))
        split(pool, o_raw[:, :, :], [w[:, :, :] for w in o_w], o_split, 2 * j)

    def bias_col(at, i, h):
        return small[:, bass.ds(2 * i + (at + h), 1)] if not isinstance(i, int) \
            else small[:, at + 2 * i + h:at + 2 * i + h + 1]


    def qk_product(pe, bank, u, k):
        h, b = u % 2, u // 2
        cols = slice(b * S, (b + 1) * S)
        for c in range(DC):
            mm = mm3(pe, bank[:, :], [w[:, h, c, k, :] for w in qk_w], (xt_hi[:, c, cols], xt_lo[:, c, cols]),
                     c == 0, c == DC - 1)
        return mm

    def qk_high(act, bank, u, k, j):
        return act.activation(qk_T[0][:, k, u, :], bank[:, :], ACT.Identity, bias=bias_col((BQ0, BK0)[k], j, u % 2))

    def qk_low(dve, bank, u, k, j):
        return dve.scalar_tensor_tensor(qk_T[1][:, k, u, :], bank[:, :], bias_col((BQ0, BK0)[k], j, u % 2),
                                        qk_T[0][:, k, u, :].bitcast(F32), ALU.add, ALU.subtract)

    loaded_x = [sem(f"loaded_x{n}") for n in range(B)]
    loaded_const = sem("loaded_const")
    loaded_sim = sem("loaded_sim")
    loaded_ident = sem("loaded_ident")
    loaded_sel = sem("loaded_sel")
    loaded_ev = [sem(f"loaded_ev{t}") for t in range(2)]
    loaded_eo = [sem(f"loaded_eo{t}") for t in range(2)]
    ln0 = layer_norm("0")
    st1, xn, rows_done, hi_done, lo_done, ln_dve, ln_act, ln_pe = ln0
    with st1:
        sm = sbuf(st1, "sim", [P, DC, E0])
        gates = sbuf(st1, "gates", [B, E0])
        sr = sbuf(st1, "seq_rep", [P, DC, B])
        sq = sbuf(st1, "squares", [P, DC, B + E0])
        sel_half = sbuf(st1, "sel_half", [E0, P])
        sel_tile = sbuf(st1, "sel_tile", [E0, EH])
        same_h = sbuf(st1, "same_h", [P, H0])
        mask = sbuf(st1, "after", [P, P])
        g = sbuf(st1, "gating", [B, 16, E0])
        gs = sbuf(st1, "gating_scalars", [B, 8])
        cmp1, cmp2 = (xn[0:B, k * TS:(k + 1) * TS, :].rearrange("b t d -> b (t d)")
                      .rearrange("b (e j) -> b e j", e=E0) for k in range(2))
        below = att.probs[0][0:B, 0:E0 * E0].rearrange("b (e j) -> b e j", e=E0)
        spread = raw[:, :, :].rearrange("p c n -> p (c n)").rearrange("p (t n) -> p t n", t=EH)
        wv_hi, wv_lo = (x[:, 0:D].rearrange("p (c m) -> p c m", c=DC) for x in (att.pt_hi[0], att.pt_lo[0]))
        wo_hi, wo_lo = (x[:, D:2 * D] for x in (att.pt_hi[0], att.pt_lo[0]))
        c_hi, c_lo = (x[:, :, :].rearrange("p h t -> p (h t)") for x in attn_T)
        r_T = sbuf(st1, "routing_T", [E0, B])
        r_spread = sbuf(st1, "routing_spread", [E0, EH, B])
        r_col = sbuf(st1, "routing_col", [P, EH, B])
        ev = sbuf(st1, "expert_v", [P, EH, D])
        eo = sbuf(st1, "expert_o", [P, EH, D])

        bias_scaled = sem("bias_scaled")
        rep_done = sem("rep_done")
        gate_step = sem("gate_step")
        sr_done = sem("sr_done")
        norms_done = sem("norms_done")
        gate_act = sem("gate_act")
        r_turned = sem("r_turned")
        r_sp_done = sem("r_sp_done")
        r_col_done = sem("r_col_done")
        spread_done = sem("spread_done")
        mixed = sem("mixed")
        mixed_hi = sem("mixed_hi")
        mixed_lo = sem("mixed_lo")
        comb = sem("comb")
        comb_hi = sem("comb_hi")
        comb_lo = sem("comb_lo")
        ffn_ready = sem("ffn_ready")
        biased = sem("biased")
        ffn_added = sem("ffn_added")

        FIRST_BANKS = [banks[n] for n in (6, 7, 0, 1, 2, 3)]

        with nc.Block() as block:
            @block.sync
            def _(sp):
                for n in range(B):
                    sp.dma_start(xs[:, n * TS:(n + 1) * TS, :],
                                 x_in[n * S:(n + 1) * S, :].rearrange("(t p) d -> p t d", p=P))\
                      .then_inc(loaded_x[n], 16)
                sp.dma_start(ident[:, :], ins["ident"]).then_inc(loaded_ident, 16)
                sp.dma_start(small[:, :], ins["biases"]).then_inc(loaded_const, 16)
                sp.dma_start(out_bias[:, :, :], ins["out_bias"]).then_inc(loaded_const, 16)
                for h in range(2):
                    load_qk(sp, h, 0)
                sp.dma_start(sm[:, :, :], ins["sim"].rearrange("(c p) e -> p c e", p=P)).then_inc(loaded_sim, 16)
                sp.dma_start(gates[:, :], ins["gates"]).then_inc(loaded_sim, 16)
                for tile, name in ((below, "below"), (sel_half[:, :], "sel_half"), (sel_tile[:, :], "sel_tile"),
                                   (same_h[:, :], "same_h"), (mask[:, :], "after")):
                    sp.dma_start(tile, ins[name]).then_inc(loaded_sel, 16)
                load_v(sp, 0)
                for n in range(2):
                    h = slice(n * EH // 2, (n + 1) * EH // 2)
                    sp.dma_start(ev[:, h, :], ins["expert_v"].rearrange("(t p) d -> p t d", p=P)[:, h, :])\
                      .then_inc(loaded_ev[n], 16)
                for n in range(2):
                    h = slice(n * EH // 2, (n + 1) * EH // 2)
                    sp.dma_start(eo[:, h, :], ins["expert_o"].rearrange("(t p) d -> p t d", p=P)[:, h, :])\
                      .then_inc(loaded_eo[n], 16)
                for h in range(2):
                    load_qk(sp, h, 1)

            @block.gpsimd
            def _(pool):
                pool.memset(ones[:, :], 1.0).then_inc(consts_done, 1)
                pool.memset(zeros_bf[:, :], 0.0).then_inc(consts_done, 1)
                pool.memset(c_hi[:, :].bitcast(F32), 0.0).then_inc(consts_done, 1)
                pool.memset(c_lo[:, :].bitcast(F32), 0.0).then_inc(consts_done, 1)
                for h in range(2):
                    split_qk(pool, h, 0, None)
                split_v(pool, 0, None)
                pool.wait_ge(loaded_ident, 16)
                pool.tensor_scalar(ident_bf[:, :], ident[:, :], 1.0, 1.0, ALU.mult, ALU.mult)\
                    .then_inc(consts_done, 1)
                pool.wait_ge(loaded_sel, 80)
                pool.tensor_scalar(mask_bf[:, :], mask[:, :], MASKED, 1.0, ALU.mult, ALU.mult)\
                    .then_inc(consts_done, 1)
                pool.wait_ge(loaded_const, 32)
                for t in range(NT):
                    pool.wait_ge(rows_done, t + 1)
                    pool.tensor_tensor(xs[:, t, :], xs[:, t, :], out_bias[:, 0, :], ALU.add).then_inc(biased, 1)
                split_qk(pool, 0, 1, 6)

            @block.scalar
            def _(act):
                def high(n):
                    act.wait_ge(ring_full, n + 1)
                    qk_high(act, FIRST_BANKS[n % len(FIRST_BANKS)], n // 2, n % 2, 0).then_inc(ring_high, 1)

                ln_act(act)
                act.wait_ge(bias_scaled, 1)
                high(0)
                act.wait_ge(gate_step, 2)
                act.activation(g[:, 2, :], g[:, 1, :], ACT.Sqrt).then_inc(gate_act, 1)
                act.activation(gs[:, 1:2], gs[:, 0:1], ACT.Sqrt).then_inc(gate_act, 1)
                act.wait_ge(loaded_sim, 32)
                act.activation(g[:, 3, :], gates[:, :], ACT.Exp, scale=-1.0).then_inc(gate_act, 1)
                for n in range(1, len(FIRST_BANKS)):
                    high(n)
                act.wait_ge(gate_step, 20)
                act.activation(g[:, 14, :], g[:, 13, :], ACT.Exp, bias=gs[:, 4:5], scale=1.0,
                               accum_out=gs[:, 5:6]).then_inc(gate_act, 1)
                act.wait_ge(mixed, 1)
                act.activation(wv_hi[:, :, :], banks[4][:, 0:D].rearrange("p (c m) -> p c m", c=DC), ACT.Copy)\
                    .then_inc(mixed_hi, 1)
                act.wait_ge(mixed, 2)
                act.activation(wo_hi[:, :], banks[5][:, 0:D], ACT.Copy).then_inc(mixed_hi, 1)
                for n in range(len(FIRST_BANKS), 2 * UNITS):
                    high(n)
                for b in range(B):
                    act.wait_ge(comb, b + 1)
                    act.wait_ge(consts_done, 4)
                    act.activation(c_hi[b * H0:(b + 1) * H0, b * S:(b + 1) * S], banks[b][b * H0:(b + 1) * H0, :],
                                   ACT.Copy).then_inc(comb_hi, 1)

            @block.vector
            def _(dve):
                def low(n):
                    dve.wait_ge(ring_high, n + 1)
                    qk_low(dve, FIRST_BANKS[n % len(FIRST_BANKS)], n // 2, n % 2, 0).then_inc(ring_free, 1)

                ln_dve(dve, lambda e, t: e.wait_ge(loaded_x[t // TS], 16))
                dve.wait_ge(loaded_const, 32)
                for at, n, by in ((BQ0, NH0, SCALE0), (BQ1, DC, SCALE1)):
                    dve.tensor_scalar(small[:, at:at + n], small[:, at:at + n], by, None, ALU.mult)\
                       .then_inc(bias_scaled, 1)
                dve.wait_ge(rep_done, 1)
                dve.tensor_scalar(sr[:, :, :], banks[4][:, 0:DC * B].rearrange("p (c b) -> p c b", c=DC),
                                  1.0 / S, None, ALU.mult).then_inc(sr_done, 1)
                dve.wait_ge(sr_done, 1)
                dve.tensor_tensor(sq[:, :, 0:B], sr[:, :, :], sr[:, :, :], ALU.mult).then_inc(sr_done, 1)
                dve.wait_ge(loaded_sim, 32)
                dve.tensor_tensor(sq[:, :, B:], sm[:, :, :], sm[:, :, :], ALU.mult).then_inc(sr_done, 1)
                steps = [0]

                def link(ins_):
                    steps[0] += 1
                    ins_.then_inc(gate_step, 1)
                    dve.wait_ge(gate_step, steps[0])

                dve.wait_ge(norms_done, 1)
                nrm = banks[5]
                link(dve.tensor_copy(g[:, 1, :], nrm[0:B, E0:2 * E0]))
                link(dve.tensor_copy(gs[:, 0:1], nrm[0:B, 2 * E0:2 * E0 + 1]))
                dve.wait_ge(gate_act, 3)
                link(dve.reciprocal(g[:, 4, :], g[:, 2, :]))
                link(dve.reciprocal(gs[:, 2:3], gs[:, 1:2]))
                link(dve.tensor_scalar(g[:, 5, :], g[:, 3, :], 1.0, None, ALU.add))
                link(dve.reciprocal(g[:, 6, :], g[:, 5, :]))
                link(dve.scalar_tensor_tensor(g[:, 7, :], nrm[0:B, 0:E0], gs[:, 2:3], g[:, 4, :],
                                              ALU.mult, ALU.mult))
                link(dve.tensor_tensor(g[:, 8, :], g[:, 7, :], g[:, 6, :], ALU.subtract))
                link(dve.tensor_scalar(g[:, 9, :], g[:, 8, :], 0.0, None, ALU.max))
                link(dve.tensor_scalar(g[:, 10, :], g[:, 9, :], 0.0, None, ALU.is_gt))
                link(dve.tensor_reduce(gs[:, 3:4], g[:, 10, :], AX, ALU.max))
                row = g[:, 8:9, :].to_broadcast([B, E0, E0])
                col = g[:, 8, :].rearrange("b (e o) -> b e o", o=1).to_broadcast([B, E0, E0])
                link(dve.tensor_tensor(cmp1[:, :, :], row, col, ALU.is_gt))
                link(dve.tensor_tensor(cmp2[:, :, :], row, col, ALU.is_equal))
                dve.wait_ge(loaded_sel, 80)
                link(dve.tensor_tensor(cmp2[:, :, :], cmp2[:, :, :], below[:, :, :], ALU.mult))
                link(dve.tensor_tensor(cmp1[:, :, :], cmp1[:, :, :], cmp2[:, :, :], ALU.add))
                link(dve.tensor_reduce(g[:, 11, :], cmp1[:, :, :], AX, ALU.add))
                link(dve.tensor_scalar(g[:, 12, :], g[:, 11, :], E0 / 2, gs[:, 3:4], ALU.is_lt, ALU.is_gt))
                link(dve.tensor_tensor(g[:, 12, :], g[:, 10, :], g[:, 12, :], ALU.max))
                link(dve.tensor_scalar(g[:, 0, :], g[:, 12, :], FLT_MAX, FLT_MAX, ALU.mult, ALU.subtract))
                dve.tensor_tensor(g[:, 13, :], g[:, 9, :], g[:, 0, :], ALU.add).then_inc(r_sp_done, 1)
                dve.wait_ge(r_sp_done, 1)
                link(dve.tensor_reduce(gs[:, 4:5], g[:, 13, :], AX, ALU.max, negate=True))
                dve.wait_ge(gate_act, 4)
                link(dve.reciprocal(gs[:, 6:7], gs[:, 5:6]))
                link(dve.scalar_tensor_tensor(g[:, 15, :], g[:, 14, :], gs[:, 6:7], g[:, 12, :],
                                              ALU.mult, ALU.mult))
                dve.wait_ge(r_turned, 1)
                dve.tensor_copy(r_T[:, :], banks[4][0:E0, 0:B]).then_inc(r_sp_done, 1)
                dve.wait_ge(r_sp_done, 2)
                dve.wait_ge(loaded_sel, 80)
                dve.tensor_tensor(r_spread[:, :, :],
                                  r_T[:, :].rearrange("e (o b) -> e o b", o=1).to_broadcast([E0, EH, B]),
                                  sel_tile[:, :].rearrange("e (t o) -> e t o", o=1).to_broadcast([E0, EH, B]),
                                  ALU.mult).then_inc(r_sp_done, 1)
                dve.wait_ge(r_col_done, 1)
                dve.tensor_copy(r_col[:, :, :], banks[5][:, 0:EH * B].rearrange("p (t b) -> p t b", b=B))\
                   .then_inc(r_sp_done, 1)
                dve.wait_ge(r_sp_done, 4)
                for n in range(2):
                    tiles, tb = slice(n * EH // 2, (n + 1) * EH // 2), EH // 2 * B
                    dve.tensor_tensor(spread[:, tiles, :].rearrange("p t (b h) -> p (t b) h", b=B),
                                      same_h[:, :].rearrange("p (o h) -> p o h", o=1).to_broadcast([P, tb, H0]),
                                      r_col[:, tiles, :].rearrange("p t (b o) -> p (t b) o", o=1)
                                      .to_broadcast([P, tb, H0]), ALU.mult).then_inc(spread_done, 1)
                for n in range(len(FIRST_BANKS)):
                    low(n)
                dve.wait_ge(mixed_hi, 1)
                dve.tensor_tensor(wv_lo[:, :, :], banks[4][:, 0:D].rearrange("p (c m) -> p c m", c=DC),
                                  wv_hi[:, :, :].bitcast(F32), ALU.subtract).then_inc(mixed_lo, 1)
                dve.wait_ge(mixed_hi, 2)
                dve.tensor_tensor(wo_lo[:, :], banks[5][:, 0:D], wo_hi[:, :].bitcast(F32), ALU.subtract)\
                   .then_inc(mixed_lo, 1)
                for n in range(len(FIRST_BANKS), 2 * UNITS):
                    low(n)
                for b in range(B):
                    dve.wait_ge(comb_hi, b + 1)
                    rows, cols = slice(b * H0, (b + 1) * H0), slice(b * S, (b + 1) * S)
                    dve.tensor_tensor(c_lo[rows, cols], banks[b][rows, :], c_hi[rows, cols].bitcast(F32),
                                      ALU.subtract).then_inc(comb_lo, 1)
                dve.wait_ge(biased, NT)
                for n in range(NT // 2):
                    dve.wait_ge(ffn_ready, n + 1)
                    rows = xs[:, 2 * n:2 * n + 2, :]
                    dve.tensor_tensor(rows, banks[4 + n][:, :].rearrange("p (t d) -> p t d", d=D), rows, ALU.add)\
                       .then_inc(ffn_added, 1)

            @block.tensor
            def _(pe):
                def project(n):
                    u, k = n // 2, n % 2
                    pe.wait_ge(qk_split[u % 2], 3)
                    if n >= len(FIRST_BANKS):
                        pe.wait_ge(ring_free, n - len(FIRST_BANKS) + 1)
                    qk_product(pe, FIRST_BANKS[n % len(FIRST_BANKS)], u, k).then_inc(ring_full, 1)

                pe.wait_ge(loaded_ident, 16)
                pe.wait_ge(consts_done, 2)
                ln_pe(pe)
                for c in range(DC):
                    for b in range(B):
                        for j in range(TS):
                            mm = pe.matmul(banks[4][:, c * B + b:c * B + b + 1],
                                           xn[:, b * TS + j, c * P:(c + 1) * P], ones[:, 0:1],
                                           start=(j == 0), stop=(j == TS - 1))
                mm.then_inc(rep_done, 1)
                pe.wait_ge(lo_done, 2 * DC)
                project(0)
                pe.wait_ge(sr_done, 3)
                pe.wait_ge(loaded_sim, 32)
                for c in range(DC):
                    pe.matmul(banks[5][0:B, 0:E0], sr[:, c, :], sm[:, c, :], start=(c == 0), stop=(c == DC - 1))
                for c in range(DC):
                    pe.matmul(banks[5][0:B, E0:2 * E0], ones[:, 0:B], sq[:, c, B:], start=(c == 0),
                              stop=(c == DC - 1))
                for c in range(DC):
                    mm = pe.matmul(banks[5][0:B, 2 * E0:2 * E0 + 1], sq[:, c, 0:B], ones[:, 0:1],
                                   start=(c == 0), stop=(c == DC - 1))
                mm.then_inc(norms_done, 1)
                for n in range(1, len(FIRST_BANKS)):
                    project(n)
                pe.wait_ge(gate_step, 22)
                pe.transpose(banks[4][0:E0, 0:B], g[:, 15, :], ident[0:B, 0:B]).then_inc(r_turned, 1)
                pe.wait_ge(r_sp_done, 3)
                pe.wait_ge(loaded_sel, 80)
                pe.matmul(banks[5][:, 0:EH * B], sel_half[:, :], r_spread[:, :, :].rearrange("e t b -> e (t b)"),
                          start=True, stop=True).then_inc(r_col_done, 1)
                for c in range(DC):
                    for t in range(EH):
                        if c == 0 and t % (EH // 2) == 0:
                            pe.wait_ge(loaded_ev[t // (EH // 2)], 16)
                            pe.wait_ge(spread_done, t // (EH // 2) + 1)
                        mm = pe.matmul(banks[4][:, c * P:(c + 1) * P], ev[:, t, c * P:(c + 1) * P],
                                       spread[:, t, :], start=(t == 0), stop=(t == EH - 1))
                mm.then_inc(mixed, 1)
                for t in range(EH):
                    if t % (EH // 2) == 0:
                        pe.wait_ge(loaded_eo[t // (EH // 2)], 16)
                    mm = pe.matmul(banks[5][:, 0:D], spread[:, t, :], eo[:, t, :], start=(t == 0),
                                   stop=(t == EH - 1))
                mm.then_inc(mixed, 1)
                for n in range(len(FIRST_BANKS), 2 * UNITS):
                    project(n)
                pe.wait_ge(mixed_lo, 1)
                pe.wait_ge(ring_free, 4)
                for b in range(B):
                    for c in range(DC):
                        cols = slice(b * S, (b + 1) * S)
                        mm = mm3(pe, banks[b][:, :], (wv_hi[:, c, :], wv_lo[:, c, :]),
                                 (xt_hi[:, c, cols], xt_lo[:, c, cols]), c == 0, c == DC - 1)
                    mm.then_inc(comb, 1)
                pe.wait_ge(mixed_lo, 2)
                pe.wait_ge(comb_lo, 2)
                pe.wait_ge(ring_free, 2 * UNITS)
                for n in range(NT // 2):
                    for t in (2 * n, 2 * n + 1):
                        cols = slice(t * P, (t + 1) * P)
                        mm = mm3(pe, banks[4 + n][:, (t % 2) * D:(t % 2 + 1) * D], (c_hi[:, cols], c_lo[:, cols]),
                                 (wo_hi[:, :], wo_lo[:, :]), True, True)
                    mm.then_inc(ffn_ready, 1)

    with st2, nc.Block() as block:
        @block.sync
        def _(sp):
            load_o(sp, 0)
            load_v(sp, 1)
            load_qk(sp, 0, 2)
            sp.dma_start(raw[:, :, :], ins["w_qkv1"].rearrange("(c p) n -> p c n", p=P)).then_inc(loaded_raw1, 16)
            sp.dma_start(al[:, :], ins["alibi"].rearrange("h (a t) -> (h a) t", a=P // NH1)).then_inc(loaded1, 16)
            sp.dma_start(rw[:, :, :], ins["router"].rearrange("(c p) e -> p c e", p=P)).then_inc(loaded1, 16)
            sp.dma_start(before8[:, :, :], ins["before8"]).then_inc(loaded1, 16)
            with sp.Fori(0, PAIRS - 3) as i:
                load_qk(sp, 1, i + 2)
                load_v(sp, i + 2)
                load_o(sp, i + 1)
                load_qk(sp, 0, i + 3)
            load_qk(sp, 1, PAIRS - 1)
            load_v(sp, PAIRS - 1)
            load_o(sp, PAIRS - 2)
            load_o(sp, PAIRS - 1)

        @block.gpsimd
        def _(pool):
            def iteration(i, first=False, project=True, more=True):
                r = RING0 + RING * i
                for u in range(UNITS):
                    if u == 0 and project:
                        split_qk(pool, 1, i + 1, r - 2)
                        split_v(pool, i + 1, r + 2 if first else r)
                    if project or u < UNITS - 1:
                        att.normalise(pool, UNITS * i + u + 1, u + 1)
                    if u == 0:
                        split_o(pool, i, r + 2)
                    if u == 3 and more:
                        split_qk(pool, 0, i + 2, r + QK_USE[2] + 2)

            att.normalise(pool, 0, 0)
            iteration(0, first=True)
            with pool.Fori(1, PAIRS - 2) as i:
                iteration(i)
            iteration(PAIRS - 2, more=False)
            iteration(PAIRS - 1, project=False, more=False)

            pool.wait_ge(loaded1, 48)
            pool.tensor_scalar(rw_hi[:, :, :], rw[:, :, :], 1.0, 1.0, ALU.mult, ALU.mult).then_inc(rw_split, 1)
            pool.tensor_scalar(al_hi[:, :], al[:, :], 1.0, 1.0, ALU.mult, ALU.mult).then_inc(al_split, 1)
            pool.wait_ge(loaded_raw1, 16)
            for c in range(DC):
                pool.tensor_scalar(raw[:, c, 0:D], raw[:, c, 0:D], SCALE1, 1.0, ALU.mult, ALU.mult)\
                    .then_inc(scaled1, 1)
            pool.wait_ge(rw_split, 1)
            pool.tensor_tensor(rw_lo[:, :, :], rw[:, :, :], rw_hi[:, :, :].bitcast(F32), ALU.subtract)\
                .then_inc(rw_split, 1)
            pool.wait_ge(scaled1, DC)
            for c in range(DC):
                pool.tensor_scalar(wqkv_hi[:, c, :], raw[:, c, :], 1.0, 1.0, ALU.mult, ALU.mult)\
                    .then_inc(split1, 1)
            pool.wait_ge(split1, DC)
            for c in range(DC):
                pool.tensor_tensor(wqkv_lo[:, c, :], raw[:, c, :], wqkv_hi[:, c, :].bitcast(F32), ALU.subtract)\
                    .then_inc(split1, 1)
            pool.wait_ge(al_split, 1)
            pool.tensor_tensor(al_lo[:, :], al[:, :], al_hi[:, :].bitcast(F32), ALU.subtract)\
                .then_inc(al_split, 1)
            pool.wait_ge(al_split, 2)
            pool.tensor_tensor(sel16[:, :, :],
                               ident[0:2 * E1, 0:E1].rearrange("k (e o) -> k e o", o=1)
                               .to_broadcast([2 * E1, E1, P]),
                               ident[0:2 * E1, E1:2 * E1].rearrange("k (e o) -> k e o", o=1)
                               .to_broadcast([2 * E1, E1, P]), ALU.add).then_inc(sel_done, 1)
            pool.wait_ge(sel_done, 1)

        @block.tensor
        def _(pe):
            def take(r):
                if not isinstance(r, int) or r >= 2:
                    pe.wait_ge(ring_free, r - 1)

            def project_qk(u, j, r, k):
                h = u % 2
                if k == 0:
                    pe.wait_ge(qk_split[h], 3 * j + 3)
                take(r + k)
                qk_product(pe, R_BANK[k], u, k).then_inc(ring_full, 1)

            def project_v(b, j, r):
                pe.wait_ge(v_split, 2 * j + 2)
                for k in range(2):
                    take(r + k)
                    for n in range(2):
                        t = b * TS + 2 * k + n
                        rows = slice(t * P, (t + 1) * P)
                        for c in range(DC):
                            mm = mm3(pe, R_BANK[k][:, n * 2 * P:(n + 1) * 2 * P],
                                     (xt_hi[:, c, rows], xt_lo[:, c, rows]), [w[:, c, :] for w in v_w],
                                     c == 0, c == DC - 1)
                    mm.then_inc(ring_full, 1)

            def project_out(b, i, r):
                pe.wait_ge(o_split, 2 * i + 2)
                pe.wait_ge(o_low, UNITS * i + 2 * b + 2)
                for k in range(2):
                    take(r + k)
                    for n in range(2):
                        j = 2 * k + n
                        for h in range(2):
                            mm = mm3(pe, R_BANK[k][:, n * D:(n + 1) * D],
                                     [x[:, h, j * P:(j + 1) * P] for x in attn_T], [w[:, h, :] for w in o_w],
                                     h == 0, h == 1)
                    mm.then_inc(ring_full, 1)

            def score(U, u):
                def product(pe_, region, q):
                    q_T = [x[:, 0, u, q * P:(q + 1) * P] for x in qk_T]
                    k_T = [x[:, 1, u, 0:(q + 1) * P] for x in qk_T]
                    mm3(pe_, region, q_T, k_T, True, False)

                att.scores(pe, U, product)

            def weigh_v(U, u):
                h, b = u % 2, u // 2
                if not isinstance(U, int) or U:
                    pe.wait_ge(o_low, U)
                for kt in range(TS):
                    att.wait_pt(pe, U, kt)
                    mm = mm3(pe, O_BANK[:, kt * P:S], [v[:, b, kt, h * P:(h + 1) * P] for v in v_rows],
                             att.pt(u, kt), kt == 0, kt == TS - 1)
                mm.then_inc(o_ready, 1)

            def iteration(i, first=False, project=True):
                r = RING0 + RING * i
                outs = OUT_USE if project else OUT_USE_LAST
                for u in range(UNITS):
                    U = UNITS * i + u
                    if project or u < UNITS - 1:
                        score(U + 1, (u + 1) % UNITS)
                    if u == 0 and not first:
                        project_out(1, i - 1, r + outs[1])
                    if u == 2:
                        project_out(0, i, r + outs[0])
                    if u % 2 and project:
                        project_qk(u, i + 1, r + QK_USE[u], 0)
                    att.turn(pe, U, u, 0)
                    att.turn(pe, U, u, 1)
                    if project:
                        project_qk(u, i + 1, r + QK_USE[u], u % 2)
                    att.turn(pe, U, u, 2)
                    if u % 2 == 0 and project:
                        project_qk(u, i + 1, r + QK_USE[u], 1)
                    weigh_v(U, u)
                    if u % 2 and project:
                        project_v(u // 2, i + 1, r + V_USE[u // 2])

            score(0, 0)
            for b in range(B):
                project_v(b, 0, 8 + 2 * b)
            iteration(0, first=True)
            with pe.Fori(1, PAIRS - 1) as i:
                iteration(i)
            iteration(PAIRS - 1, project=False)
            project_out(1, PAIRS - 1, RING0 + RING * (PAIRS - 1) + 4)

        def v_dest(parts, b, k):
            return parts[:, b, 2 * k:2 * k + 2, :].rearrange("p t n -> p (t n)")

        @block.scalar
        def _(act):
            def high_qk(u, j, r, k):
                wait_apart(act, (ring_full, r + k + 1))
                qk_high(act, R_BANK[k], u, k, j).then_inc(ring_high, 1)

            def high_v(b, r):
                for k in range(2):
                    act.wait_ge(ring_full, r + k + 1)
                    act.activation(v_dest(v_rows[0], b, k), R_BANK[k][:, :], ACT.Copy).then_inc(ring_high, 1)

            def high_out(U, u, i):
                wait_apart(act, (o_ready, U + 1))
                act.activation(attn_T[0][:, u % 2, :], O_BANK[:, :], ACT.Identity,
                               bias=bias_col(BV0, i, u % 2)).then_inc(o_high, 1)

            def iteration(i, first=False, project=True):
                r = RING0 + RING * i
                for u in range(UNITS):
                    U = UNITS * i + u
                    if project or u < UNITS - 1:
                        att.exps(act, U + 1, u + 1)
                    if u % 2 and project:
                        high_qk(u, i + 1, r + QK_USE[u], 0)
                    att.turned_high(act, U, u, 0)
                    att.turned_high(act, U, u, 1)
                    if project:
                        high_qk(u, i + 1, r + QK_USE[u], u % 2)
                    att.turned_high(act, U, u, 2)
                    if u % 2 == 0 and project:
                        high_qk(u, i + 1, r + QK_USE[u], 1)
                    high_out(U, u, i)
                    if u % 2 and project:
                        high_v(u // 2, r + V_USE[u // 2])

            att.exps(act, 0, 0)
            for b in range(B):
                high_v(b, 8 + 2 * b)
            iteration(0, first=True)
            with act.Fori(1, PAIRS - 1) as i:
                iteration(i)
            iteration(PAIRS - 1, project=False)

        @block.vector
        def _(dve):
            def low_qk(u, j, n, k):
                dve.wait_ge(ring_high, n + 1)
                qk_low(dve, R_BANK[k], u, k, j).then_inc(ring_free, 1)

            def low_v(b, n, k):
                dve.wait_ge(ring_high, n + 1)
                dve.tensor_tensor(v_dest(v_rows[1], b, k), R_BANK[k][:, :],
                                  v_dest(v_rows[0], b, k).bitcast(F32), ALU.subtract).then_inc(ring_free, 1)

            def low_out(U, u, i):
                dve.wait_ge(o_high, U + 1)
                dve.scalar_tensor_tensor(attn_T[1][:, u % 2, :], O_BANK[:, :], bias_col(BV0, i, u % 2),
                                         attn_T[0][:, u % 2, :].bitcast(F32), ALU.add, ALU.subtract)\
                   .then_inc(o_low, 1)

            def add_out(b, r):
                for k in range(2):
                    dve.wait_ge(ring_full, r + k + 1)
                    rows = xs[:, b * TS + 2 * k:b * TS + 2 * k + 2, :]
                    dve.tensor_tensor(rows, R_BANK[k][:, :].rearrange("p (t d) -> p t d", d=D), rows, ALU.add)\
                       .then_inc(ring_free, 1)

            def iteration(i, first=False, project=True):
                r = RING0 + RING * i
                n = HIGHS + HIGHS * i
                outs = OUT_USE if project else OUT_USE_LAST
                for u in range(UNITS):
                    U = UNITS * i + u
                    if project or u < UNITS - 1:
                        att.maxima(dve, U + 1, u + 1)
                    if u % 2:
                        low_out(U - 1, u - 1, i)
                    elif u == 0:
                        low_v(1, n - 1, 1)
                    elif project:
                        low_v(0, n + V_HIGH[0] + 1, 1)
                    if u == 0 and not first:
                        add_out(1, r + outs[1])
                    if u == 2:
                        add_out(0, r + outs[0])
                    if u % 2 and project:
                        low_qk(u, i + 1, n + QK_HIGH[u], 0)
                    if project or u < UNITS - 1:
                        att.reciprocals(dve, U + 1, u + 1)
                    att.turned_low(dve, U, u, 0)
                    att.turned_low(dve, U, u, 1)
                    if project:
                        low_qk(u, i + 1, n + QK_HIGH[u] + u % 2, u % 2)
                    att.turned_low(dve, U, u, 2)
                    if u % 2 == 0 and project:
                        low_qk(u, i + 1, n + QK_HIGH[u] + 1, 1)
                    if u % 2:
                        low_out(U, u, i)
                        if project:
                            low_v(u // 2, n + V_HIGH[u // 2], 0)

            att.maxima(dve, 0, 0)
            for n, (b, k) in enumerate(((0, 0), (0, 1), (1, 0))):
                low_v(b, 8 + n, k)
                if n == 1:
                    att.reciprocals(dve, 0, 0)
            iteration(0, first=True)
            with dve.Fori(1, PAIRS - 1) as i:
                iteration(i)
            iteration(PAIRS - 1, project=False)
            add_out(1, RING0 + RING * (PAIRS - 1) + 4)

    scratch = nc.dram_tensor("head_rows", (2, 2, D, T), F32, kind="Internal").ap()
    alibi_scratch = nc.dram_tensor("alibi_rows", (NH1, 2, T), F32, kind="Internal").ap()
    GROUPS = D // P
    GROUP_PAIRS = P // HD1 // 2
    PAIR = 2 * HD1
    KR = 4 * HD1 + 2
    HALF = ins["w_down"].shape[3] // D * P
    IC = HALF // P
    v1 = sbuf(late, "v1", [P, 2, NT, D], F32R)
    w_parts = sbuf(late, "expert_weight_parts", [P, NT, 2, E1], F32R)
    w1_raw = sbuf(late, "w1_raw", [P, DC, 2, HALF])
    w2_raw = sbuf(late, "w2_raw", [P, IC, D])
    w1 = [[sbuf(late, f"w1_0{x}", [P, DC, 2, HALF], F32R) for x in ("hi", "lo")]]
    w2 = [[sbuf(late, f"w2_0{x}", [P, IC, D], F32R) for x in ("hi", "lo")]]
    w1_loaded = sem("w1_loaded")
    w2_loaded = sem("w2_loaded")
    w1_split = sem("w1_split")
    w2_split = sem("w2_split")
    qk1 = [sbuf(late, f"qk1_{x}", [P, 2, DC, T], F32R) for x in ("hi", "lo")]
    a1_hi, a1_lo = (x[:, 0, :, :] for x in qk1)
    st4 = ExitStack()
    q4 = sbuf(st4, "q_rows", [KR, 2, T], F32R)
    k4 = sbuf(st4, "k_rows", [KR, 2, T], F32R)
    vz = sbuf(st4, "v_placed", [P, 2, 2 * NT, P], F32R)
    lg = sbuf(st4, "router_work", [P, 6, NT, E1])
    ls = sbuf(st4, "router_scalars", [P, 4, NT])
    stored_rows = sem("stored_rows")
    STORES = 2 + 4 * DC
    logits_copied = sem("logits_copied")
    rows_loaded = [sem(f"rows_loaded{h}") for h in range(2)]
    q4_ones = sem("q4_ones")
    cleared = sem("cleared")

    def span(at):
        return slice(at, at + HD1) if isinstance(at, int) else bass.ds(at, HD1)

    def load_head(sp, j, h, wait):
        rows = span((2 * j + h) * HD1)
        head = slice(2 * j + h, 2 * j + h + 1) if isinstance(j, int) else bass.ds(2 * j + h, 1)
        alibi_rows = alibi_scratch[head].rearrange("o k t -> (o k) t")
        if wait is not None:
            sp.wait_ge(*wait)
        for n in range(2):
            at = slice(2 * n * HD1, 2 * (n + 1) * HD1)
            for tile, source in ((q4, scratch[0, n:n + 1, rows, :].to_broadcast([2, HD1, T])),
                                 (k4, scratch[1, :, rows, :])):
                sp.dma_start(tile[at, h, :].bitcast(F32), source)\
                  .then_inc(rows_loaded[h], 16)
        sp.dma_start(k4[4 * HD1:KR, h, :].bitcast(F32), alibi_rows).then_inc(rows_loaded[h], 16)

    def load_half(sp, e, hf):
        at = e if isinstance(e, int) else bass.ds(e, 1)
        w1_src, w2_src = ins["w_gate_up"][at, hf], ins["w_down"][at, hf]
        if not isinstance(e, int):
            w1_src, w2_src = (w.rearrange("o p n -> (o p) n") for w in (w1_src, w2_src))
        sp.dma_start(w1_raw[:, :, :, :].rearrange("p c k n -> p (c k n)"), w1_src).then_inc(w1_loaded, 16)
        sp.dma_start(w2_raw[:, :, :].rearrange("p c n -> p (c n)"), w2_src).then_inc(w2_loaded, 16)

    def split_half_part(pool, raw_, parts, loaded, done, j, used):
        wait_apart(pool, (loaded, 16 * (j + 1)), *used)
        pool.tensor_scalar(parts[0], raw_, 1.0, 1.0, ALU.mult, ALU.mult).then_inc(done, 1)
        pool.wait_ge(done, 2 * j + 1)
        pool.tensor_tensor(parts[1], raw_, parts[0].bitcast(F32), ALU.subtract).then_inc(done, 1)

    def split_w1(pool, slot, j, *used):
        split_half_part(pool, w1_raw[:, :, :, :].rearrange("p c k n -> p (c k n)"),
                        [w[:, :, :, :].rearrange("p c k n -> p (c k n)") for w in w1[slot]], w1_loaded, w1_split,
                        j, used)

    def split_w2(pool, slot, j, *used):
        split_half_part(pool, w2_raw[:, :, :], [w[:, :, :] for w in w2[slot]], w2_loaded, w2_split, j, used)

    with ExitStack() as st3:
        lg_T = raw[0:E1, 0, :]

        biased1 = sem("biased1")
        routed_T = sem("routed_T")
        lg_T_done = sem("lg_T_done")
        routed = sem("routed")
        ring1_full = sem("ring1_full")
        ring1_high = sem("ring1_high")
        ring1_free = sem("ring1_free")
        ROUTE_BANK, W_BANKS = banks[4], banks[3:5]
        RING1 = [banks[n] for n in (5, 6, 7, 0, 1, 2)]
        QKV_USES = 12

        stn, xn, rows_done, hi_done, lo_done, ln_dve, ln_act, ln_pe = layer_norm("1")
        with stn, nc.Block() as block:
            @block.sync
            def _(sp):
                load_half(sp, 0, 0)
                sp.dma_start(alibi_scratch[:, 0, :].rearrange("h (a t) -> h a t", a=P // NH1),
                             al_hi[:, :].bitcast(F32)).then_inc(stored_rows, 16)
                sp.dma_start(alibi_scratch[:, 1, :].rearrange("h (a t) -> h a t", a=P // NH1),
                             al_lo[:, :].bitcast(F32)).then_inc(stored_rows, 16)
                for m in range(DC):
                    for k in range(2):
                        sp.wait_ge(ring1_free, 4 * m + 2 * k + 2)
                        for which in range(2):
                            sp.dma_start(scratch[k, which, m * P:(m + 1) * P, :], qk1[which][:, k, m, :].bitcast(F32))\
                              .then_inc(stored_rows, 16)
                    if m == 0:
                        sp.wait_ge(stored_rows, 16 * (2 + 4))
                        for h in range(2):
                            load_head(sp, 0, h, None)

            @block.gpsimd
            def _(pool):
                pool.memset(q4[4 * HD1:KR, :, :].bitcast(F32), 1.0).then_inc(q4_ones, 1)
                pool.wait_ge(q4_ones, 1)
                pool.memset(vz[:, :, :, :].bitcast(F32), 0.0).then_inc(cleared, 1)
                for t in range(NT):
                    pool.wait_ge(rows_done, t + 1)
                    pool.tensor_tensor(xs[:, t, :], xs[:, t, :], out_bias[:, 1, :], ALU.add).then_inc(biased1, 1)
                split_w1(pool, 0, 0)
                split_w2(pool, 0, 0)

            @block.scalar
            def _(act):
                def bias1(k, m):
                    return small[:, (BQ1, BK1)[k] + m:(BQ1, BK1)[k] + m + 1]

                ln_act(act)
                for n in range(2 * 2 * DC):
                    m, k, b = n // 4, n // 2 % 2, n % 2
                    act.wait_ge(ring1_full, n + 1)
                    act.activation(qk1[0][:, k, m, b * S:(b + 1) * S], RING1[n % 6][:, :], ACT.Identity,
                                   bias=bias1(k, m)).then_inc(ring1_high, 1)
                for b in range(B):
                    act.wait_ge(routed_T, b + 1)
                    act.activation(lg_T[:, b * S:(b + 1) * S], W_BANKS[b][0:E1, :], ACT.Copy).then_inc(lg_T_done, 1)
                for n in range(8, QKV_USES):
                    at = 2 * (n - 8)
                    act.wait_ge(ring1_full, n + 1)
                    act.activation(v1[:, 0, at:at + 2, :], RING1[n % 6][:, :].rearrange(
                        "p (t d) -> p t d", d=D), ACT.Copy).then_inc(ring1_high, 1)
                    if n == 8:
                        act.wait_ge(routed, 1)
                        act.activation(lg[:, 0, :, :], ROUTE_BANK[:, 0:NT * E1].rearrange("p (t e) -> p t e", e=E1),
                                       ACT.Copy).then_inc(logits_copied, 1)

            @block.vector
            def _(dve):
                ln_dve(dve, lambda e, t: None)
                for n in range(2 * 2 * DC):
                    m, k, b = n // 4, n // 2 % 2, n % 2
                    dve.wait_ge(ring1_high, n + 1)
                    at = slice(b * S, (b + 1) * S)
                    dve.scalar_tensor_tensor(qk1[1][:, k, m, at], RING1[n % 6][:, :],
                                             small[:, (BQ1, BK1)[k] + m:(BQ1, BK1)[k] + m + 1],
                                             qk1[0][:, k, m, at].bitcast(F32), ALU.add, ALU.subtract)\
                       .then_inc(ring1_free, 1)
                for n in range(8, QKV_USES):
                    at = 2 * (n - 8)
                    dve.wait_ge(ring1_high, n + 1)
                    dve.tensor_tensor(v1[:, 1, at:at + 2, :], RING1[n % 6][:, :].rearrange(
                        "p (t d) -> p t d", d=D), v1[:, 0, at:at + 2, :].bitcast(F32), ALU.subtract)\
                       .then_inc(ring1_free, 1)

            @block.tensor
            def _(pe):
                ln_pe(pe)
                pe.wait_ge(lo_done, 2 * DC)
                for n in range(2 * 2 * DC):
                    m, k, b = n // 4, n // 2 % 2, n % 2
                    if n >= 6:
                        pe.wait_ge(ring1_free, n - 5)
                    w = slice(k * D + m * P, k * D + (m + 1) * P)
                    cols = slice(b * S, (b + 1) * S)
                    for c in range(DC):
                        mm = mm3(pe, RING1[n % 6][:, :], (wqkv_hi[:, c, w], wqkv_lo[:, c, w]),
                                 (xt_hi[:, c, cols], xt_lo[:, c, cols]), c == 0, c == DC - 1)
                    mm.then_inc(ring1_full, 1)
                for b in range(B):
                    cols = slice(b * S, (b + 1) * S)
                    for c in range(DC):
                        mm = mm3(pe, W_BANKS[b][0:E1, :], (rw_hi[:, c, :], rw_lo[:, c, :]),
                                 (xt_hi[:, c, cols], xt_lo[:, c, cols]), c == 0, c == DC - 1)
                    mm.then_inc(routed_T, 1)
                for n in range(8, QKV_USES):
                    if n == 8:
                        pe.wait_ge(lg_T_done, B)
                        for t in range(NT):
                            mm = pe.transpose(ROUTE_BANK[:, t * E1:(t + 1) * E1], lg_T[:, t * P:(t + 1) * P],
                                              ident[0:E1, 0:E1])
                        mm.then_inc(routed, 1)
                    pe.wait_ge(ring1_free, n - 5)
                    for t in (2 * (n - 8), 2 * (n - 8) + 1):
                        rows = slice(t * P, (t + 1) * P)
                        for c in range(DC):
                            mm = mm3(pe, RING1[n % 6][:, (t % 2) * D:(t % 2 + 1) * D],
                                     (xt_hi[:, c, rows], xt_lo[:, c, rows]),
                                     (wqkv_hi[:, c, 2 * D:3 * D], wqkv_lo[:, c, 2 * D:3 * D]), c == 0, c == DC - 1)
                    mm.then_inc(ring1_full, 1)

    with st4:
        att = Attention("1", st4, [banks[3], banks[4], banks[7]],
                        [sbuf(st4, f"probs1_{k}", [P, SCORES]) for k in range(2)],
                        [sbuf(st4, f"probs1_T_lo{k}", [P, SCORES], F32R) for k in range(2)])
        gt8, eq8 = (sbuf(st4, f"rank8_{x}", [P, NT, E1, E1]) for x in ("gt", "eq"))
        route_step = sem("route_step")
        route_exp = sem("route_exp")
        placed = sem("placed")
        pv_done = sem("pv_done")
        o1_ready = sem("o1_ready")
        o1_high = sem("o1_high")
        o1_low = sem("o1_low")
        O_BANKS = banks[5:7]
        LAST = GROUPS * GROUP_PAIRS - 1

        def each_pair(eng, body):
            for grp in range(GROUPS):
                first = GROUP_PAIRS * grp
                body(grp, 0, first)
                with eng.Fori(1, GROUP_PAIRS - 1) as i:
                    body(grp, i, i + first)
                body(grp, GROUP_PAIRS - 1, first + GROUP_PAIRS - 1)

        def is_(value, number):
            return isinstance(value, int) and value == number

        with nc.Block() as block:
            @block.sync
            def _(sp):
                load_half(sp, 0, 1)
                sp.wait_ge(stored_rows, 16 * STORES)
                with sp.Fori(1, NH1 // 2) as j:
                    for h in range(2):
                        load_head(sp, j, h, (att.scores_ready, 3 * (4 * j - 4 + 2 * h + 2)))

            @block.gpsimd
            def _(pool):
                def place(i, J, h):
                    if not is_(J, 0):
                        pool.wait_ge(pv_done, 4 * J + 2 * h - 2)
                    was = ((i if not is_(i, 0) else GROUP_PAIRS) - 1) * PAIR + h * HD1
                    at, source = i * PAIR + h * HD1, (2 * J + h) * HD1
                    pool.tensor_copy(vz[:, h, :, span(was)], 
                                     zeros_bf[:, 0:2 * NT * HD1].rearrange("p (k d) -> p k d", d=HD1))\
                        .then_inc(placed, 1)
                    pool.tensor_copy(vz[:, h, :, span(at)], v1[:, :, :, span(source)].rearrange(
                        "p k t d -> p (k t) d")).then_inc(placed, 1)

                def pair(grp, i, J):
                    for u in range(4):
                        if u % 2 == 0:
                            place(i, J, u // 2)
                        if not (is_(J, LAST) and u == 3):
                            att.normalise(pool, 4 * J + u + 1, u + 1)

                att.normalise(pool, 0, 0)
                each_pair(pool, pair)

            @block.tensor
            def _(pe):
                def score(J, u):
                    h, b = u % 4 // 2, u % 2
                    if b == 0:
                        pe.wait_ge(rows_loaded[h], 5 * 16 * (J + u // 4) + 5 * 16)

                    def product(pe_, region, q):
                        pe.matmul(region, q4[:, h, b * S + q * P:b * S + (q + 1) * P],
                                  k4[:, h, b * S:b * S + (q + 1) * P], start=True, stop=False)

                    att.scores(pe, 4 * J + u, product)

                def weigh_v(J, u):
                    h, b = u // 2, u % 2
                    if b == 0:
                        pe.wait_ge(placed, 4 * J + 2 * h + 2)
                    for kt in range(TS):
                        att.wait_pt(pe, 4 * J + u, kt)
                        v = [vz[:, h, k * NT + b * TS + kt, :] for k in range(2)]
                        mm = mm3(pe, O_BANKS[b][:, kt * P:S], v, att.pt(u, kt), False, False, skip_group_check=True)
                    mm.then_inc(pv_done, 1)

                def zeros(b, start, stop):
                    return pe.matmul(O_BANKS[b][:, :], zeros_bf[:, 0:P], zeros_bf[:, :], start=start, stop=stop,
                                     skip_group_check=True)

                def close():
                    for b in range(B):
                        zeros(b, False, True).then_inc(o1_ready, 1)

                def pair(grp, i, J):
                    for u in range(4):
                        if not (is_(J, LAST) and u == 3):
                            score(J, u + 1)
                        if is_(i, 0) and u == 2:
                            if grp:
                                pe.wait_ge(o1_low, B * grp)
                            for b in range(B):
                                zeros(b, True, False)
                        if u >= 2:
                            weigh_v(J, u - 2)
                        elif not is_(J, 0):
                            weigh_v(J - 1, u + 2)
                            if is_(i, 0) and u == 1:
                                close()
                        for n in range(3):
                            if not (is_(J, 0) and u == 0):
                                pe.wait_ge(att.t_low, 12 * J + 3 * u + n - 2)
                            att.turn(pe, 4 * J + u, u, n)

                score(0, 0)
                each_pair(pe, pair)
                for u in (2, 3):
                    weigh_v(LAST, u)
                close()

            @block.scalar
            def _(act):
                def high_out(grp):
                    act.wait_ge(stored_rows, 16 * STORES)
                    for b in range(B):
                        act.wait_ge(o1_ready, B * grp + b + 1)
                        act.activation(a1_hi[:, grp, b * S:(b + 1) * S], O_BANKS[b][:, :], ACT.Identity,
                                       bias=small[:, BV1 + grp:BV1 + grp + 1]).then_inc(o1_high, 1)

                def highs(U, u):
                    for n in range(3):
                        att.turned_high(act, U, u % 4, n)

                def pair(grp, i, J):
                    for u in range(4):
                        if is_(i, 0) and u == 2 and grp:
                            high_out(grp - 1)
                        if not (is_(J, 0) and u == 0):
                            highs(4 * J + u - 1, u - 1)
                        if not (is_(J, LAST) and u == 3):
                            att.exps(act, 4 * J + u + 1, u + 1)
                        if is_(J, 0) and u == 0:
                            act.wait_ge(route_step, 2)
                            act.activation(lg[:, 2, :, :], lg[:, 1, :, :], ACT.Exp).then_inc(route_exp, 1)

                att.exps(act, 0, 0)
                each_pair(act, pair)
                highs(4 * LAST + 3, 3)
                high_out(GROUPS - 1)

            @block.vector
            def _(dve):
                def low_out(grp):
                    dve.wait_ge(stored_rows, 16 * STORES)
                    for b in range(B):
                        dve.wait_ge(o1_high, B * grp + b + 1)
                        at = slice(b * S, (b + 1) * S)
                        dve.scalar_tensor_tensor(a1_lo[:, grp, at], O_BANKS[b][:, :],
                                                 small[:, BV1 + grp:BV1 + grp + 1],
                                                 a1_hi[:, grp, at].bitcast(F32), ALU.add, ALU.subtract)\
                           .then_inc(o1_low, 1)

                def lows(U, u, groups):
                    for n in groups:
                        att.turned_low(dve, U, u % 4, n)

                steps = [0]

                def link(ins_):
                    steps[0] += 1
                    ins_.then_inc(route_step, 1)
                    dve.wait_ge(route_step, steps[0])

                def per_expert(col):
                    return ls[:, col, :].rearrange("p (t o) -> p t o", o=1).to_broadcast([P, NT, E1])

                def flat(k):
                    return lg[:, k, :, :].rearrange("p t e -> p (t e)")

                four = [P, NT, E1, E1]
                row = lg[:, 3, :, :].rearrange("p t (o j) -> p t o j", o=1).to_broadcast(four)
                col = lg[:, 3, :, :].rearrange("p t (e o) -> p t e o", o=1).to_broadcast(four)
                eq = eq8[:, :, :, :].rearrange("p t e j -> p t (e j)")

                def route(stage):
                    if stage == 0:
                        link(dve.tensor_reduce(ls[:, 0, :], lg[:, 0, :, :], AX, ALU.max))
                        link(dve.tensor_tensor(lg[:, 1, :, :], lg[:, 0, :, :], per_expert(0), ALU.subtract))
                    elif stage == 1:
                        dve.wait_ge(route_exp, 1)
                        link(dve.tensor_reduce(ls[:, 1, :], lg[:, 2, :, :], AX, ALU.add))
                        link(dve.reciprocal(ls[:, 2, :], ls[:, 1, :]))
                        link(dve.tensor_tensor(lg[:, 3, :, :], lg[:, 2, :, :], per_expert(2), ALU.mult))
                        link(dve.tensor_tensor(eq8[:, :, :, :], row, col, ALU.is_equal))
                    elif stage == 2:
                        link(dve.tensor_tensor(eq, eq, before8[:, :, :].rearrange("p (o e) j -> p o (e j)", o=1)
                                               .to_broadcast([P, NT, E1 * E1]), ALU.mult))
                        link(dve.tensor_tensor(gt8[:, :, :, :], row, col, ALU.is_gt))
                        link(dve.tensor_tensor(gt8[:, :, :, :], gt8[:, :, :, :], eq8[:, :, :, :], ALU.add))
                        link(dve.tensor_reduce(lg[:, 4, :, :], gt8[:, :, :, :], AX, ALU.add))
                    else:
                        link(dve.scalar_tensor_tensor(flat(5), flat(4), 2.0, flat(3), ALU.is_lt, ALU.mult))
                        link(dve.tensor_reduce(ls[:, 3, :], lg[:, 5, :, :], AX, ALU.add))
                        link(dve.reciprocal(ls[:, 0, :], ls[:, 3, :]))
                        link(dve.tensor_tensor(lg[:, 0, :, :], lg[:, 5, :, :], per_expert(0), ALU.mult))
                        link(dve.tensor_copy(w_parts[:, :, 0, :], lg[:, 0, :, :]))
                        link(dve.tensor_tensor(w_parts[:, :, 1, :], lg[:, 0, :, :],
                                               w_parts[:, :, 0, :].bitcast(F32), ALU.subtract))

                def pair(grp, i, J):
                    for u in range(4):
                        if is_(i, 0) and u == 2 and grp:
                            low_out(grp - 1)
                        if not (is_(J, 0) and u == 0):
                            lows(4 * J + u - 1, u - 1, [0])
                        if not (is_(J, LAST) and u == 3):
                            att.maxima(dve, 4 * J + u + 1, u + 1)
                        if not (is_(J, 0) and u == 0):
                            lows(4 * J + u - 1, u - 1, [1, 2])
                        if not (is_(J, LAST) and u == 3):
                            att.reciprocals(dve, 4 * J + u + 1, u + 1)
                        if is_(J, 0):
                            route(u)

                att.maxima(dve, 0, 0)
                att.reciprocals(dve, 0, 0)
                each_pair(dve, pair)
                lows(4 * LAST + 3, 3, range(3))
                low_out(GROUPS - 1)

    with late, ExitStack() as st5:
        w1.append([sbuf(st5, f"w1_1{x}", [P, DC, 2, HALF], F32R) for x in ("hi", "lo")])
        w2.append([sbuf(st5, f"w2_1{x}", [P, IC, D], F32R) for x in ("hi", "lo")])
        w_T = sbuf(st5, "expert_weight_T", [2 * E1, T], F32R)
        w_bc = sbuf(st5, "expert_weight", [P, E1, T])
        silu = sbuf(st5, "silu_gate", [P, 2, S])
        gated = sbuf(st5, "gated_up", [P, 2, S])
        weighed = sbuf(st5, "weighed", [P, 2, S])
        hid = [sbuf(st5, f"hidden_{x}", [P, B, IC, S], F32R) for x in ("hi", "lo")]
        w_turned = sem("w_turned")
        w_T_done = sem("w_T_done")
        bc_ready = sem("bc_ready")
        bc_act = sem("bc_act")
        bc_dve = sem("bc_dve")
        gu_ready = sem("gu_ready")
        silu_done = sem("silu_done")
        up_done = sem("up_done")
        weigh_done = sem("weigh_done")
        hid_high = sem("hid_high")
        hid_low = sem("hid_low")
        down_done = sem("down_done")
        sums_ready = sem("sums_ready")
        out_added = sem("out_added")
        stored = sem("stored")
        Y_BANK = banks[0:4]
        W_BANKS = banks[4:6]
        BC_BANKS = [banks[n] for n in (6, 7, 4, 5)]
        NHALF = E1 * HALVES

        with nc.Block() as block:
            @block.sync
            def _(sp):
                with sp.Fori(1, E1) as e:
                    for hf in range(2):
                        sp.wait_ge(w1_split, 4 * e + 2 * hf)
                        sp.wait_ge(w2_split, 4 * e + 2 * hf)
                        load_half(sp, e, hf)
                for n in range(4):
                    sp.wait_ge(out_added, n + 1)
                    sp.dma_start(out[2 * n * P:(2 * n + 2) * P, :].rearrange("(t p) d -> p t d", p=P),
                                 xs[:, 2 * n:2 * n + 2, :]).then_inc(stored, 16)
                sp.wait_ge(stored, 64)

            @block.gpsimd
            def _(pool):
                def half(e, hf, more, first):
                    j = 2 * e + hf
                    for k in range(2 * IC):
                        s, b = 4 * j + k, k // IC
                        waits = [(up_done, s + 1)]
                        if not (first and k < 2):
                            waits.append((hid_low, s - 1))
                        wait_apart(pool, *waits)
                        weight = (w_bc[:, e, b * S:(b + 1) * S] if isinstance(e, int) else
                                  w_bc[:, bass.ds(e, 1), b * S:(b + 1) * S].rearrange("p o t -> p (o t)"))
                        pool.tensor_tensor(weighed[:, k % 2, :], gated[:, k % 2, :], weight, ALU.mult)\
                            .then_inc(weigh_done, 1)
                        if more and k == 0:
                            split_w1(pool, 1 - hf, j + 1, *([] if first else [(gu_ready, 4 * j)]))
                        if more and k == 2:
                            split_w2(pool, 1 - hf, j + 1, *([] if first else [(down_done, 2 * j)]))

                pool.wait_ge(bc_act, E1)
                pool.wait_ge(bc_dve, E1)
                half(0, 0, True, True)
                half(0, 1, True, False)
                with pool.Fori(1, E1 - 1) as e:
                    half(e, 0, True, False)
                    half(e, 1, True, False)
                half(E1 - 1, 0, True, False)
                half(E1 - 1, 1, False, False)

            @block.tensor
            def _(pe):
                for n in range(NT // 2):
                    pe.matmul(Y_BANK[n][:, :], zeros_bf[:, 0:P], zeros_bf[:, :], start=True, stop=False,
                              skip_group_check=True)
                for t in range(NT):
                    mm = pe.transpose(W_BANKS[t // TS][0:2 * E1, (t % TS) * P:(t % TS + 1) * P],
                                      w_parts[:, t, :, :].rearrange("p k e -> p (k e)").bitcast(F32), ident[:, :])
                    if t % TS == TS - 1:
                        mm.then_inc(w_turned, 1)
                for t in range(NT):
                    rows = slice(t * P, (t + 1) * P)
                    for grp in range(GROUPS):
                        mm3(pe, Y_BANK[t // 2][:, (t % 2) * D:(t % 2 + 1) * D],
                            (a1_hi[:, grp, rows], a1_lo[:, grp, rows]),
                            (wqkv_hi[:, grp, 3 * D:], wqkv_lo[:, grp, 3 * D:]), False, False,
                            skip_group_check=True)
                    if t == 0:
                        continue
                    for n in range(2 * t - 2, 2 * t if t < NT - 1 else 2 * E1):
                        if n == 0:
                            pe.wait_ge(w_T_done, B)
                        if n >= len(BC_BANKS):
                            pe.wait_ge((bc_act, bc_dve)[n % 2], (n - len(BC_BANKS)) // 2 + 1)
                        pe.matmul(BC_BANKS[n % 4][:, :], sel16[:, n // 2, :], w_T[:, (n % 2) * S:(n % 2 + 1) * S],
                                  start=True, stop=True).then_inc(bc_ready, 1)
                pe.wait_ge(bc_act, E1)
                pe.wait_ge(bc_dve, E1)

                def down(g, hf, b, last=False):
                    pe.wait_ge(hid_low, 2 * g + 2)
                    for j in range(TS):
                        t = b * TS + j
                        for ic in range(IC):
                            mm = mm3(pe, Y_BANK[t // 2][:, (t % 2) * D:(t % 2 + 1) * D],
                                     [h[:, b, ic, j * P:(j + 1) * P] for h in hid], [w[:, ic, :] for w in w2[hf]],
                                     False, last and ic == IC - 1, skip_group_check=True)
                        if last and t % 2:
                            mm.then_inc(sums_ready, 1)
                    if not last:
                        mm.then_inc(down_done, 1)

                def expert(e, first):
                    for hf in range(2):
                        j = 2 * e + hf
                        pe.wait_ge(w1_split, 2 * j + 2)
                        for b in range(B):
                            g = 2 * j + b
                            for ic in range(IC):
                                s = 2 * g + ic
                                if not (first and hf == 0 and b == 0):
                                    pe.wait_ge(up_done, s - 1)
                                for k in range(2):
                                    for c in range(DC):
                                        at = slice(b * S, (b + 1) * S)
                                        mm = mm3(pe, banks[4 + 2 * ic + k][:, :],
                                                 [w[:, c, k, ic * P:(ic + 1) * P] for w in w1[hf]],
                                                 (xt_hi[:, c, at], xt_lo[:, c, at]), c == 0, c == DC - 1)
                                mm.then_inc(gu_ready, 1)
                            if not (first and hf == 0 and b == 0):
                                if b == 1:
                                    pe.wait_ge(w2_split, 2 * j + 2)
                                down(g - 1, hf if b else 1 - hf, 1 - b)

                expert(0, True)
                with pe.Fori(1, E1) as e:
                    expert(e, False)
                for n in range(TS // 2):
                    pe.matmul(Y_BANK[n][:, :], zeros_bf[:, 0:P], zeros_bf[:, :], start=False, stop=True,
                              skip_group_check=True).then_inc(sums_ready, 1)
                down(2 * NHALF - 1, 1, 1, last=True)

            @block.scalar
            def _(act):
                for e in range(E1):
                    act.wait_ge(bc_ready, 2 * e + 1)
                    act.activation(w_bc[:, e, 0:S], BC_BANKS[2 * e % 4][:, :], ACT.Copy).then_inc(bc_act, 1)

                def step(s, k, lag):
                    act.wait_ge(gu_ready, s + 1)
                    act.activation(silu[:, k % 2, :], banks[4 + 2 * (k % 2)][:, :], ACT.Silu).then_inc(silu_done, 1)
                    if lag:
                        high(s - 1, (k - 1) % 4)

                def high(s, k):
                    act.wait_ge(weigh_done, s + 1)
                    act.activation(hid[0][:, k // 2, k % 2, :], weighed[:, k % 2, :], ACT.Copy).then_inc(hid_high, 1)

                for k in range(8):
                    step(k, k % 4, k > 0)
                with act.Fori(1, E1) as e:
                    for k in range(8):
                        step(8 * e + k, k % 4, True)
                high(4 * NHALF - 1, 3)

            @block.vector
            def _(dve):
                for b in range(B):
                    dve.wait_ge(w_turned, b + 1)
                    dve.tensor_copy(w_T[:, b * S:(b + 1) * S], W_BANKS[b][0:2 * E1, :]).then_inc(w_T_done, 1)
                for e in range(E1):
                    dve.wait_ge(bc_ready, 2 * e + 2)
                    dve.tensor_copy(w_bc[:, e, S:T], BC_BANKS[(2 * e + 1) % 4][:, :]).then_inc(bc_dve, 1)

                def step(s, k, lag):
                    dve.wait_ge(silu_done, s + 1)
                    dve.tensor_tensor(gated[:, k % 2, :], banks[5 + 2 * (k % 2)][:, :], silu[:, k % 2, :], ALU.mult)\
                       .then_inc(up_done, 1)
                    if lag:
                        low(s - 1, (k - 1) % 4)

                def low(s, k):
                    dve.wait_ge(hid_high, s + 1)
                    dve.tensor_tensor(hid[1][:, k // 2, k % 2, :], weighed[:, k % 2, :],
                                      hid[0][:, k // 2, k % 2, :].bitcast(F32), ALU.subtract).then_inc(hid_low, 1)

                for k in range(8):
                    step(k, k % 4, k > 0)
                with dve.Fori(1, E1) as e:
                    for k in range(8):
                        step(8 * e + k, k % 4, True)
                low(4 * NHALF - 1, 3)
                for n in range(NT // 2):
                    dve.wait_ge(sums_ready, n + 1)
                    rows = xs[:, 2 * n:2 * n + 2, :]
                    dve.tensor_tensor(rows, Y_BANK[n][:, :].rearrange("p (t d) -> p t d", d=D), rows, ALU.add)\
                       .then_inc(out_added, 1)
    whole.close()


def kernel(**inputs):
    import concourse.bacc as bacc
    from concourse.bass_utils import run_bass_kernel_spmd

    def layout(a):
        return np.ascontiguousarray(a)

    x = np.asarray(inputs["L0_attn_query"])
    B, S, D = x.shape
    DC = D // P
    w_q, w_k, w_v, w_o = (np.asarray(inputs[f"L0_attn_w_{n}"]) for n in "qkvo")
    pairs = w_q.shape[1] // (2 * P)
    qk = np.stack([w_q, w_k]).reshape(2, DC, P, pairs, 2, P).transpose(4, 3, 2, 1, 0, 5)
    v = w_v.reshape(DC, P, pairs, 2 * P).transpose(2, 1, 0, 3)
    o = w_o.reshape(pairs, 2, P, D).transpose(0, 2, 1, 3)

    def columns(name):
        return np.asarray(inputs[name]).reshape(-1, P).T

    biases = np.concatenate([columns(f"L0_attn_b_{n}") for n in "qkv"]
                            + [columns(f"L1_attn_b{n}") for n in "qkv"], axis=1)
    e0 = inputs["L0_ffn_sim_matrix"].shape[1]
    e = np.arange(e0)
    p = np.arange(P)
    width = inputs["L0_ffn_w_v"].shape[1]
    gate_up = np.asarray(inputs["L1_ffn_gate_up_proj"])
    down = np.asarray(inputs["L1_ffn_down_proj"])
    e1, two_i, _ = gate_up.shape
    half = two_i // 4
    gu = gate_up.reshape(e1, 2, 2, half, DC, P).transpose(0, 2, 5, 4, 1, 3)
    dn = down.reshape(e1, D, 2, half // P, P).transpose(0, 2, 4, 3, 1)
    nh1 = 16
    start = 2 ** (-2 ** (-(np.log2(nh1) - 3)))
    slopes = np.array([start * start ** i for i in range(nh1)], dtype=np.float32)
    alibi = (-slopes[:, None] * (S - 1 - np.arange(S, dtype=np.float32))[None, :]).astype(np.float32)
    alibi = np.concatenate([alibi] * B, axis=1)

    arrays = {
        "x": layout(x.reshape(B * S, D)),
        "w_qk0": layout(qk.reshape(2, pairs, P, DC * 2 * P)),
        "w_v0": layout(v.reshape(pairs, P, DC * 2 * P)),
        "w_o0": layout(o.reshape(pairs, P, 2 * D)),
        "biases": layout(biases),
        "out_bias": layout(np.broadcast_to(np.stack([np.asarray(inputs["L0_attn_b_o"]),
                                                     np.asarray(inputs["L1_attn_bo"])]), (P, 2, D))),
        "sim": layout(inputs["L0_ffn_sim_matrix"]),
        "gates": layout(np.broadcast_to(np.asarray(inputs["L0_ffn_gates"]), (B, e0))),
        "expert_v": layout(np.asarray(inputs["L0_ffn_w_v"]).reshape(e0 * width, D)),
        "expert_o": layout(np.asarray(inputs["L0_ffn_o_weights"]).reshape(e0 * width, D)),
        "w_qkv1": layout(np.concatenate([np.asarray(inputs[f"L1_attn_W{n}"]) for n in "qkvo"], axis=1)),
        "router": layout(np.asarray(inputs["L1_ffn_gate_weight"]).T),
        "w_gate_up": layout(gu.reshape(e1, 2, P, DC * 2 * half)),
        "w_down": layout(dn.reshape(e1, 2, P, (half // P) * D)),
        "ident": np.eye(P, dtype=np.float32),
        "after": (p[None, :] > p[:, None]).astype(np.float32),
        "below": layout(np.broadcast_to(e[None, :] < e[:, None], (B, e0, e0)).astype(np.float32)),
        "sel_half": (e[:, None] % 2 == p[None, :] // width).astype(np.float32),
        "sel_tile": (e[:, None] // 2 == np.arange(e0 * width // P)[None, :]).astype(np.float32),
        "same_h": (p[:, None] % width == np.arange(width)[None, :]).astype(np.float32),
        "alibi": layout(alibi),
        "before8": layout(np.broadcast_to(np.arange(e1)[None, :] < np.arange(e1)[:, None],
                                          (P, e1, e1)).astype(np.float32)),
    }
    nc = bacc.Bacc("TRN2", target_bir_lowering=False, num_devices=1)
    ins = {n: nc.dram_tensor(f"in_{n}", a.shape, mybir.dt.from_np(a.dtype), kind="ExternalInput").ap()
           for n, a in arrays.items()}
    out = nc.dram_tensor("out_x", (B * S, D), F32, kind="ExternalOutput").ap()
    build(nc, ins, out)
    r = run_bass_kernel_spmd(nc, [{f"in_{n}": a for n, a in arrays.items()}], core_ids=[0])
    return r.results[0]["out_x"].reshape(B, S, D)
```
